# Optimizing a Trainium2 kernel written in Bass

```python
import numpy as np
import jax
import jax.numpy as jnp

def _softmax(x, axis=-1):
    return jax.nn.softmax(x, axis=axis)

def _gelu(x):
    return jax.nn.gelu(x, approximate=True)

def _silu(x):
    return jax.nn.silu(x)

def _sigmoid(x):
    return jax.nn.sigmoid(x)

def _layernorm(x, axis=-1, eps=1e-05):
    m = jnp.mean(x, axis=axis, keepdims=True)
    v = jnp.var(x, axis=axis, keepdims=True)
    return (x - m) / jnp.sqrt(v + eps)

def _scatter_add(tgt, idx, src, axis=0):
    return tgt.at[idx].add(src)

def _segment_sum(src, seg, n):
    return jax.ops.segment_sum(src, seg, n)
kernel_name = 'mk_adaln_d2_jaxref_r8_d8a1b7'

def setup_inputs(seed: int=0):
    np.random.seed(seed)
    _w = jnp.asarray

    def _L0_attn_setup():
        import jax, jax.numpy as jnp
        import numpy as np
        DT = 1.0
        N_HEAD = 16
        key = jax.random.key(seed)
        ks = jax.random.split(key, 10)
        B, T, D = (2, 256, 128)
        s = 1.0 / np.sqrt(D)
        return {'x': jax.random.normal(ks[0], (B, T, D), dtype=jnp.float32), 'Wq': jax.random.uniform(ks[1], (D, D), jnp.float32, -s, s), 'bq': jnp.zeros((D,), jnp.float32), 'Wk': jax.random.uniform(ks[2], (D, D), jnp.float32, -s, s), 'bk': jnp.zeros((D,), jnp.float32), 'Wv': jax.random.uniform(ks[3], (D, D), jnp.float32, -s, s), 'bv': jnp.zeros((D,), jnp.float32), 'Wo': jax.random.uniform(ks[4], (D, D), jnp.float32, -s, s), 'bo': jnp.zeros((D,), jnp.float32), 'alpha': jnp.float32(0.01)}
    _L0_attn_in = _L0_attn_setup()

    def _L0_ffn_setup():
        import jax, jax.numpy as jnp
        import numpy as np
        B, T, C = (4, 256, 128)
        H = 128
        E_ATT = 8
        E_MOE = 8
        I = 128
        MIN_ATT = 2
        MIN_MOE = 2
        EPS_LN = 1e-05

        def _normalize(x, axis):
            n = jnp.linalg.norm(x, axis=axis, keepdims=True)
            return x / jnp.maximum(n, 1e-12)

        def _layernorm(x, w, b):
            m = jnp.mean(x, axis=-1, keepdims=True)
            v = jnp.mean(jnp.square(x - m), axis=-1, keepdims=True)
            return (x - m) / jnp.sqrt(v + EPS_LN) * w + b

        def _gating(flat_hs, sim, gates, min_experts):
            logits = _normalize(flat_hs, -1) @ _normalize(sim, 0) - jax.nn.sigmoid(gates)
            gated = jax.nn.relu(logits)
            mask = (gated > 0).astype(gated.dtype)
            inactive = jnp.sum(mask, axis=1) == 0
            _, idx = jax.lax.top_k(logits, min_experts)
            onehot = jnp.sum(jax.nn.one_hot(idx, logits.shape[-1], dtype=gated.dtype), axis=1)
            put = inactive[:, None] & (onehot > 0)
            mask = jnp.where(put, 1.0, mask)
            masked = jnp.where(mask > 0, gated, -jnp.inf)
            return jax.nn.softmax(masked, axis=-1)
        key = jax.random.key(seed)
        ks = jax.random.split(key, 12)
        d = {}
        d['x'] = jax.random.normal(ks[0], (B, T, C), dtype=jnp.float32)
        d['ln1_w'] = jnp.ones((C,), jnp.float32)
        d['ln1_b'] = jnp.zeros((C,), jnp.float32)
        d['ln2_w'] = jnp.ones((C,), jnp.float32)
        d['ln2_b'] = jnp.zeros((C,), jnp.float32)
        d['smha_sim'] = jax.random.normal(ks[1], (C, E_ATT), dtype=jnp.float32)
        d['smha_gates'] = jnp.zeros((E_ATT,), jnp.float32)
        sq = 1.0 / np.sqrt(C + H)
        d['q_proj'] = jax.random.normal(ks[2], (E_ATT, C, H), dtype=jnp.float32) * sq
        d['k_proj'] = jax.random.normal(ks[3], (E_ATT, C, H), dtype=jnp.float32) * sq
        d['v_proj'] = jax.random.normal(ks[4], (E_ATT, C, H), dtype=jnp.float32) * sq
        d['o_proj'] = jax.random.normal(ks[5], (E_ATT, H, C), dtype=jnp.float32) * sq
        d['moe_sim'] = jax.random.normal(ks[6], (C, E_MOE), dtype=jnp.float32)
        d['moe_gates'] = jnp.zeros((E_MOE,), jnp.float32)
        d['w1'] = jax.random.normal(ks[7], (E_MOE, C, I), dtype=jnp.float32) * (1.0 / np.sqrt(C))
        d['w2'] = jax.random.normal(ks[8], (E_MOE, I, C), dtype=jnp.float32) * (1.0 / np.sqrt(I))
        return d
    _L0_ffn_in = _L0_ffn_setup()
    _L0_c = _w((lambda *s: np.random.randn(*s).astype(np.float32) * 0.05)(2, 128))
    _L0_wmod = _w((lambda *s: np.random.randn(*s).astype(np.float32) * 0.05)(128, 6 * 128) * 128 ** (-0.5))

    def _L1_attn_setup():
        import jax, jax.numpy as jnp
        import numpy as np
        D_MODEL = 128
        D_STATE = 16
        EXPAND = 2
        D_INNER = D_MODEL * EXPAND
        KSIZE = 4
        B, L = (2, 256)

        def _causal_depthwise_conv(x_bcl, W_conv, b_conv):
            y = jax.lax.conv_general_dilated(x_bcl, W_conv, window_strides=(1,), padding=[(KSIZE - 1, 0)], feature_group_count=D_INNER, dimension_numbers=('NCH', 'OIH', 'NCH'))
            return y + b_conv[None, :, None]

        def _selective_scan(x_in, dt, A, B_ssm, C_ssm):

            def step(h, inp):
                x_t, dt_t, B_t, C_t = inp
                dA = jnp.exp(dt_t[..., None] * A[None])
                dB = dt_t[..., None] * B_t[:, None, :]
                h = dA * h + dB * x_t[..., None]
                y_t = jnp.sum(h * C_t[:, None, :], axis=-1)
                return (h, y_t)
            h0 = jnp.zeros((x_in.shape[0], D_INNER, D_STATE), x_in.dtype)
            xs = (jnp.swapaxes(x_in, 0, 1), jnp.swapaxes(dt, 0, 1), jnp.swapaxes(B_ssm, 0, 1), jnp.swapaxes(C_ssm, 0, 1))
            _, ys = jax.lax.scan(step, h0, xs)
            return jnp.swapaxes(ys, 0, 1)
        key = jax.random.key(seed)
        ks = jax.random.split(key, 9)
        s = lambda fan_in: 1.0 / np.sqrt(fan_in)
        x = jax.random.normal(ks[0], (B, L, D_MODEL), dtype=jnp.float32)
        W_in = jax.random.normal(ks[1], (D_MODEL, 2 * D_INNER), dtype=jnp.float32) * s(D_MODEL)
        W_conv = jax.random.normal(ks[2], (D_INNER, 1, KSIZE), dtype=jnp.float32) * s(KSIZE)
        b_conv = jax.random.normal(ks[3], (D_INNER,), dtype=jnp.float32) * 0.01
        W_x = jax.random.normal(ks[4], (D_INNER, 2 * D_STATE + 1), dtype=jnp.float32) * s(D_INNER)
        W_dt = jax.random.normal(ks[5], (1, D_INNER), dtype=jnp.float32)
        b_dt = jax.random.normal(ks[6], (D_INNER,), dtype=jnp.float32) * 0.01
        W_out = jax.random.normal(ks[7], (D_INNER, D_MODEL), dtype=jnp.float32) * s(D_INNER)
        A_log = jnp.log(jnp.arange(1, D_STATE + 1, dtype=jnp.float32))[None, :] * jnp.ones((D_INNER, 1), jnp.float32)
        D = jnp.ones((D_INNER,), jnp.float32)
        return {'x': x, 'W_in': W_in, 'W_conv': W_conv, 'b_conv': b_conv, 'W_x': W_x, 'W_dt': W_dt, 'b_dt': b_dt, 'W_out': W_out, 'A_log': A_log, 'D': D}
    _L1_attn_in = _L1_attn_setup()

    def _L1_ffn_setup():
        import jax, jax.numpy as jnp
        import numpy as np
        B, S, H, E, K = (2, 128, 128, 8, 2)
        F = 4 * H
        key = jax.random.key(seed)
        ks = jax.random.split(key, 8)
        std = 0.02
        return {'x': jax.random.normal(ks[0], (B, S, H), jnp.float32), 'gate_w': jax.random.normal(ks[1], (E, H), jnp.float32) * (std / np.sqrt(H)), 'gate_bias': jnp.zeros((E,), jnp.float32), 'Wu': jax.random.normal(ks[2], (E, F, H), jnp.float32) * std, 'bu': jnp.zeros((E, F), jnp.float32), 'Wd': jax.random.normal(ks[3], (E, H, F), jnp.float32) * std, 'bd': jnp.zeros((E, H), jnp.float32), 'sWu': jax.random.normal(ks[4], (F, H), jnp.float32) * std, 'sbu': jnp.zeros((F,), jnp.float32), 'sWd': jax.random.normal(ks[5], (H, F), jnp.float32) * std, 'sbd': jnp.zeros((H,), jnp.float32)}
    _L1_ffn_in = _L1_ffn_setup()
    _L1_c = _w((lambda *s: np.random.randn(*s).astype(np.float32) * 0.05)(2, 128))
    _L1_wmod = _w((lambda *s: np.random.randn(*s).astype(np.float32) * 0.05)(128, 6 * 128) * 128 ** (-0.5))
    _d = {'L0_attn_x': _L0_attn_in['x'], 'L0_attn_Wq': _L0_attn_in['Wq'], 'L0_attn_bq': _L0_attn_in['bq'], 'L0_attn_Wk': _L0_attn_in['Wk'], 'L0_attn_bk': _L0_attn_in['bk'], 'L0_attn_Wv': _L0_attn_in['Wv'], 'L0_attn_bv': _L0_attn_in['bv'], 'L0_attn_Wo': _L0_attn_in['Wo'], 'L0_attn_bo': _L0_attn_in['bo'], 'L0_attn_alpha': _L0_attn_in['alpha'], 'L0_ffn_ln1_w': _L0_ffn_in['ln1_w'], 'L0_ffn_ln1_b': _L0_ffn_in['ln1_b'], 'L0_ffn_ln2_w': _L0_ffn_in['ln2_w'], 'L0_ffn_ln2_b': _L0_ffn_in['ln2_b'], 'L0_ffn_smha_sim': _L0_ffn_in['smha_sim'], 'L0_ffn_smha_gates': _L0_ffn_in['smha_gates'], 'L0_ffn_q_proj': _L0_ffn_in['q_proj'], 'L0_ffn_k_proj': _L0_ffn_in['k_proj'], 'L0_ffn_v_proj': _L0_ffn_in['v_proj'], 'L0_ffn_o_proj': _L0_ffn_in['o_proj'], 'L0_ffn_moe_sim': _L0_ffn_in['moe_sim'], 'L0_ffn_moe_gates': _L0_ffn_in['moe_gates'], 'L0_ffn_w1': _L0_ffn_in['w1'], 'L0_ffn_w2': _L0_ffn_in['w2'], 'L0_c': _L0_c, 'L0_wmod': _L0_wmod, 'L1_attn_W_in': _L1_attn_in['W_in'], 'L1_attn_W_conv': _L1_attn_in['W_conv'], 'L1_attn_b_conv': _L1_attn_in['b_conv'], 'L1_attn_W_x': _L1_attn_in['W_x'], 'L1_attn_W_dt': _L1_attn_in['W_dt'], 'L1_attn_b_dt': _L1_attn_in['b_dt'], 'L1_attn_W_out': _L1_attn_in['W_out'], 'L1_attn_A_log': _L1_attn_in['A_log'], 'L1_attn_D': _L1_attn_in['D'], 'L1_ffn_gate_w': _L1_ffn_in['gate_w'], 'L1_ffn_gate_bias': _L1_ffn_in['gate_bias'], 'L1_ffn_Wu': _L1_ffn_in['Wu'], 'L1_ffn_bu': _L1_ffn_in['bu'], 'L1_ffn_Wd': _L1_ffn_in['Wd'], 'L1_ffn_bd': _L1_ffn_in['bd'], 'L1_ffn_sWu': _L1_ffn_in['sWu'], 'L1_ffn_sbu': _L1_ffn_in['sbu'], 'L1_ffn_sWd': _L1_ffn_in['sWd'], 'L1_ffn_sbd': _L1_ffn_in['sbd'], 'L1_c': _L1_c, 'L1_wmod': _L1_wmod}
    _x0 = _d['L0_attn_x']
    _d['L0_attn_x'] = jax.random.normal(jax.random.fold_in(jax.random.key(seed), 1), (2, 1024, 128), dtype=_x0.dtype)
    del _x0
    return _d

def reference(L0_attn_x, L0_attn_Wq, L0_attn_bq, L0_attn_Wk, L0_attn_bk, L0_attn_Wv, L0_attn_bv, L0_attn_Wo, L0_attn_bo, L0_attn_alpha, L0_ffn_ln1_w, L0_ffn_ln1_b, L0_ffn_ln2_w, L0_ffn_ln2_b, L0_ffn_smha_sim, L0_ffn_smha_gates, L0_ffn_q_proj, L0_ffn_k_proj, L0_ffn_v_proj, L0_ffn_o_proj, L0_ffn_moe_sim, L0_ffn_moe_gates, L0_ffn_w1, L0_ffn_w2, L0_c, L0_wmod, L1_attn_W_in, L1_attn_W_conv, L1_attn_b_conv, L1_attn_W_x, L1_attn_W_dt, L1_attn_b_dt, L1_attn_W_out, L1_attn_A_log, L1_attn_D, L1_ffn_gate_w, L1_ffn_gate_bias, L1_ffn_Wu, L1_ffn_bu, L1_ffn_Wd, L1_ffn_bd, L1_ffn_sWu, L1_ffn_sbu, L1_ffn_sWd, L1_ffn_sbd, L1_c, L1_wmod):

    def _L0_attn_ref(x, Wq, bq, Wk, bk, Wv, bv, Wo, bo, alpha):
        import jax, jax.numpy as jnp
        import numpy as np
        DT = 1.0
        N_HEAD = 16
        B, T, D = x.shape
        H = N_HEAD
        hd = D // H
        scale = hd ** (-0.5)
        q = (x @ Wq.T + bq).reshape(B, T, H, hd)
        k = (x @ Wk.T + bk).reshape(B, T, H, hd)
        v = (x @ Wv.T + bv).reshape(B, T, H, hd)
        scores = jnp.einsum('bqhd,bkhd->bhqk', q, k) * scale
        idx = jnp.arange(T)
        lag = jnp.abs(idx[:, None] - idx[None, :]).astype(jnp.float32)
        decay = jnp.exp(-alpha * lag * DT)
        scores = scores * decay
        attn = jax.nn.softmax(scores, axis=-1)
        out = jnp.einsum('bhqk,bkhd->bqhd', attn, v).reshape(B, T, D)
        return out @ Wo.T + bo

    def _L0_ffn_ref(x, ln1_w, ln1_b, ln2_w, ln2_b, smha_sim, smha_gates, q_proj, k_proj, v_proj, o_proj, moe_sim, moe_gates, w1, w2):
        import jax, jax.numpy as jnp
        import numpy as np
        B, T, C = (4, 256, 128)
        H = 128
        E_ATT = 8
        E_MOE = 8
        I = 128
        MIN_ATT = 2
        MIN_MOE = 2
        EPS_LN = 1e-05

        def _normalize(x, axis):
            n = jnp.linalg.norm(x, axis=axis, keepdims=True)
            return x / jnp.maximum(n, 1e-12)

        def _layernorm(x, w, b):
            m = jnp.mean(x, axis=-1, keepdims=True)
            v = jnp.mean(jnp.square(x - m), axis=-1, keepdims=True)
            return (x - m) / jnp.sqrt(v + EPS_LN) * w + b

        def _gating(flat_hs, sim, gates, min_experts):
            logits = _normalize(flat_hs, -1) @ _normalize(sim, 0) - jax.nn.sigmoid(gates)
            gated = jax.nn.relu(logits)
            mask = (gated > 0).astype(gated.dtype)
            inactive = jnp.sum(mask, axis=1) == 0
            _, idx = jax.lax.top_k(logits, min_experts)
            onehot = jnp.sum(jax.nn.one_hot(idx, logits.shape[-1], dtype=gated.dtype), axis=1)
            put = inactive[:, None] & (onehot > 0)
            mask = jnp.where(put, 1.0, mask)
            masked = jnp.where(mask > 0, gated, -jnp.inf)
            return jax.nn.softmax(masked, axis=-1)
        b, t, c = x.shape
        n1 = _layernorm(x, ln1_w, ln1_b)
        rw = _gating(n1.reshape(b * t, c), smha_sim, smha_gates, MIN_ATT).reshape(b, t, -1)
        q = jnp.einsum('btc,ech,bte->bth', n1, q_proj, rw)
        k = jnp.einsum('btc,ech,bte->bth', n1, k_proj, rw)
        v = jnp.einsum('btc,ech,bte->bth', n1, v_proj, rw)
        scale = 1.0 / jnp.sqrt(jnp.asarray(q.shape[-1], q.dtype))
        scores = jnp.einsum('bth,bsh->bts', q, k) * scale
        causal = jnp.tril(jnp.ones((t, t), dtype=bool))
        scores = jnp.where(causal, scores, -jnp.inf)
        attn = jnp.einsum('bts,bsh->bth', jax.nn.softmax(scores, axis=-1), v)
        attn_out = jnp.einsum('bth,ehc,bte->btc', attn, o_proj, rw)
        hs = x + attn_out
        n2 = _layernorm(hs, ln2_w, ln2_b)
        rw2 = _gating(n2.reshape(b * t, c), moe_sim, moe_gates, MIN_MOE).reshape(b, t, -1)
        inter = jax.nn.gelu(jnp.einsum('btc,eci->btei', n2, w1), approximate=False)
        moe_out = jnp.einsum('btei,eic,bte->btc', inter, w2, rw2)
        return hs + moe_out

    def _L1_attn_ref(x, W_in, W_conv, b_conv, W_x, W_dt, b_dt, W_out, A_log, D):
        import jax, jax.numpy as jnp
        import numpy as np
        D_MODEL = 128
        D_STATE = 16
        EXPAND = 2
        D_INNER = D_MODEL * EXPAND
        KSIZE = 4
        B, L = (2, 256)

        def _causal_depthwise_conv(x_bcl, W_conv, b_conv):
            y = jax.lax.conv_general_dilated(x_bcl, W_conv, window_strides=(1,), padding=[(KSIZE - 1, 0)], feature_group_count=D_INNER, dimension_numbers=('NCH', 'OIH', 'NCH'))
            return y + b_conv[None, :, None]

        def _selective_scan(x_in, dt, A, B_ssm, C_ssm):

            def step(h, inp):
                x_t, dt_t, B_t, C_t = inp
                dA = jnp.exp(dt_t[..., None] * A[None])
                dB = dt_t[..., None] * B_t[:, None, :]
                h = dA * h + dB * x_t[..., None]
                y_t = jnp.sum(h * C_t[:, None, :], axis=-1)
                return (h, y_t)
            h0 = jnp.zeros((x_in.shape[0], D_INNER, D_STATE), x_in.dtype)
            xs = (jnp.swapaxes(x_in, 0, 1), jnp.swapaxes(dt, 0, 1), jnp.swapaxes(B_ssm, 0, 1), jnp.swapaxes(C_ssm, 0, 1))
            _, ys = jax.lax.scan(step, h0, xs)
            return jnp.swapaxes(ys, 0, 1)
        xz = x @ W_in
        x_in, z = jnp.split(xz, 2, axis=-1)
        x_in = jnp.swapaxes(_causal_depthwise_conv(jnp.swapaxes(x_in, 1, 2), W_conv, b_conv), 1, 2)
        x_in = jax.nn.silu(x_in)
        xBC = x_in @ W_x
        dt_raw = xBC[..., :1]
        B_ssm = xBC[..., 1:1 + D_STATE]
        C_ssm = xBC[..., 1 + D_STATE:]
        dt = jax.nn.softplus(dt_raw @ W_dt + b_dt)
        A = -jnp.exp(A_log)
        y = _selective_scan(x_in, dt, A, B_ssm, C_ssm)
        y = y + D[None, None, :] * x_in
        return y * jax.nn.silu(z) @ W_out

    def _L1_ffn_ref(x, gate_w, gate_bias, Wu, bu, Wd, bd, sWu, sbu, sWd, sbd):
        import jax, jax.numpy as jnp
        import numpy as np
        B, S, H, E, K = (2, 128, 128, 8, 2)
        F = 4 * H
        b, s, h = x.shape
        x_flat = x.reshape(-1, h)
        T = x_flat.shape[0]
        scores = jax.nn.sigmoid(x_flat @ gate_w.T + gate_bias)
        top_scores, top_idx = jax.lax.top_k(scores, K)
        top_scores = top_scores / (top_scores.sum(-1, keepdims=True) + 1e-06)
        w = jnp.zeros((T, E), x.dtype).at[jnp.arange(T)[:, None], top_idx].add(top_scores)
        h1 = jnp.einsum('th,efh->etf', x_flat, Wu) + bu[:, None, :]
        a1 = jax.nn.gelu(h1, approximate=False)
        y = jnp.einsum('etf,ehf->eth', a1, Wd) + bd[:, None, :]
        combined = jnp.einsum('te,eth->th', w, y)
        sh = jax.nn.gelu(x_flat @ sWu.T + sbu, approximate=False)
        shared = (sh @ sWd.T + sbd) * 0.1
        return (combined + shared).reshape(b, s, h)
    x = L0_attn_x
    mod = (_silu(L0_c) @ L0_wmod).reshape(L0_c.shape[0], 6, 1, -1)
    sa, ca, ga, sb, cb, gb = (mod[:, 0], mod[:, 1], mod[:, 2], mod[:, 3], mod[:, 4], mod[:, 5])
    ga = (2 * (ga >= 0) - 1) * jnp.maximum(jnp.abs(ga), 0.25)
    gb = (2 * (gb >= 0) - 1) * jnp.maximum(jnp.abs(gb), 0.25)
    h = _layernorm(x, axis=-1) * (1 + ca) + sa
    x = x + ga * _L0_attn_ref(h, L0_attn_Wq, L0_attn_bq, L0_attn_Wk, L0_attn_bk, L0_attn_Wv, L0_attn_bv, L0_attn_Wo, L0_attn_bo, L0_attn_alpha)
    h = _layernorm(x, axis=-1) * (1 + cb) + sb
    x = x + gb * _L0_ffn_ref(h, L0_ffn_ln1_w, L0_ffn_ln1_b, L0_ffn_ln2_w, L0_ffn_ln2_b, L0_ffn_smha_sim, L0_ffn_smha_gates, L0_ffn_q_proj, L0_ffn_k_proj, L0_ffn_v_proj, L0_ffn_o_proj, L0_ffn_moe_sim, L0_ffn_moe_gates, L0_ffn_w1, L0_ffn_w2)
    mod = (_silu(L1_c) @ L1_wmod).reshape(L1_c.shape[0], 6, 1, -1)
    sa, ca, ga, sb, cb, gb = (mod[:, 0], mod[:, 1], mod[:, 2], mod[:, 3], mod[:, 4], mod[:, 5])
    ga = (2 * (ga >= 0) - 1) * jnp.maximum(jnp.abs(ga), 0.25)
    gb = (2 * (gb >= 0) - 1) * jnp.maximum(jnp.abs(gb), 0.25)
    h = _layernorm(x, axis=-1) * (1 + ca) + sa
    x = x + ga * _L1_attn_ref(h, L1_attn_W_in, L1_attn_W_conv, L1_attn_b_conv, L1_attn_W_x, L1_attn_W_dt, L1_attn_b_dt, L1_attn_W_out, L1_attn_A_log, L1_attn_D)
    h = _layernorm(x, axis=-1) * (1 + cb) + sb
    x = x + gb * _L1_ffn_ref(h, L1_ffn_gate_w, L1_ffn_gate_bias, L1_ffn_Wu, L1_ffn_bu, L1_ffn_Wd, L1_ffn_bd, L1_ffn_sWu, L1_ffn_sbu, L1_ffn_sWd, L1_ffn_sbd)
    return x

_drawn_inputs = setup_inputs


def setup_inputs(seed=0):
    import zlib

    import numpy as np

    out = dict(_drawn_inputs(seed))
    spreads = {'L0_attn_bq': (0.0, 0.8),
     'L0_attn_bk': (0.0, 0.8),
     'L0_attn_bv': (0.0, 0.361),
     'L0_attn_bo': (0.0, 0.1),
     'L0_ffn_ln1_w': (1.0, 0.6),
     'L0_ffn_ln1_b': (0.0, 0.421),
     'L0_ffn_ln2_w': (1.0, 0.2),
     'L0_ffn_ln2_b': (0.0, 0.29),
     'L0_ffn_smha_gates': (0.0, 0.418),
     'L0_ffn_moe_gates': (0.0, 0.1),
     'L1_attn_D': (1.0, 0.6),
     'L1_ffn_gate_bias': (0.0, 0.357),
     'L1_ffn_bu': (0.0, 0.8),
     'L1_ffn_bd': (0.0, 0.451),
     'L1_ffn_sbu': (0.0, 2.0),
     'L1_ffn_sbd': (0.0, 2.0)}
    factors = {'L0_attn_Wq': 8.0,
     'L0_attn_Wk': 8.0,
     'L0_attn_Wv': 7.462,
     'L0_attn_Wo': 2.933,
     'L0_ffn_q_proj': 6.637,
     'L0_ffn_k_proj': 5.406,
     'L1_attn_b_conv': 25.719,
     'L1_attn_b_dt': 52.087,
     'L1_ffn_gate_w': 4.97,
     'L1_ffn_Wu': 6.177,
     'L1_ffn_Wd': 5.597,
     'L1_ffn_sWu': 8.0,
     'L1_ffn_sWd': 8.0,
     'L1_attn_A_log': 2.839}
    for name, (base, spread) in spreads.items():
        noise = np.random.default_rng([zlib.crc32(name.encode()), seed]).standard_normal(out[name].shape)
        drawn = base * np.exp(spread * noise) if base else spread * noise
        out[name] = jnp.asarray(drawn.astype(out[name].dtype))
    for name, factor in factors.items():
        out[name] = (out[name] * factor).astype(out[name].dtype)
    return out
```

```python
from collections import namedtuple
from contextlib import ExitStack

import numpy as np
import concourse.bass as bass
from concourse import mybir

F32 = mybir.dt.float32
BF16 = mybir.dt.bfloat16
ALU = mybir.AluOpType
ACT = mybir.ActivationFunctionType
AX = mybir.AxisListType

P = 128
B, T, D = 2, 1024, 128
N = B * T
SUP = 512
NSUP = N // SUP
SUPB = T // SUP
NBLK = N // P
BLKS = SUP // P
NH, HD = 16, 8
HG = 4
NG = NH // HG
QB = T // P
E = 8
DI, DS, KC = 256, 16, 4
HALVES = DI // P
F = 512
FC = F // P
EPS = 1e-5
NEG = -3.0e38
NPART = 3
TERMS = [(0, 0), (0, 1), (1, 0), (0, 2), (2, 0), (1, 1), (1, 2), (2, 1)]
STACK = len(TERMS) * HD

PRIMED = 1


def columns(parts):
    at, out = 0, {}
    for name, width in parts:
        out[name] = (at, width)
        at += width
    return out, at


ATT_COLS, ATT_W = columns([
    ("wq", D), ("wk", D), ("wv", D), ("wo", D), ("wmod0", 6 * D), ("wmod1", 6 * D), ("c", 2 * B),
    ("bq", 1), ("bk", 1), ("bv", 1), ("bo", 1), ("ln1w", 1), ("ln1b", 1), ("ln2w", 1), ("ln2b", 1),
    ("smha_sim", E), ("moe_sim", E)])
FFN_COLS, FFN_W = columns([
    ("qp", E * D), ("kp", E * D), ("vp", E * D), ("op", E * D), ("w1", E * D), ("w2", E * D)])
L1_COLS, L1_W = columns([
    ("w_in", 2 * DI), ("w_x", HALVES * (2 * DS + 1)), ("w_out", HALVES * D), ("b_conv", HALVES), ("w_dt", HALVES),
    ("b_dt", HALVES), ("a_log", HALVES * DS), ("dskip", HALVES), ("gate_w", E), ("wu", E * F), ("bu", E * FC),
    ("wd", E * F), ("swu", F), ("sbu", FC), ("swd", F), ("sbd", 1), ("bd", D)])
ROW_COLS, ROW_W = columns([("alpha", 1), ("smha_gates", E), ("moe_gates", E), ("gate_bias", E), ("w_conv", KC * DI)])


class Shared:
    pass


def semaphores(sem, prefix, names):
    return namedtuple("Semaphores", names)(*[sem(prefix + name) for name in names])


class Steps:

    def __init__(self, sem):
        self.sem, self.count = sem, 0

    def on(self, engine):
        def step(ins):
            self.count += 1
            ins.then_inc(self.sem, 1)
            engine.wait_ge(self.sem, self.count)
        return step


def apart(engine):
    engine.nop(nofuse=True)


def prime(engine, *sems):
    for sem in sems:
        engine.nop(nofuse=True).then_inc(sem, PRIMED)


def build(nc, att_in, ffn_in, l1_in, row_in, x_in, out):
    ctx = ExitStack()
    with ctx:
        def sb(name, shape, dt=F32):
            return ctx.enter_context(nc.sbuf_tensor(name, shape, dt))

        def sem(name):
            return ctx.enter_context(nc.semaphore(name))

        m = Shared()
        m.nc, m.sem, m.out = nc, sem, out
        m.xC = sb("xC", [P, N])
        m.att = sb("att_tile", [P, ATT_W])
        m.ffn = sb("ffn_tile", [P, FFN_W])
        m.late = sb("late", [P, L1_W])
        m.row = sb("row", [P, ROW_W])
        m.ident = sb("ident", [P, P])
        m.ones = sb("ones", [P, P])
        m.causal = sb("causal", [P, P])
        m.tri = sb("tri", [P, E * E])
        m.sel_e = sb("sel_e", [NPART * E, E, P], BF16)
        m.mod = sb("mod", [P, 2 * 6 * B])
        m.gsign = sb("gsign", [P, 2 * 6 * B])
        m.gate = sb("gate", [P, 2 * 6 * B])
        m.small = sb("small", [P, 64])
        m.eps = m.small[:, 2:3]
        m.rowg = sb("rowg", [P, 2 * E])
        m.rwT = sb("rwT", [NPART * E, N], BF16)
        m.arena = sb("arena", [P, 27600])
        m.bank = [ctx.enter_context(nc.psum_tensor(f"bank{i}", [P, 2 * SUP], F32)) for i in range(4)]
        m.stackq = nc.dram_tensor("stackq", [NH, STACK, N], BF16).ap()
        m.stackk = nc.dram_tensor("stackk", [NH, STACK, N], BF16).ap()
        m.att_in, m.ffn_in, m.l1_in, m.row_in, m.x_in = att_in, ffn_in, l1_in, row_in, x_in
        m.dve = Steps(sem("dve_step"))
        m.act = Steps(sem("act_step"))
        m.pool = Steps(sem("pool_step"))
        m.att_loaded, m.ffn_loaded, m.l1_loaded = sem("att_loaded"), sem("ffn_loaded"), sem("l1_loaded")
        m.ln = semaphores(sem, "ln_", ("raw_T", "var", "std", "norm", "out_T"))
        m.gt = semaphores(sem, "gate_", ("sq", "simsq", "simstd", "sim", "logits", "norms", "act_out", "act_in", "split",
                                        "splitT"))
        m.ln_calls = m.gt_calls = 0

        def a(name):
            at, w = ATT_COLS[name]
            return m.att[:, at:at + w]

        def f(name):
            at, w = FFN_COLS[name]
            return m.ffn[:, at:at + w]

        def l(name):
            at, w = L1_COLS[name]
            return m.late[:, at:at + w]

        def r(name):
            at, w = ROW_COLS[name]
            return m.row[:, at:at + w]

        m.a, m.f, m.l, m.r = a, f, l, r
        ar = m.arena

        load_and_constants(m)
        modulation(m)
        hC = ar[:, 0:N]
        layer_norm(m, m.xC, lambda s: hC[:, s * SUP:(s + 1) * SUP], lambda s: m.scale1(0, 1, s), lambda s: m.shift(0, 0, s), tmp=2 * N)
        head_projections(m, hC)
        decayed_attention(m)
        attention_output(m)
        feed_forward(m)
        mixer(m)
        experts(m)



def load_and_constants(m):
    nc = m.nc
    zeroed, lag_ready, negalpha = m.sem("zeroed"), m.sem("lag_ready"), m.sem("negalpha")
    vaug, decay = attention_tiles(m).vaug, attention_tiles(m).decay
    m.decay_ready = m.sem("decay_ready")
    with nc.Block() as block:
        @block.sync
        def _(sp):
            sp.dma_start(m.att[:, :], m.att_in).then_inc(m.att_loaded, 16)
            sp.dma_start(m.row[:, :], m.row_in.partition_broadcast(P)).then_inc(m.att_loaded, 16)
            sp.dma_start(m.xC[:, :], m.x_in).then_inc(m.att_loaded, 16)
            sp.dma_start(m.ffn[:, :], m.ffn_in).then_inc(m.ffn_loaded, 16)
            sp.wait_ge(m.att_loaded, 48)

        @block.gpsimd
        def _(pool):
            step = m.pool.on(pool)
            nc.gpsimd.memset(m.ident[:, :], 0.0)
            nc.gpsimd.memset(m.causal[:, :], 0.0)
            nc.gpsimd.memset(m.sel_e[:, :, :], 0.0)
            nc.gpsimd.memset(m.ones[:, :], 1.0)
            nc.gpsimd.memset(m.eps, EPS)
            nc.gpsimd.memset(vaug[:, :, :, HD:HD + 1], 1.0)
            step(nc.gpsimd.memset(m.small[:, 3:4], 0.0))
            (nc.gpsimd.iota(decay[:, :], pattern=[[1, 2 * T - P]], base=-(T - P), channel_multiplier=-1,
                                allow_small_or_imprecise_dtypes=True)).then_inc(lag_ready, 1)
            nc.gpsimd.affine_select(out=m.ident[:, :], in_=m.ident[:, :], compare_op=ALU.not_equal, fill=1.0,
                                    base=0, pattern=[[-1, P]], channel_multiplier=1)
            nc.gpsimd.affine_select(out=m.causal[:, :], in_=m.causal[:, :], compare_op=ALU.is_ge, fill=NEG,
                                    base=0, pattern=[[-1, P]], channel_multiplier=1)
            for part in range(NPART):
                step(nc.gpsimd.affine_select(out=m.sel_e[:, :, :], in_=m.sel_e[:, :, :], compare_op=ALU.not_equal,
                                             fill=1.0, base=-part * E, pattern=[[-1, E], [0, P]],
                                             channel_multiplier=1))
            step(nc.gpsimd.iota(m.tri[:, :], pattern=[[1, E], [-1, E]], base=0, channel_multiplier=0,
                                allow_small_or_imprecise_dtypes=True))

        @block.vector
        def _(dve):
            dve.wait_ge(m.att_loaded, 48)
            nc.vector.tensor_scalar(m.small[:, 0:1], m.r("alpha"), -1.0, None, ALU.mult).then_inc(negalpha, 1)

        @block.scalar
        def _(act):
            act.wait_ge(lag_ready, 1)
            step = m.act.on(act)
            step(nc.scalar.activation(decay[:, :], decay[:, :], ACT.Abs))
            act.wait_ge(negalpha, 1)
            nc.scalar.activation(decay[:, :], decay[:, :], ACT.Exp, scale=m.small[:, 0:1])
            nc.scalar.activation(m.rowg[:, 0:2 * E], m.row[:, ROW_COLS["smha_gates"][0]:ROW_COLS["smha_gates"][0] + 2 * E],
                                 ACT.Sigmoid)


def modulation(m):
    nc = m.nc
    silu_ready, mod_summed = m.sem("silu_ready"), m.sem("mod_summed")
    silu_c = m.small[:, 4:4 + 2 * B]
    ps = m.bank[0]
    W = 2 * 6 * B
    with nc.Block() as block:
        @block.scalar
        def _(act):
            nc.scalar.activation(silu_c, m.a("c"), ACT.Silu).then_inc(silu_ready, 1)

        @block.tensor
        def _(pe):
            pe.wait_ge(silu_ready, 1)
            for layer in range(2):
                w = m.a(f"wmod{layer}")
                for j in range(6):
                    at = (layer * 6 + j) * B
                    mm = nc.tensor.matmul(ps[:, at:at + B], w[:, j * D:(j + 1) * D],
                                          silu_c[:, layer * B:(layer + 1) * B], start=True, stop=True)
            mm.then_inc(mod_summed, 1)

        @block.vector
        def _(dve):
            step = m.dve.on(dve)
            nc.vector.tensor_scalar(m.tri[:, :], m.tri[:, :], 0.0, None, ALU.is_gt)
            dve.wait_ge(mod_summed, 1)
            step(nc.vector.tensor_copy(m.mod[:, :], ps[:, 0:W]))
            step(nc.vector.tensor_scalar(m.gsign[:, :], m.mod[:, :], 0.0, 2.0, ALU.is_ge, ALU.mult))
            step(nc.vector.scalar_tensor_tensor(out=m.gate[:, :], in0=m.mod[:, :], scalar=-1.0, in1=m.mod[:, :],
                                                op0=ALU.mult, op1=ALU.max))
            step(nc.vector.tensor_scalar(m.gate[:, :], m.gate[:, :], 0.25, None, ALU.max))
            step(nc.vector.scalar_tensor_tensor(out=m.gate[:, :], in0=m.gsign[:, :], scalar=-1.0, in1=m.gate[:, :],
                                                op0=ALU.add, op1=ALU.mult))
            step(nc.vector.tensor_scalar(m.gsign[:, :], m.mod[:, :], 1.0, None, ALU.add))
            step(nc.vector.tensor_scalar(m.small[:, 1:2], m.a("bq"), float(HD) ** -0.5, None, ALU.mult))

    def column(tile, layer, j, b):
        at = (layer * 6 + j) * B + b
        return tile[:, at:at + 1]

    m.scale1 = lambda layer, j, s: column(m.gsign, layer, j, s // SUPB)
    m.shift = lambda layer, j, s: column(m.mod, layer, j, s // SUPB)
    m.gated = lambda layer, j, s: column(m.gate, layer, j, s // SUPB)



def layer_norm(m, src, dst, scale, bias, tmp):
    nc, ln = m.nc, m.ln
    call = m.ln_calls
    m.ln_calls += 1
    c4, c1 = call * NSUP, call * NBLK
    t0 = tmp
    xn = m.arena[:, t0:t0 + NSUP * SUP].rearrange("p (s j c) -> p s j c", s=NSUP, j=BLKS)
    t1 = t0 + NSUP * SUP
    stats = m.arena[:, t1:t1 + 96].rearrange("p (k c) -> p k c", c=6)
    mv = m.arena[:, t1 + 96:t1 + 128].rearrange("p (k c) -> p k c", c=2)
    std = m.small[:, 8:8 + NBLK]
    rstd = m.small[:, 24:24 + NBLK]
    raw = lambda s: m.bank[s // 2][:, (s % 2) * SUP:(s % 2 + 1) * SUP]
    back = lambda s: m.bank[2 + s // 2][:, (s % 2) * SUP:(s % 2 + 1) * SUP]
    with nc.Block() as block:
        @block.tensor
        def _(pe):
            for s in range(NSUP):
                for j in range(BLKS):
                    at = s * SUP + j * P
                    mm = nc.tensor.transpose(raw(s)[:, j * P:(j + 1) * P], src[:, at:at + P], m.ident[:, :])
                mm.then_inc(ln.raw_T, 1)
            for s in range(NSUP):
                pe.wait_ge(ln.norm, c4 + s + 1)
                for j in range(BLKS):
                    mm = nc.tensor.transpose(back(s)[:, j * P:(j + 1) * P], xn[:, s, j, :], m.ident[:, :])
                mm.then_inc(ln.out_T, 1)

        @block.vector
        def _(dve):
            step = m.dve.on(dve)

            def statistics(s):
                dve.wait_ge(ln.raw_T, c4 + s + 1)
                for j in range(BLKS):
                    ins = nc.vector.bn_stats(stats[:, s * BLKS + j, :], raw(s)[:, j * P:(j + 1) * P])
                step(ins)
                for j in range(BLKS):
                    ins = nc.vector.bn_aggr(mv[:, s * BLKS + j, :], stats[:, s * BLKS + j, :])
                ins.then_inc(ln.var, 1)

            def normalise(s):
                k0 = s * BLKS
                dve.wait_ge(ln.std, c4 + s + 1)
                step(nc.vector.reciprocal(rstd[:, k0:k0 + BLKS], std[:, k0:k0 + BLKS]))
                for j in range(BLKS):
                    k = k0 + j
                    ins = nc.vector.tensor_scalar(xn[:, s, j, :], raw(s)[:, j * P:(j + 1) * P], mv[:, k, 0:1],
                                                  rstd[:, k:k + 1], ALU.subtract, ALU.mult)
                ins.then_inc(ln.norm, 1)

            statistics(0)
            for s in range(1, NSUP):
                statistics(s)
                normalise(s - 1)
            normalise(NSUP - 1)

        @block.scalar
        def _(act):
            for s in range(NSUP):
                k0 = s * BLKS
                act.wait_ge(ln.var, c4 + s + 1)
                nc.scalar.activation(std[:, k0:k0 + BLKS], mv[:, k0:k0 + BLKS, 1], ACT.Sqrt,
                                     bias=m.eps[:, 0:1]).then_inc(ln.std, 1)
            for s in range(NSUP):
                act.wait_ge(ln.out_T, c4 + s + 1)
                nc.scalar.activation(dst(s), back(s), ACT.Identity, bias=bias(s), scale=scale(s))



def attention_tiles(m):
    ar = m.arena
    t = Shared()
    at = 0

    def take(width):
        nonlocal at
        at += width
        return ar[:, at - width:at]

    t.kpad = take(2 * HG * T // 2).bitcast(BF16).rearrange("p (u h k) -> p u h k", u=2, h=HG)
    t.qpair = take(2 * 2 * T // 2).bitcast(BF16).rearrange("p (u h q) -> p u h q", u=2, h=2)
    t.weighted = take(4 * T).rearrange("p (u k) -> p u k", u=4)
    t.probsT = take(2 * HG * QB * P).rearrange("p (u h k q) -> p u h k q", u=2, h=HG, k=QB)
    t.vstat = take(2 * QB * HG * 32).rearrange("p (u k h c) -> p u k h c", u=2, k=QB, h=HG)
    t.vaug = take(NBLK * NH * (HD + 1)).rearrange("p (k h c) -> p k h c", k=NBLK, h=NH)
    t.decay = take(2 * T - P)
    assert at <= ar.shape[1], at
    t.raw = m.late[:, 0:B * NG * QB * P].rearrange("p (n q) -> p n q", q=P)
    return t


def head_projections(m, hC):
    nc, t = m.nc, attention_tiles(m)
    s_q, s_k, s_v = m.sem("q_summed"), m.sem("k_summed"), m.sem("v_summed")
    s_first, s_second, s_third = m.sem("part1_ready"), m.sem("part2_ready"), m.sem("part3_ready")
    s_rest, s_qk_free, s_v_free = m.sem("rest_ready"), m.sem("qk_free"), m.sem("v_free")
    stored = m.sem("parts_stored")
    m.stacked = stored
    base = N
    full = [m.arena[:, base + i * N:base + (i + 1) * N] for i in range(2)]
    rest = [m.arena[:, base + (2 + i) * N:base + (3 + i) * N] for i in range(2)]
    parts = [[m.arena[:, base + 4 * N + (i * NPART + j) * N // 2:base + 4 * N + (i * NPART + j + 1) * N // 2].bitcast(BF16)
              for j in range(NPART)] for i in range(2)]
    assert base + 4 * N + 2 * NPART * N // 2 <= m.arena.shape[1] - (2 * T - P) - NBLK * NH * (HD + 1)
    sup = lambda tile, s: tile[:, s * SUP:(s + 1) * SUP]
    half = lambda tile, s: tile[:, (s % 2) * SUP:(s % 2 + 1) * SUP]
    with nc.Block() as block:
        @block.tensor
        def _(pe):
            for s in range(NSUP):
                if s >= 2:
                    pe.wait_ge(s_qk_free, 2 * (s - 1))
                    pe.wait_ge(s_v_free, s - 1)
                nc.tensor.matmul(half(m.bank[0], s), m.a("wq"), sup(hC, s), start=True, stop=True).then_inc(s_q, 1)
                nc.tensor.matmul(half(m.bank[1], s), m.a("wk"), sup(hC, s), start=True, stop=True).then_inc(s_k, 1)
                for j in range(BLKS):
                    at = s * SUP + j * P
                    mm = nc.tensor.matmul(half(m.bank[2], s)[:, j * P:(j + 1) * P], hC[:, at:at + P], m.a("wv"),
                                          start=True, stop=True)
                mm.then_inc(s_v, 1)

        @block.scalar
        def _(act):
            for s in range(NSUP):
                act.wait_ge(s_q, s + 1)
                nc.scalar.activation(sup(full[0], s), half(m.bank[0], s), ACT.Identity, bias=m.small[:, 1:2],
                                     scale=float(HD) ** -0.5)
                nc.scalar.activation(sup(parts[0][0], s), half(m.bank[0], s), ACT.Identity, bias=m.small[:, 1:2],
                                     scale=float(HD) ** -0.5).then_inc(s_qk_free, 1)
                act.wait_ge(s_k, s + 1)
                nc.scalar.activation(sup(full[1], s), half(m.bank[1], s), ACT.Identity, bias=m.a("bk"))
                nc.scalar.activation(sup(parts[1][0], s), half(m.bank[1], s), ACT.Identity,
                                     bias=m.a("bk")).then_inc(s_qk_free, 1)
                for i in range(2):
                    act.wait_ge(s_rest, 2 * s + i + 1)
                    nc.scalar.activation(sup(parts[i][1], s), sup(rest[i], s), ACT.Copy).then_inc(s_second, 1)

        @block.vector
        def _(dve):
            for s in range(NSUP):
                for i in range(2):
                    dve.wait_ge(s_qk_free, 2 * s + i + 1)
                    nc.vector.tensor_tensor(sup(rest[i], s), sup(full[i], s), sup(parts[i][0], s),
                                            ALU.subtract).then_inc(s_rest, 1)
                dve.wait_ge(s_v, s + 1)
                nc.vector.tensor_copy(
                    t.vaug[:, s * BLKS:(s + 1) * BLKS, :, 0:HD].rearrange("p k h c -> p (k h) c"),
                    half(m.bank[2], s).rearrange("p (k c) -> p k c", c=HD)).then_inc(s_v_free, 1)
                for i in range(2):
                    dve.wait_ge(s_second, 2 * s + i + 1)
                    nc.vector.tensor_tensor(sup(parts[i][2], s), sup(rest[i], s), sup(parts[i][1], s),
                                            ALU.subtract).then_inc(s_third, 1)

        @block.sync
        def _(sp):
            for b in range(B):
                sp.wait_ge(s_third, 2 * SUPB * (b + 1))
                for row, pair in enumerate(TERMS):
                    for i, stack in enumerate((m.stackq, m.stackk)):
                        sp.dma_start(stack[:, row * HD:(row + 1) * HD, b * T:(b + 1) * T],
                                     parts[i][pair[i]][:, b * T:(b + 1) * T]).then_inc(stored, 16)
            sp.wait_ge(stored, 2 * B * len(TERMS) * 16)


def decayed_attention(m):
    nc, t = m.nc, attention_tiles(m)
    names = ("scored", "weighted", "negmax", "exped", "turnedA", "turnedB", "copiedA", "copiedB", "pv_done",
             "raw_saved", "v_early", "v_late", "group_loaded", "tiles_zeroed")
    z = semaphores(m.sem, "att_", names)
    negm = m.small[:, 8:16]
    rowmax = m.small[:, 16:24]
    score = [m.bank[0], m.bank[1]]
    turnA, turnB = m.bank[2][:, 0:SUP], m.bank[2][:, SUP:2 * SUP]
    pv = [m.bank[3][:, 0:P], m.bank[3][:, SUP:SUP + P]]
    KB = QB // 2
    GROUPS = B * NG

    def every_group(engine, steps):
        steps(0)
        with engine.Fori(1, GROUPS - 1) as g:
            steps(g)
        steps(GROUPS - 1)

    with nc.Block() as block:
        @block.sync
        def _(sp):
            def load(g):
                b, hg, u = g // NG, g % NG, g % 2
                qsrc = m.stackq[:, :, b * T:(b + 1) * T].rearrange("(g j w) r k -> g (w r) j k", g=NG, w=2)
                sp.dma_start(t.qpair[:, u], qsrc[hg]).then_inc(z.group_loaded, 16)
                ksrc = m.stackk[:, :, b * T:(b + 1) * T].rearrange("(g j w) r k -> g w r j k", g=NG, w=2)
                for w in range(2):
                    sp.dma_start(t.kpad[w * STACK:(w + 1) * STACK, u, w:HG:2, :], ksrc[hg, w]).then_inc(z.group_loaded, 16)

            sp.wait_ge(z.tiles_zeroed, 3)
            for g in range(GROUPS):
                if g >= 2:
                    sp.wait_ge(z.scored, HG * QB * (g - 1))
                if g:
                    sp.wait_ge(z.group_loaded, 48 * g)
                load(g)

        @block.gpsimd
        def _(pool):
            nc.gpsimd.memset(t.kpad[0:STACK, :, 1:HG:2, :], 0.0).then_inc(z.tiles_zeroed, 1)
            pool.wait_ge(z.tiles_zeroed, 1)
            nc.gpsimd.memset(t.kpad[STACK:P, :, 0:HG:2, :], 0.0).then_inc(z.tiles_zeroed, 1)
            pool.wait_ge(z.tiles_zeroed, 2)
            nc.gpsimd.memset(t.vstat[:, :, :, :, :], 0.0).then_inc(z.tiles_zeroed, 1)
            pool.wait_ge(z.tiles_zeroed, 3)

            def steps(g):
                vg = t.vaug[:, bass.ds(((g >> 2) & (B - 1)) * QB, QB), bass.ds((g & (NG - 1)) * HG, HG), :]
                for i in range(QB):
                    n = QB * g + i
                    for u in range(HG):
                        k = HG * n + u
                        if i == 0 and u == 2:
                            after(pool, z.pv_done, n - 1)
                            apart(pool)
                            nc.gpsimd.tensor_copy(t.vstat[:, 0, :, :, 0:HD + 1], vg).then_inc(z.v_early, 1)
                        if i == 2 and u == 2:
                            after(pool, z.pv_done, n - 2)
                            apart(pool)
                            nc.gpsimd.tensor_copy(t.vstat[:, 1, :, :, 0:HD + 1], vg).then_inc(z.v_late, 1)
                        slot = k_slot(i, u)
                        after(pool, z.weighted, k + 1)
                        after(pool, z.exped, k - 7)
                        apart(pool)
                        nc.gpsimd.tensor_scalar(negm[:, slot:slot + 1], rowmax[:, slot:slot + 1], -1.0, None,
                                                ALU.mult).then_inc(z.negmax, 1)

            every_group(pool, steps)

        @block.tensor
        def _(pe):
            def scores(g, i, u):
                n = QB * g + i
                if i == 0 and u == 0:
                    after(pe, z.group_loaded, 48 * (g + 1))
                after(pe, z.weighted, HG * n + u - 1)
                for h in range(2):
                    mm = nc.tensor.matmul(score[u % 2][:, h * SUP:(h + 1) * SUP],
                                          t.qpair[:, g & 1, u // 2, i * P:(i + 1) * P],
                                          t.kpad[:, g & 1, u, h * SUP:(h + 1) * SUP], start=True, stop=True)
                mm.then_inc(z.scored, 1)

            def turn(g, i, u):
                k = HG * (QB * g + i) + u
                after(pe, z.exped, k + 1)
                for turned, bank, copied, k0 in ((z.turnedA, turnA, z.copiedA, 0), (z.turnedB, turnB, z.copiedB, KB)):
                    after(pe, copied, k)
                    for j in range(KB):
                        mm = nc.tensor.transpose(bank[:, j * P:(j + 1) * P], t.weighted[:, u, (k0 + j) * P:(k0 + j + 1) * P],
                                                 m.ident[:, :])
                    mm.then_inc(turned, 1)

            def values(g, i, u):
                n, par = QB * g + i, i % 2
                if u == 0:
                    after(pe, z.copiedA, HG * (n + 1))
                    after(pe, z.copiedB, HG * (n + 1))
                    if i == QB - 1:
                        after(pe, z.v_late, g + 1)
                    elif i == 0:
                        after(pe, z.v_early, g + 1)
                    after(pe, z.raw_saved, n - 1)
                for kb in (2 * u, 2 * u + 1):
                    for h in range(HG):
                        mm = nc.tensor.matmul(pv[par][32 * h:32 * (h + 1), :], t.vstat[:, i // (QB - 1), kb, h, :],
                                              t.probsT[:, par, h, kb, :], start=(kb == 0), stop=(kb == QB - 1))
                if u == HG - 1:
                    mm.then_inc(z.pv_done, 1)

            def steps(g):
                first, last = type(g) is int and g == 0, type(g) is int and g == GROUPS - 1
                for i in range(QB):
                    for u in range(HG):
                        if u < 2:
                            scores(g, i, u + 2)
                        elif i < QB - 1:
                            scores(g, i + 1, u - 2)
                        elif not last:
                            scores(g + 1, 0, u - 2)
                        turn(g, i, u)
                        if i:
                            values(g, i - 1, u)
                        elif not first:
                            values(g - 1, QB - 1, u)

            pe.wait_ge(z.tiles_zeroed, 3)
            scores(0, 0, 0)
            scores(0, 0, 1)
            every_group(pe, steps)
            for u in range(HG):
                values(GROUPS - 1, QB - 1, u)

        @block.vector
        def _(dve):
            def copy_a(g, i, u):
                n, par = QB * g + i, i % 2
                if u == 0:
                    after(dve, z.pv_done, n - 1)
                after(dve, z.turnedA, HG * n + u + 1)
                nc.vector.tensor_copy(t.probsT[:, par, u, 0:KB, :].rearrange("p k q -> p (k q)"), turnA).then_inc(z.copiedA, 1)

            def steps(g):
                for i in range(QB):
                    for u in range(HG):
                        k, slot = HG * (QB * g + i) + u, k_slot(i, u)
                        after(dve, z.turnedB, k - 3)
                        after(dve, z.scored, k + 1)
                        start = (QB - 1 - i) * P
                        apart(dve)
                        nc.vector.tensor_tensor_reduce(t.weighted[:, u, :], score[u % 2][:, :],
                                                       t.decay[:, start:start + T], 1.0, NEG, ALU.mult, ALU.max,
                                                       rowmax[:, slot:slot + 1]).then_inc(z.weighted, 1)
                        if u >= 2:
                            copy_a(g, i, u - 2)
                        elif i:
                            copy_a(g, i - 1, u + 2)
                        elif not (type(g) is int and g == 0):
                            copy_a(g - 1, QB - 1, u + 2)

            every_group(dve, steps)
            copy_a(GROUPS - 1, QB - 1, HG - 2)
            copy_a(GROUPS - 1, QB - 1, HG - 1)

        @block.scalar
        def _(act):
            def copy_b(g, i, u):
                n, par = QB * g + i, i % 2
                if u == 0:
                    after(act, z.pv_done, n - 1)
                after(act, z.turnedB, HG * n + u + 1)
                nc.scalar.activation(t.probsT[:, par, u, KB:QB, :].rearrange("p k q -> p (k q)"), turnB,
                                     ACT.Copy).then_inc(z.copiedB, 1)

            def save(g, i):
                n = QB * g + i
                after(act, z.pv_done, n + 1)
                nc.scalar.activation(t.raw[:, n, :], pv[i % 2], ACT.Copy).then_inc(z.raw_saved, 1)

            def steps(g):
                first = type(g) is int and g == 0
                for i in range(QB):
                    for u in range(HG):
                        k, slot = HG * (QB * g + i) + u, k_slot(i, u)
                        after(act, z.negmax, k + 1)
                        nc.scalar.activation(t.weighted[:, u, :], t.weighted[:, u, :], ACT.Exp,
                                             bias=negm[:, slot:slot + 1]).then_inc(z.exped, 1)
                        unit_before(g, i, u, copy_b)
                        if u == 1:
                            if i >= 2:
                                save(g, i - 2)
                            elif not first:
                                save(g - 1, QB - 2 + i)

            nc.scalar.preload_act_table(ACT.Exp)
            every_group(act, steps)
            copy_b(GROUPS - 1, QB - 1, HG - 1)
            save(GROUPS - 1, QB - 2)
            save(GROUPS - 1, QB - 1)


def k_slot(i, u):
    return (HG * i + u) % 8


def unit_before(g, i, u, do):
    if u:
        do(g, i, u - 1)
    elif i:
        do(g, i - 1, HG - 1)
    elif not (type(g) is int and g == 0):
        do(g - 1, QB - 1, HG - 1)


def after(engine, sem, count):
    if type(count) is not int:
        engine.wait_ge(sem, count)
    elif count > 0:
        engine.wait_ge(sem, count)


def attention_output(m):
    nc, t = m.nc, attention_tiles(m)
    names = ("turned", "rec", "normed", "turned_back", "biased", "wo_summed", "wo_biased", "x_added")
    z = semaphores(m.sem, "ao_", names)
    rec = m.arena[:, 0:2 * NH].rearrange("p (u h) -> p u h", u=2)
    on = m.arena[:, 64:64 + 4 * D].rearrange("p (u c) -> p u c", u=4)
    oC = m.arena[:, 1024:1024 + N]
    yC = m.arena[:, 1024 + N:1024 + N + 2 * SUP].rearrange("p (u c) -> p u c", u=2)
    raw_bank = lambda k: m.bank[0][:, (k % 2) * SUP:(k % 2 + 1) * SUP]
    half = lambda tile, s: tile[:, (s % 2) * SUP:(s % 2 + 1) * SUP]
    with nc.Block() as block:
        @block.tensor
        def _(pe):
            def turn(k):
                if k >= 2:
                    pe.wait_ge(z.normed, k - 1)
                b, i = divmod(k, QB)
                for hg in range(NG):
                    mm = nc.tensor.transpose(raw_bank(k)[:, hg * P:(hg + 1) * P], t.raw[:, (b * NG + hg) * QB + i, :],
                                             m.ident[:, :])
                mm.then_inc(z.turned, 1)

            def back(k):
                s, j = divmod(k, BLKS)
                pe.wait_ge(z.normed, k + 1)
                if j == 0 and s >= 2:
                    pe.wait_ge(z.biased, s - 1)
                mm = nc.tensor.transpose(half(m.bank[1], s)[:, j * P:(j + 1) * P], on[:, k % 4, :], m.ident[:, :])
                mm.then_inc(z.turned_back, 1)
                if j == BLKS - 1:
                    pe.wait_ge(z.biased, s + 1)
                    if s >= 2:
                        pe.wait_ge(z.wo_biased, s - 1)
                    nc.tensor.matmul(half(m.bank[2], s), m.a("wo"), oC[:, s * SUP:(s + 1) * SUP], start=True,
                                     stop=True).then_inc(z.wo_summed, 1)

            turn(0)
            for k in range(NBLK):
                if k + 1 < NBLK:
                    turn(k + 1)
                back(k)

        @block.vector
        def _(dve):
            for k in range(NBLK):
                raw = raw_bank(k).rearrange("p (h c) -> p h c", c=32)
                dve.wait_ge(z.turned, k + 1)
                nc.vector.reciprocal(rec[:, k % 2, :], raw[:, :, HD]).then_inc(z.rec, 1)
                dve.wait_ge(z.rec, k + 1)
                if k >= 4:
                    dve.wait_ge(z.turned_back, k - 3)
                nc.vector.tensor_tensor(on[:, k % 4, :].rearrange("p (h c) -> p h c", c=HD), raw[:, :, 0:HD],
                                        rec[:, k % 2, :].unsqueeze(2).broadcast_to([P, NH, HD]), ALU.mult).then_inc(z.normed, 1)
            for s in range(NSUP):
                xs = m.xC[:, s * SUP:(s + 1) * SUP]
                dve.wait_ge(z.wo_biased, s + 1)
                nc.vector.scalar_tensor_tensor(out=xs, in0=yC[:, s % 2, :], scalar=m.gated(0, 2, s), in1=xs,
                                               op0=ALU.mult, op1=ALU.add).then_inc(z.x_added, 1)

        @block.scalar
        def _(act):
            for s in range(NSUP):
                act.wait_ge(z.turned_back, BLKS * (s + 1))
                nc.scalar.activation(oC[:, s * SUP:(s + 1) * SUP], half(m.bank[1], s), ACT.Identity,
                                     bias=m.a("bv")).then_inc(z.biased, 1)
                act.wait_ge(z.wo_summed, s + 1)
                if s >= 2:
                    act.wait_ge(z.x_added, s - 1)
                nc.scalar.activation(yC[:, s % 2, :], half(m.bank[2], s), ACT.Identity,
                                     bias=m.a("bo")).then_inc(z.wo_biased, 1)



def top_two(m, step, score, tmp):
    nc = m.nc
    above = tmp[:, 0:NBLK * E * E].rearrange("p (k e f) -> p k e f", k=NBLK, e=E)
    equal = tmp[:, NBLK * E * E:2 * NBLK * E * E].rearrange("p (k e f) -> p k e f", k=NBLK, e=E)
    flat = lambda v: v.rearrange("p k e f -> p (k e) f")
    rank = tmp[:, 2 * NBLK * E * E:2 * NBLK * E * E + NBLK * E]
    shape = [P, NBLK, E, E]
    mine, other = score.unsqueeze(3).broadcast_to(shape), score.unsqueeze(2).broadcast_to(shape)
    tri = m.tri[:, :].rearrange("p (e f) -> p e f", f=E).unsqueeze(1).broadcast_to(shape)
    step(nc.vector.tensor_tensor(equal, other, mine, ALU.is_equal))
    step(nc.vector.tensor_tensor(equal, equal, tri, ALU.mult))
    step(nc.vector.tensor_tensor(above, other, mine, ALU.is_gt))
    step(nc.vector.tensor_tensor(above, above, equal, ALU.add))
    step(nc.vector.tensor_reduce(rank, flat(above), AX.X, ALU.add))
    step(nc.vector.tensor_scalar(rank, rank, 2.0, None, ALU.is_lt))
    return rank.rearrange("p (k e) -> p k e", e=E)


def split_weights(m, step, rw, rw3, low):
    nc = m.nc
    step(nc.vector.tensor_copy(low, rw))
    step(nc.vector.tensor_copy(rw3[:, :, 0, :], low))
    step(nc.vector.tensor_tensor(rw3[:, :, 2, :], rw, rw3[:, :, 0, :], ALU.subtract))
    step(nc.vector.tensor_copy(low, rw3[:, :, 2, :]))
    step(nc.vector.tensor_copy(rw3[:, :, 1, :], low))
    nc.vector.tensor_tensor(rw3[:, :, 2, :], rw3[:, :, 2, :], rw3[:, :, 1, :], ALU.subtract).then_inc(m.gt.split, 1)


def turn_weights(m, pe, rw3, call):
    pe.wait_ge(m.gt.split, call + 1)
    for s in range(NSUP):
        for j in range(BLKS):
            mm = m.nc.tensor.transpose(m.bank[s][0:NPART * E, j * P:(j + 1) * P],
                                       rw3[:, s * BLKS + j].rearrange("p a e -> p (a e)"), m.ident[:, :])
        mm.then_inc(m.gt.splitT, 1)


def copy_weights(m, act, call, also=None):
    for s in range(NSUP):
        act.wait_ge(m.gt.splitT, call * NSUP + s + 1)
        m.nc.scalar.activation(m.rwT[:, s * SUP:(s + 1) * SUP], m.bank[s][0:NPART * E, 0:SUP], ACT.Copy)
        if also is not None:
            m.nc.scalar.activation(also[:, s * SUP:(s + 1) * SUP], m.bank[s][0:NPART * E, 0:SUP], ACT.Copy)


def similarity_gating(m, nC, sim, gates, tmp):
    nc, g = m.nc, m.gt
    call = m.gt_calls
    m.gt_calls += 1
    at = 0

    def take(width):
        nonlocal at
        at += width
        return tmp[:, at - width:at]

    sq = take(N)
    simsq, simn, simstd = take(E), take(E), take(E)
    KE = NBLK * E
    std, lg, gated, mask, top, rw = take(NBLK), take(KE), take(KE), take(KE), take(KE), take(KE)
    mx, put = take(NBLK), take(NBLK)
    rw3 = take(NPART * KE).rearrange("p (k a e) -> p k a e", k=NBLK, a=NPART)
    low = take(KE // 2).bitcast(BF16).rearrange("p (k e) -> p k e", e=E)
    rank_tmp = take(2 * NBLK * E * E + KE)
    ke = lambda v: v.rearrange("p (k e) -> p k e", e=E)
    over = lambda v: v.unsqueeze(2).broadcast_to([P, NBLK, E])
    raw = m.bank[0][:, 0:KE]
    ss = m.bank[1][:, 0:NBLK]
    simss = m.bank[2][:, 0:E]
    with nc.Block() as block:
        @block.scalar
        def _(act):
            nc.scalar.activation(sq, nC, ACT.Square).then_inc(g.sq, 1)
            act.wait_ge(g.simsq, 2 * call + 2)
            nc.scalar.activation(simstd, simss, ACT.Sqrt).then_inc(g.simstd, 1)
            act.wait_ge(g.norms, call + 1)
            nc.scalar.activation(std, ss, ACT.Sqrt).then_inc(g.act_out, 1)
            act.wait_ge(g.act_in, call + 1)
            nc.scalar.activation(rw, lg, ACT.Exp).then_inc(g.act_out, 1)
            copy_weights(m, act, call)

        @block.tensor
        def _(pe):
            pe.wait_ge(g.simsq, 2 * call + 1)
            nc.tensor.matmul(simss, m.ones[:, :], simsq, start=True, stop=True).then_inc(g.simsq, 1)
            pe.wait_ge(g.sq, call + 1)
            for k in range(NBLK):
                mm = nc.tensor.matmul(ss[:, k:k + 1], sq[:, k * P:(k + 1) * P], m.ones[:, 0:1], start=True, stop=True)
            mm.then_inc(g.norms, 1)
            pe.wait_ge(g.sim, call + 1)
            for k in range(NBLK):
                mm = nc.tensor.matmul(raw[:, k * E:(k + 1) * E], nC[:, k * P:(k + 1) * P], simn, start=True, stop=True)
            mm.then_inc(g.logits, 1)
            turn_weights(m, pe, rw3, call)

        @block.vector
        def _(dve):
            step = m.dve.on(dve)
            nc.vector.tensor_tensor(simsq, sim, sim, ALU.mult).then_inc(g.simsq, 1)
            dve.wait_ge(g.simstd, call + 1)
            step(nc.vector.tensor_scalar(simstd, simstd, 1e-12, None, ALU.max))
            step(nc.vector.reciprocal(simstd, simstd))
            nc.vector.tensor_tensor(simn, sim, simstd, ALU.mult).then_inc(g.sim, 1)
            dve.wait_ge(g.act_out, 2 * call + 1)
            step(nc.vector.tensor_scalar(std, std, 1e-12, None, ALU.max))
            step(nc.vector.reciprocal(std, std))
            dve.wait_ge(g.logits, call + 1)
            step(nc.vector.tensor_tensor(ke(lg), ke(raw), over(std), ALU.mult))
            step(nc.vector.tensor_tensor(ke(lg), ke(lg), gates.unsqueeze(1).broadcast_to([P, NBLK, E]), ALU.subtract))
            step(nc.vector.tensor_scalar(gated, lg, 0.0, None, ALU.max))
            step(nc.vector.tensor_scalar(mask, lg, 0.0, None, ALU.is_gt))
            step(nc.vector.tensor_reduce(mx, ke(lg), AX.X, ALU.max))
            step(nc.vector.tensor_scalar(put, mx, 0.0, None, ALU.is_le))
            chosen = top_two(m, step, ke(lg), rank_tmp)
            step(nc.vector.tensor_tensor(ke(top), chosen, over(put), ALU.mult))
            step(nc.vector.tensor_tensor(mask, mask, top, ALU.max))
            step(nc.vector.tensor_scalar(mx, mx, 0.0, None, ALU.max))
            nc.vector.tensor_tensor(ke(lg), ke(gated), over(mx), ALU.subtract).then_inc(g.act_in, 1)
            dve.wait_ge(g.act_out, 2 * call + 2)
            step(nc.vector.tensor_tensor(rw, rw, mask, ALU.mult))
            step(nc.vector.tensor_reduce(mx, ke(rw), AX.X, ALU.add))
            step(nc.vector.reciprocal(mx, mx))
            step(nc.vector.tensor_tensor(ke(rw), ke(rw), over(mx), ALU.mult))
            split_weights(m, step, ke(rw), rw3, low)



def feed_forward(m):
    ar = m.arena
    at = 0

    def take(width):
        nonlocal at
        at += width
        return ar[:, at - width:at]

    m.nC, m.hC, m.qT, m.kT, m.vS, m.aC = (take(N) for _ in range(6))
    tmp = ar[:, at:ar.shape[1]]
    sup = lambda tile: (lambda s: tile[:, s * SUP:(s + 1) * SUP])
    layer_norm(m, m.xC, sup(m.hC), lambda s: m.scale1(0, 4, s), lambda s: m.shift(0, 3, s), tmp=at)
    load_layer1(m)
    layer_norm(m, m.hC, sup(m.nC), lambda s: m.a("ln1w"), lambda s: m.a("ln1b"), tmp=at)
    similarity_gating(m, m.nC, m.a("smha_sim"), m.rowg[:, 0:E], tmp)
    routed_projections(m, tmp)
    causal_attention(m, tmp)
    routed_output(m, tmp)
    layer_norm(m, m.hC, sup(m.nC), lambda s: m.a("ln2w"), lambda s: m.a("ln2b"), tmp=at)
    similarity_gating(m, m.nC, m.a("moe_sim"), m.rowg[:, E:2 * E], tmp)
    routed_mlp(m, tmp)


def load_layer1(m):
    with m.nc.Block() as block:
        @block.sync
        def _(sp):
            sp.dma_start(m.late[:, :], m.l1_in).then_inc(m.l1_loaded, 16)
            sp.wait_ge(m.ffn_loaded, 16)


def spread(m, out, e, s):
    return m.nc.tensor.matmul(out, m.sel_e[:, e, :], m.rwT[:, bass.ds(s * SUP, SUP)], start=True, stop=True)


def routed_projections(m, tmp):
    nc = m.nc
    names = ("spread", "scaled", "used", "q_done", "k_done", "v_done", "q_free", "k_free", "v_free")
    z = semaphores(m.sem, "rp_", names)
    XB = 4
    xe = tmp[:, 0:XB * SUP].rearrange("p (u c) -> p u c", u=XB)
    wB = [m.bank[0][:, 0:SUP], m.bank[0][:, SUP:2 * SUP]]
    acc = lambda i, par: m.bank[1 + i][:, par * SUP:(par + 1) * SUP]
    PAIRS = NSUP // 2
    with nc.Block() as block:
        @block.tensor
        def _(pe):
            prime(pe, z.used)
            with pe.Fori(0, PAIRS) as p2:
                for par in range(2):
                    s = 2 * p2 + par
                    pe.wait_ge(z.scaled, PRIMED + E * s)
                    apart(pe)
                    spread(m, wB[0], 0, s).then_inc(z.spread, 1)
                    for e in range(E):
                        if e + 1 < E:
                            if e >= 1:
                                pe.wait_ge(z.scaled, PRIMED + E * s + e)
                                apart(pe)
                            spread(m, wB[(e + 1) % 2], e + 1, s).then_inc(z.spread, 1)
                        x = xe[:, e % XB, :]
                        pe.wait_ge(z.scaled, PRIMED + E * s + e + 1)
                        if e == 0:
                            pe.wait_ge(z.q_free, PRIMED + 2 * p2)
                            pe.wait_ge(z.k_free, PRIMED + 2 * p2)
                            pe.wait_ge(z.v_free, PRIMED + 2 * p2)
                        ws = slice(e * D, (e + 1) * D)
                        q = nc.tensor.matmul(acc(0, par), m.f("qp")[:, ws], x, start=(e == 0), stop=(e == E - 1))
                        k = nc.tensor.matmul(acc(1, par), m.f("kp")[:, ws], x, start=(e == 0), stop=(e == E - 1))
                        for j in range(BLKS):
                            v = nc.tensor.matmul(acc(2, par)[:, j * P:(j + 1) * P], x[:, j * P:(j + 1) * P],
                                                 m.f("vp")[:, ws], start=(e == 0 and j == 0), stop=(e == E - 1),
                                                 skip_group_check=True)
                        v.then_inc(z.used, 1)
                        if e == E - 1:
                            q.then_inc(z.q_done, 1)
                            k.then_inc(z.k_done, 1)

        @block.vector
        def _(dve):
            prime(dve, z.scaled, z.v_free)
            with dve.Fori(0, PAIRS) as p2:
                for par in range(2):
                    s = 2 * p2 + par
                    for e in range(E):
                        if e >= XB:
                            dve.wait_ge(z.used, PRIMED + E * s + e - XB + 1)
                        else:
                            dve.wait_ge(z.used, PRIMED + E * s)
                        dve.wait_ge(z.spread, E * s + e + 1)
                        apart(dve)
                        nc.vector.tensor_tensor(xe[:, e % XB, :], m.nC[:, bass.ds(s * SUP, SUP)], wB[e % 2],
                                                ALU.mult).then_inc(z.scaled, 1)
                    dve.wait_ge(z.used, PRIMED + E * (s + 1))
                    apart(dve)
                    nc.vector.tensor_copy(m.vS[:, bass.ds(s * SUP, SUP)], acc(2, par)).then_inc(z.v_free, 1)

        @block.scalar
        def _(act):
            prime(act, z.q_free, z.k_free)
            with act.Fori(0, PAIRS) as p2:
                for par in range(2):
                    s = 2 * p2 + par
                    act.wait_ge(z.q_done, s + 1)
                    apart(act)
                    nc.scalar.activation(m.qT[:, bass.ds(s * SUP, SUP)], acc(0, par), ACT.Copy).then_inc(z.q_free, 1)
                    act.wait_ge(z.k_done, s + 1)
                    apart(act)
                    nc.scalar.activation(m.kT[:, bass.ds(s * SUP, SUP)], acc(1, par), ACT.Copy).then_inc(z.k_free, 1)


def causal_attention(m, tmp):
    nc = m.nc
    names = ("scored", "maxed", "negmax", "exped", "normed", "turned", "copied", "summed", "saved", "masked")
    z = semaphores(m.sem, "ca_", names)
    p = tmp[:, 0:2 * T].rearrange("p (u k) -> p u k", u=2)
    pT = tmp[:, 2 * T:4 * T].rearrange("p (u k) -> p u k", u=2)
    col = tmp[:, 4 * T:4 * T + 8]
    mx, nm, l, rl = (col[:, 2 * i:2 * i + 2] for i in range(4))
    scale = float(D) ** -0.5
    score = lambda n: m.bank[n % 2]
    turn = m.bank[2]
    out = lambda n: m.bank[3][:, (n % 2) * SUP:(n % 2) * SUP + P]
    halves_of = lambda w: [(a, min(a + SUP, w)) for a in range(0, w, SUP)]
    copies = [0]
    for n in range(NBLK):
        copies.append(copies[-1] + len(halves_of((n % QB + 1) * P)))
    with nc.Block() as block:
        @block.tensor
        def _(pe):
            def scores(n):
                b, i = divmod(n, QB)
                if n >= 2:
                    pe.wait_ge(z.exped, n - 1)
                for a, c in halves_of((i + 1) * P):
                    mm = nc.tensor.matmul(score(n)[:, a:c], m.qT[:, n * P:(n + 1) * P], m.kT[:, b * T + a:b * T + c],
                                          start=True, stop=True)
                mm.then_inc(z.scored, 1)

            def turns(n):
                b, i = divmod(n, QB)
                pe.wait_ge(z.normed, n + 1)
                for h, (a, c) in enumerate(halves_of((i + 1) * P)):
                    if n:
                        last = copies[n] if h == 0 or copies[n] - copies[n - 1] == 2 else copies[n]
                        pe.wait_ge(z.copied, last)
                    for k in range(a, c, P):
                        mm = nc.tensor.transpose(turn[:, k:k + P], p[:, n % 2, k:k + P], m.ident[:, :])
                    mm.then_inc(z.turned, 1)

            def values(n):
                b, i = divmod(n, QB)
                pe.wait_ge(z.copied, copies[n + 1])
                if n >= 2:
                    pe.wait_ge(z.saved, n - 1)
                for kb in range(i + 1):
                    mm = nc.tensor.matmul(out(n), m.vS[:, (b * QB + kb) * P:(b * QB + kb + 1) * P],
                                          pT[:, n % 2, kb * P:(kb + 1) * P], start=(kb == 0), stop=(kb == i))
                mm.then_inc(z.summed, 1)

            scores(0)
            for n in range(NBLK):
                if n + 1 < NBLK:
                    scores(n + 1)
                turns(n)
                if n:
                    values(n - 1)
            values(NBLK - 1)

        @block.vector
        def _(dve):
            def top(n):
                i = n % QB
                w = (i + 1) * P
                dve.wait_ge(z.scored, n + 1)
                nc.vector.tensor_tensor(score(n)[:, i * P:w], score(n)[:, i * P:w], m.causal[:, :],
                                        ALU.add).then_inc(z.masked, 1)
                dve.wait_ge(z.masked, n + 1)
                nc.vector.tensor_reduce(mx[:, n % 2:n % 2 + 1], score(n)[:, 0:w], AX.X, ALU.max).then_inc(z.maxed, 1)
                dve.wait_ge(z.maxed, n + 1)
                nc.vector.tensor_scalar(nm[:, n % 2:n % 2 + 1], mx[:, n % 2:n % 2 + 1], -scale, None,
                                        ALU.mult).then_inc(z.negmax, 1)

            step = m.dve.on(dve)
            top(0)
            for n in range(NBLK):
                w = (n % QB + 1) * P
                if n + 1 < NBLK:
                    top(n + 1)
                dve.wait_ge(z.exped, n + 1)
                step(nc.vector.reciprocal(rl[:, n % 2:n % 2 + 1], l[:, n % 2:n % 2 + 1]))
                nc.vector.tensor_scalar(p[:, n % 2, 0:w], p[:, n % 2, 0:w], rl[:, n % 2:n % 2 + 1], None,
                                        ALU.mult).then_inc(z.normed, 1)

        @block.scalar
        def _(act):
            def exps(n):
                w = (n % QB + 1) * P
                act.wait_ge(z.negmax, n + 1)
                if n >= 2:
                    act.wait_ge(z.turned, copies[n - 1])
                nc.scalar.activation(p[:, n % 2, 0:w], score(n)[:, 0:w], ACT.Exp, bias=nm[:, n % 2:n % 2 + 1],
                                     scale=scale, accum_out=l[:, n % 2:n % 2 + 1]).then_inc(z.exped, 1)

            def copy(n):
                if n >= 2:
                    act.wait_ge(z.summed, n - 1)
                for h, (a, c) in enumerate(halves_of((n % QB + 1) * P)):
                    act.wait_ge(z.turned, copies[n] + h + 1)
                    nc.scalar.activation(pT[:, n % 2, a:c], turn[:, a:c], ACT.Copy).then_inc(z.copied, 1)

            def save(n):
                act.wait_ge(z.summed, n + 1)
                nc.scalar.activation(m.aC[:, n * P:(n + 1) * P], out(n), ACT.Copy).then_inc(z.saved, 1)

            exps(0)
            for n in range(NBLK):
                if n + 1 < NBLK:
                    exps(n + 1)
                copy(n)
                if n:
                    save(n - 1)
            save(NBLK - 1)


def routed_output(m, tmp):
    nc = m.nc
    names = ("spread", "scaled", "used", "added")
    z = semaphores(m.sem, "ro_", names)
    XB = 4
    xe = tmp[:, 0:XB * SUP].rearrange("p (u c) -> p u c", u=XB)
    wB = [m.bank[0][:, 0:SUP], m.bank[0][:, SUP:2 * SUP]]
    acc = lambda par: m.bank[1][:, par * SUP:(par + 1) * SUP]
    PAIRS = NSUP // 2
    with nc.Block() as block:
        @block.tensor
        def _(pe):
            prime(pe, z.used)
            with pe.Fori(0, PAIRS) as p2:
                for par in range(2):
                    s = 2 * p2 + par
                    pe.wait_ge(z.scaled, PRIMED + E * s)
                    apart(pe)
                    spread(m, wB[0], 0, s).then_inc(z.spread, 1)
                    for e in range(E):
                        if e + 1 < E:
                            if e >= 1:
                                pe.wait_ge(z.scaled, PRIMED + E * s + e)
                                apart(pe)
                            spread(m, wB[(e + 1) % 2], e + 1, s).then_inc(z.spread, 1)
                        pe.wait_ge(z.scaled, PRIMED + E * s + e + 1)
                        if e == 0:
                            pe.wait_ge(z.added, PRIMED + 2 * p2)
                        nc.tensor.matmul(acc(par), m.f("op")[:, e * D:(e + 1) * D], xe[:, e % XB, :], start=(e == 0),
                                         stop=(e == E - 1)).then_inc(z.used, 1)

        @block.vector
        def _(dve):
            prime(dve, z.scaled, z.added)
            with dve.Fori(0, PAIRS) as p2:
                for par in range(2):
                    s = 2 * p2 + par
                    for e in range(E):
                        dve.wait_ge(z.used, PRIMED + E * s + max(0, e - XB + 1))
                        dve.wait_ge(z.spread, E * s + e + 1)
                        apart(dve)
                        nc.vector.tensor_tensor(xe[:, e % XB, :], m.aC[:, bass.ds(s * SUP, SUP)], wB[e % 2],
                                                ALU.mult).then_inc(z.scaled, 1)
                    dve.wait_ge(z.used, PRIMED + E * (s + 1))
                    apart(dve)
                    h = m.hC[:, bass.ds(s * SUP, SUP)]
                    nc.vector.tensor_tensor(h, h, acc(par), ALU.add).then_inc(z.added, 1)


def routed_mlp(m, tmp):
    nc = m.nc
    names = ("up", "gelu", "spread", "scaled", "used", "summed", "added")
    z = semaphores(m.sem, "rm_", names)
    XB = 4
    ge = tmp[:, 0:XB * SUP].rearrange("p (u c) -> p u c", u=XB)
    ie = tmp[:, XB * SUP:2 * XB * SUP].rearrange("p (u c) -> p u c", u=XB)
    yh = tmp[:, 2 * XB * SUP:2 * XB * SUP + 2 * SUP].rearrange("p (u c) -> p u c", u=2)
    wB = [m.bank[0][:, 0:SUP], m.bank[0][:, SUP:2 * SUP]]
    up = [m.bank[2][:, 0:SUP], m.bank[2][:, SUP:2 * SUP]]
    acc = lambda par: m.bank[1][:, par * SUP:(par + 1) * SUP]
    PAIRS = NSUP // 2
    with nc.Block() as block:
        @block.tensor
        def _(pe):
            prime(pe, z.used)
            with pe.Fori(0, PAIRS) as p2:
                for par in range(2):
                    s = 2 * p2 + par

                    def rise(e):
                        pe.wait_ge(z.scaled, PRIMED + E * s + max(0, e - 1))
                        pe.wait_ge(z.gelu, PRIMED + E * s + max(0, e - 1))
                        apart(pe)
                        spread(m, wB[e % 2], e, s).then_inc(z.spread, 1)
                        nc.tensor.matmul(up[e % 2], m.f("w1")[:, e * D:(e + 1) * D], m.nC[:, bass.ds(s * SUP, SUP)],
                                         start=True, stop=True).then_inc(z.up, 1)

                    rise(0)
                    rise(1)
                    for e in range(E):
                        pe.wait_ge(z.scaled, PRIMED + E * s + e + 1)
                        if e == 0:
                            pe.wait_ge(z.added, PRIMED + 2 * p2)
                        nc.tensor.matmul(acc(par), m.f("w2")[:, e * D:(e + 1) * D], ie[:, e % XB, :], start=(e == 0),
                                         stop=(e == E - 1)).then_inc(z.used, 1)
                        if e + 2 < E:
                            rise(e + 2)

        @block.scalar
        def _(act):
            prime(act, z.gelu)
            nc.scalar.preload_act_table(ACT.Gelu)
            with act.Fori(0, PAIRS) as p2:
                for par in range(2):
                    s = 2 * p2 + par
                    for e in range(E):
                        act.wait_ge(z.scaled, PRIMED + E * s + max(0, e - XB + 1))
                        act.wait_ge(z.up, E * s + e + 1)
                        nc.scalar.activation(ge[:, e % XB, :], up[e % 2], ACT.Gelu).then_inc(z.gelu, 1)

        @block.vector
        def _(dve):
            prime(dve, z.scaled, z.added)
            with dve.Fori(0, PAIRS) as p2:
                for par in range(2):
                    s = 2 * p2 + par
                    for e in range(E):
                        dve.wait_ge(z.used, PRIMED + E * s + max(0, e - XB + 1))
                        dve.wait_ge(z.spread, E * s + e + 1)
                        dve.wait_ge(z.gelu, PRIMED + E * s + e + 1)
                        nc.vector.tensor_tensor(ie[:, e % XB, :], ge[:, e % XB, :], wB[e % 2],
                                                ALU.mult).then_inc(z.scaled, 1)
                    dve.wait_ge(z.used, PRIMED + E * (s + 1))
                    apart(dve)
                    nc.vector.tensor_tensor(yh[:, par, :], acc(par), m.hC[:, bass.ds(s * SUP, SUP)],
                                            ALU.add).then_inc(z.summed, 1)
                    dve.wait_ge(z.summed, s + 1)
                    apart(dve)
                    x = m.xC[:, bass.ds(s * SUP, SUP)]
                    nc.vector.scalar_tensor_tensor(out=x, in0=yh[:, par, :], scalar=m.gate[:, bass.ds(5 * B + p2, 1)], in1=x,
                                                   op0=ALU.mult, op1=ALU.add).then_inc(z.added, 1)



def mixer(m):
    nc, ar, fr = m.nc, m.arena, m.ffn
    PAD = 4
    W = PAD + T
    at = 0

    def take(width):
        nonlocal at
        at += width
        return ar[:, at - width:at]

    halves = lambda v: v.rearrange("p (h t) -> p h t", h=HALVES)
    t = Shared()
    t.W, t.PAD = W, PAD
    t.hP = take(B * W).rearrange("p (b t) -> p b t", b=B)
    t.xs, t.sz, t.dt, t.u = (halves(take(HALVES * N)) for _ in range(4))
    t.dA = take(HALVES * T).rearrange("p (h t) -> p h t", h=HALVES)
    t.g = take(2 * HALVES * T).rearrange("p (u h t) -> p u h t", u=2, h=HALVES)
    t.scratch = ar[:, at - 6 * T:at]
    t.A, t.wrep, t.diag = take(HALVES * DS), take(HALVES * P), take(HALVES * P)
    assert at <= ar.shape[1], at
    t.sel = fr[0:NPART * 2 * DS, 0:2 * DS * P // 2].bitcast(BF16).rearrange("p (n c) -> p n c", n=2 * DS)
    t.stack = fr[0:NPART * 2 * DS, 2048:2048 + N // 2].bitcast(BF16)
    t.Cs = fr[:, 3072:3072 + 2 * T].rearrange("p (u t) -> p u t", u=2)
    t.wtap = t.scratch[:, 0:KC * DI].rearrange("p (k d) -> p k d", k=KC)
    t.tmp = 2 * N

    mixer_constants(m, t)
    layer_norm(m, m.xC, lambda s: t.hP[:, s // SUPB, PAD + (s % SUPB) * SUP:PAD + (s % SUPB + 1) * SUP],
               lambda s: m.scale1(1, 1, s), lambda s: m.shift(1, 0, s), tmp=t.tmp + 4096)
    mixer_input(m, t)
    mixer_steps(m, t)
    selective_scan(m, t)
    mixer_output(m, t)


def mixer_constants(m, t):
    nc = m.nc
    exped = m.sem("a_exped")
    with nc.Block() as block:
        @block.gpsimd
        def _(pool):
            step = m.pool.on(pool)
            nc.gpsimd.memset(t.hP[:, :, 0:t.PAD], 0.0)
            step(nc.gpsimd.memset(t.sel, 0.0))
            for part in range(NPART):
                step(nc.gpsimd.affine_select(out=t.sel, in_=t.sel, compare_op=ALU.not_equal, fill=1.0,
                                             base=-part * 2 * DS, pattern=[[-1, 2 * DS], [0, P]], channel_multiplier=1))

        @block.scalar
        def _(act):
            act.wait_ge(m.l1_loaded, 16)
            nc.scalar.activation(t.A, m.l("a_log"), ACT.Exp).then_inc(exped, 1)

        @block.vector
        def _(dve):
            dve.wait_ge(m.l1_loaded, 16)
            for k in range(KC):
                nc.vector.tensor_tensor(t.wtap[:, k, :], m.l("w_in")[:, 0:DI], m.r("w_conv")[:, k * DI:(k + 1) * DI],
                                        ALU.mult)
            for h in range(HALVES):
                nc.vector.tensor_copy(t.wrep[:, h * P:(h + 1) * P],
                                      m.l("w_x")[:, h * (2 * DS + 1):h * (2 * DS + 1) + 1].broadcast_to([P, P]))
                nc.vector.tensor_scalar(t.diag[:, h * P:(h + 1) * P], m.ident[:, :], m.l("dskip")[:, h:h + 1], None,
                                        ALU.mult)
            dve.wait_ge(exped, 1)
            nc.vector.tensor_scalar(t.A, t.A, -1.0, None, ALU.mult)


def mixer_input(m, t):
    nc = m.nc
    z = semaphores(m.sem, "mi_", ("x_done", "z_done", "freed"))
    ps = lambda i, par: m.bank[i][:, par * SUP:(par + 1) * SUP]
    with nc.Block() as block:
        @block.tensor
        def _(pe):
            with pe.Fori(0, B) as b:
                for par in range(SUPB):
                    pe.wait_ge(z.freed, PRIMED + 4 * b)
                    pe.wait_ge(z.freed, PRIMED + 8 * b)
                    for h in range(HALVES):
                        for k in range(KC):
                            at = t.PAD - (KC - 1) + k + par * SUP
                            mm = nc.tensor.matmul(ps(h, par), t.wtap[:, k, h * P:(h + 1) * P], t.hP[:, b, at:at + SUP],
                                                  start=(k == 0), stop=(k == KC - 1))
                        mm.then_inc(z.x_done, 1)
                    for h in range(HALVES):
                        at = t.PAD + par * SUP
                        nc.tensor.matmul(ps(2 + h, par), m.l("w_in")[:, DI + h * P:DI + (h + 1) * P], t.hP[:, b, at:at + SUP],
                                         start=True, stop=True).then_inc(z.z_done, 1)

        @block.scalar
        def _(act):
            prime(act, z.freed)
            nc.scalar.preload_act_table(ACT.Silu)
            with act.Fori(0, B) as b:
                for par in range(SUPB):
                    s = b * SUPB + par
                    for h in range(HALVES):
                        act.wait_ge(z.x_done, HALVES * s + h + 1)
                        apart(act)
                        nc.scalar.activation(t.xs[:, h, bass.ds(s * SUP, SUP)], ps(h, par), ACT.Silu,
                                             bias=m.l("b_conv")[:, h:h + 1]).then_inc(z.freed, 1)
                    for h in range(HALVES):
                        act.wait_ge(z.z_done, HALVES * s + h + 1)
                        apart(act)
                        nc.scalar.activation(t.sz[:, h, bass.ds(s * SUP, SUP)], ps(2 + h, par),
                                             ACT.Silu).then_inc(z.freed, 1)


def mixer_steps(m, t):
    nc = m.nc
    names = ("dt_raw", "affine", "abs", "logged", "bc_done", "first", "rest", "second", "third", "dt_free")
    z = semaphores(m.sem, "ms_", names)
    ps = lambda i, par: m.bank[i][:, par * SUP:(par + 1) * SUP]
    v = t.scratch[:, 0:HALVES * SUP * 2].rearrange("p (u h c) -> p u h c", u=2, h=HALVES)
    low = t.scratch[0:2 * DS, 2048:2048 + 2048]
    rest, part2, part3 = low[:, 0:SUP], low[:, SUP:SUP + SUP // 2].bitcast(BF16), low[:, 2 * SUP:2 * SUP + SUP // 2].bitcast(BF16)
    R = 2 * DS
    sup = lambda tile, s: tile[:, s * SUP:(s + 1) * SUP]
    with nc.Block() as block:
        @block.tensor
        def _(pe):
            for s in range(NSUP):
                par = s % 2
                if s >= 2:
                    pe.wait_ge(z.affine, s - 1)
                    pe.wait_ge(z.rest, s - 1)
                for h in range(HALVES):
                    mm = nc.tensor.matmul(ps(0, par), t.wrep[:, h * P:(h + 1) * P], sup(t.xs[:, h], s), start=(h == 0),
                                          stop=(h == HALVES - 1))
                mm.then_inc(z.dt_raw, 1)
                for h in range(HALVES):
                    c = h * (R + 1) + 1
                    mm = nc.tensor.matmul(ps(1, par)[0:R, :], m.l("w_x")[:, c:c + R], sup(t.xs[:, h], s), start=(h == 0),
                                          stop=(h == HALVES - 1))
                mm.then_inc(z.bc_done, 1)

        @block.vector
        def _(dve):
            for s in range(NSUP):
                par = s % 2
                dve.wait_ge(z.dt_raw, s + 1)
                for h in range(HALVES):
                    ins = nc.vector.tensor_scalar(sup(t.dt[:, h], s), ps(0, par), m.l("w_dt")[:, h:h + 1],
                                                  m.l("b_dt")[:, h:h + 1], ALU.mult, ALU.add)
                ins.then_inc(z.affine, 1)
                dve.wait_ge(z.bc_done, s + 1)
                if s:
                    dve.wait_ge(z.third, 2 * s)
                nc.vector.tensor_copy(sup(t.stack[0:R], s), ps(1, par)[0:R, :]).then_inc(z.first, 1)
                dve.wait_ge(z.first, s + 1)
                nc.vector.tensor_tensor(rest, ps(1, par)[0:R, :], sup(t.stack[0:R], s), ALU.subtract).then_inc(z.rest, 1)
                dve.wait_ge(z.rest, s + 1)
                nc.vector.tensor_copy(part2, rest).then_inc(z.second, 1)
                dve.wait_ge(z.second, 2 * s + 1)
                nc.vector.tensor_tensor(part3, rest, part2, ALU.subtract).then_inc(z.second, 1)
                dve.wait_ge(z.logged, s + 1)
                d = t.dt[:, :, s * SUP:(s + 1) * SUP]
                nc.vector.scalar_tensor_tensor(out=d, in0=d, scalar=0.0, in1=v[:, par], op0=ALU.max,
                                               op1=ALU.add).then_inc(z.dt_free, 1)
                dve.wait_ge(z.dt_free, s + 1)
                nc.vector.tensor_tensor(t.u[:, :, s * SUP:(s + 1) * SUP], d, t.xs[:, :, s * SUP:(s + 1) * SUP], ALU.mult)

        @block.scalar
        def _(act):
            nc.scalar.preload_act_table_set("natural_log_exp_and_others")
            for s in range(NSUP):
                par = s % 2
                d = t.dt[:, :, s * SUP:(s + 1) * SUP]
                step = m.act.on(act)
                act.wait_ge(z.affine, s + 1)
                if s >= 2:
                    act.wait_ge(z.dt_free, s - 1)
                step(nc.scalar.activation(v[:, par], d, ACT.Abs))
                step(nc.scalar.activation(v[:, par], v[:, par], ACT.Exp, scale=-1.0))
                nc.scalar.activation(v[:, par], v[:, par], ACT.Ln, bias=m.ones[:, 0:1]).then_inc(z.logged, 1)
                act.wait_ge(z.second, 2 * s + 2)
                nc.scalar.activation(sup(t.stack[R:2 * R], s), part2, ACT.Copy).then_inc(z.third, 1)
                nc.scalar.activation(sup(t.stack[2 * R:3 * R], s), part3, ACT.Copy).then_inc(z.third, 1)


def selective_scan(m, t):
    nc = m.nc
    names = ("b_spread", "c_spread", "b_used", "c_saved", "decayed", "scanned", "weighted", "y_added", "driven",
             "y_gated")
    z = semaphores(m.sem, "ss_", names)
    psB, psC = m.bank[0], m.bank[1]
    y = [m.bank[2], m.bank[3]]
    PAIRS = DS // 2
    halves_of = [(h, h * SUP, (h + 1) * SUP) for h in range(SUPB)]
    with nc.Block() as block:
        @block.tensor
        def _(pe):
            for b in range(B):
                def spread_bc(n):
                    k = b * DS + n
                    pe.wait_ge(z.b_used, 2 * k)
                    apart(pe)
                    for _, a, c in halves_of:
                        mm = nc.tensor.matmul(psB[:, a:c], t.sel[:, n, :], t.stack[:, b * T + a:b * T + c], start=True, stop=True)
                    mm.then_inc(z.b_spread, 1)
                    pe.wait_ge(z.c_saved, k)
                    apart(pe)
                    for _, a, c in halves_of:
                        mm = nc.tensor.matmul(psC[:, a:c], t.sel[:, n + DS, :], t.stack[:, b * T + a:b * T + c], start=True,
                                              stop=True)
                    mm.then_inc(z.c_spread, 1)

                def add_y(n, par, last=False):
                    for h in range(HALVES):
                        pe.wait_ge(z.weighted, 2 * (b * DS + n) + h + 1)
                        for _, a, c in halves_of:
                            mm = nc.tensor.matmul(y[h][:, a:c], m.ident[:, :], t.g[:, par, h, a:c], start=False, stop=last)
                        mm.then_inc(z.y_added, 1)

                if b:
                    pe.wait_ge(z.y_gated, HALVES * b)
                for h in range(HALVES):
                    for _, a, c in halves_of:
                        nc.tensor.matmul(y[h][:, a:c], t.diag[:, h * P:(h + 1) * P], t.xs[:, h, b * T + a:b * T + c],
                                         start=True, stop=False)
                spread_bc(0)
                with pe.Fori(0, PAIRS - 1) as mm_:
                    for par in range(2):
                        spread_bc(2 * mm_ + par + 1)
                        add_y(2 * mm_ + par, par)
                spread_bc(DS - 1)
                add_y(DS - 2, 0)
                add_y(DS - 1, 1, last=True)

        @block.scalar
        def _(act):
            nc.scalar.preload_act_table(ACT.Exp)
            for b in range(B):
                with act.Fori(0, PAIRS) as mm_:
                    for par in range(2):
                        n = 2 * mm_ + par
                        k = b * DS + n
                        for h in range(HALVES):
                            act.wait_ge(z.scanned, PRIMED + (2 * k - 1 + h if b else 2 * k + h))
                            apart(act)
                            nc.scalar.activation(t.dA[:, h, :], t.dt[:, h, b * T:(b + 1) * T], ACT.Exp,
                                                 scale=t.A[:, bass.ds(h * DS + n, 1)]).then_inc(z.decayed, 1)
                            if h == 0:
                                act.wait_ge(z.c_spread, k + 1)
                                if b:
                                    act.wait_ge(z.weighted, 2 * k - 2)
                                nc.scalar.activation(t.Cs[:, par, :], psC[:, :], ACT.Copy).then_inc(z.c_saved, 1)

        @block.vector
        def _(dve):
            prime(dve, z.scanned)
            for b in range(B):
                with dve.Fori(0, PAIRS) as mm_:
                    for par in range(2):
                        k = b * DS + 2 * mm_ + par
                        for h in range(HALVES):
                            g = t.g[:, par, h, :]
                            j = 2 * k + h
                            if b:
                                dve.wait_ge(z.y_added, j - 3)
                            dve.wait_ge(z.b_spread, k + 1)
                            nc.vector.tensor_tensor(g, psB[:, :], t.u[:, h, b * T:(b + 1) * T], ALU.mult).then_inc(z.b_used, 1)
                            dve.wait_ge(z.b_used, j + 1)
                            dve.wait_ge(z.decayed, j + 1)
                            nc.vector.tensor_tensor_scan(g, t.dA[:, h, :], g, 0.0, ALU.mult, ALU.add).then_inc(z.scanned, 1)
                for h in range(HALVES):
                    szb = t.sz[:, h, b * T:(b + 1) * T]
                    dve.wait_ge(z.y_added, HALVES * DS * (b + 1))
                    nc.vector.tensor_tensor(szb, y[h][:, :], szb, ALU.mult).then_inc(z.y_gated, 1)

        @block.gpsimd
        def _(pool):
            for b in range(B):
                with pool.Fori(0, PAIRS) as mm_:
                    for par in range(2):
                        k = b * DS + 2 * mm_ + par
                        for h in range(HALVES):
                            g = t.g[:, par, h, :]
                            pool.wait_ge(z.c_saved, k + 1)
                            pool.wait_ge(z.scanned, PRIMED + 2 * k + h + 1)
                            nc.gpsimd.tensor_tensor(g, g, t.Cs[:, par, :], ALU.mult).then_inc(z.weighted, 1)


def mixer_output(m, t):
    nc = m.nc
    z = semaphores(m.sem, "mo_", ("summed", "added"))
    with nc.Block() as block:
        @block.tensor
        def _(pe):
            for s in range(NSUP):
                for h in range(HALVES):
                    mm = nc.tensor.matmul(m.bank[s][:, 0:SUP], m.l("w_out")[:, h * D:(h + 1) * D],
                                          t.sz[:, h, s * SUP:(s + 1) * SUP], start=(h == 0), stop=(h == HALVES - 1))
                mm.then_inc(z.summed, 1)

        @block.vector
        def _(dve):
            for s in range(NSUP):
                x = m.xC[:, s * SUP:(s + 1) * SUP]
                dve.wait_ge(z.summed, s + 1)
                nc.vector.scalar_tensor_tensor(out=x, in0=m.bank[s][:, 0:SUP], scalar=m.gated(1, 2, s), in1=x,
                                               op0=ALU.mult, op1=ALU.add).then_inc(z.added, 1)



def experts(m):
    ar = m.arena
    m.hC = ar[:, 0:N]
    layer_norm(m, m.xC, lambda s: m.hC[:, s * SUP:(s + 1) * SUP], lambda s: m.scale1(1, 4, s), lambda s: m.shift(1, 3, s),
               tmp=N)
    top_two_gating(m, ar[:, N:ar.shape[1]])
    expert_sums(m, ar[:, N:ar.shape[1]])


def top_two_gating(m, tmp):
    nc, g = m.nc, m.gt
    call = m.gt_calls
    m.gt_calls += 1
    m.rwTf = m.ffn[0:NPART * E, 0:N]
    KE = NBLK * E
    at = 0

    def take(width):
        nonlocal at
        at += width
        return tmp[:, at - width:at]

    sc, rw, total = take(KE), take(KE), take(NBLK)
    rw3 = take(NPART * KE).rearrange("p (k a e) -> p k a e", k=NBLK, a=NPART)
    low = take(KE // 2).bitcast(BF16).rearrange("p (k e) -> p k e", e=E)
    rank_tmp = take(2 * NBLK * E * E + KE)
    ke = lambda v: v.rearrange("p (k e) -> p k e", e=E)
    raw = m.bank[3][:, 0:KE]
    with nc.Block() as block:
        @block.tensor
        def _(pe):
            for k in range(NBLK):
                mm = nc.tensor.matmul(raw[:, k * E:(k + 1) * E], m.hC[:, k * P:(k + 1) * P], m.l("gate_w"), start=True, stop=True)
            mm.then_inc(g.logits, 1)
            turn_weights(m, pe, rw3, call)

        @block.scalar
        def _(act):
            act.wait_ge(g.act_in, call + 1)
            nc.scalar.activation(sc, sc, ACT.Sigmoid).then_inc(g.act_out, 1)
            copy_weights(m, act, call, also=m.rwTf)

        @block.vector
        def _(dve):
            step = m.dve.on(dve)
            dve.wait_ge(g.logits, call + 1)
            nc.vector.tensor_tensor(ke(sc), ke(raw), m.r("gate_bias").unsqueeze(1).broadcast_to([P, NBLK, E]),
                                    ALU.add).then_inc(g.act_in, 1)
            dve.wait_ge(g.act_out, 2 * call + 1)
            chosen = top_two(m, step, ke(sc), rank_tmp)
            step(nc.vector.tensor_tensor(ke(rw), ke(sc), chosen, ALU.mult))
            step(nc.vector.tensor_reduce(total, ke(rw), AX.X, ALU.add))
            step(nc.vector.tensor_scalar(total, total, 1e-6, None, ALU.add))
            step(nc.vector.reciprocal(total, total))
            step(nc.vector.tensor_tensor(ke(rw), ke(rw), total.unsqueeze(2).broadcast_to([P, NBLK, E]), ALU.mult))
            split_weights(m, step, ke(rw), rw3, low)


def expert_sums(m, tmp):
    nc = m.nc
    names = ("up", "gelu", "spread", "scaled", "used", "biased", "added", "stored", "sbd")
    z = semaphores(m.sem, "ex_", names)
    XB = 4
    CH = (E + 1) * FC
    LAG = 3
    SHARED = 0.1
    ge = tmp[:, 0:XB * SUP].rearrange("p (u c) -> p u c", u=XB)
    ie = tmp[:, XB * SUP:2 * XB * SUP].rearrange("p (u c) -> p u c", u=XB)
    yb = tmp[:, 2 * XB * SUP:2 * XB * SUP + 2 * SUP].rearrange("p (u c) -> p u c", u=2)
    sbd = m.small[:, 40:41]
    up = [m.bank[i // 2][:, (i % 2) * SUP:(i % 2 + 1) * SUP] for i in range(4)]
    wB = [m.bank[2][:, 0:SUP], m.bank[2][:, SUP:2 * SUP]]
    acc = lambda par: m.bank[3][:, par * SUP:(par + 1) * SUP]
    up_w = lambda c: m.l("wu")[:, c * P:(c + 1) * P] if c < E * FC else m.l("swu")[:, (c - E * FC) * P:(c - E * FC + 1) * P]
    down_w = lambda c: m.l("wd")[:, c * P:(c + 1) * P] if c < E * FC else m.l("swd")[:, (c - E * FC) * P:(c - E * FC + 1) * P]
    up_b = lambda c: m.l("bu")[:, c:c + 1] if c < E * FC else m.l("sbu")[:, c - E * FC:c - E * FC + 1]
    PAIRS = NSUP // 2
    with nc.Block() as block:
        @block.tensor
        def _(pe):
            prime(pe, z.used)
            with pe.Fori(0, PAIRS) as p2:
                for par in range(2):
                    s = 2 * p2 + par
                    base = CH * s
                    h = m.hC[:, bass.ds(s * SUP, SUP)]
                    pe.wait_ge(z.scaled, PRIMED + base)
                    apart(pe)
                    spread(m, wB[0], 0, s).then_inc(z.spread, 1)
                    pe.wait_ge(z.added, PRIMED + 2 * p2)
                    apart(pe)
                    nc.tensor.matmul(acc(par), m.l("bd")[0:NPART * E, :], m.rwTf[:, bass.ds(s * SUP, SUP)], start=True, stop=False)
                    for c in range(CH + LAG):
                        if c < CH:
                            pe.wait_ge(z.gelu, PRIMED + base + max(0, c - XB + 1))
                            apart(pe)
                            nc.tensor.matmul(up[c % XB], up_w(c), h, start=True, stop=True).then_inc(z.up, 1)
                        if c >= LAG:
                            d = c - LAG
                            pe.wait_ge(z.scaled, PRIMED + base + d + 1)
                            nc.tensor.matmul(acc(par), down_w(d), ie[:, d % XB, :], start=False,
                                             stop=(d == CH - 1)).then_inc(z.used, 1)
                            if d % FC == 0 and d // FC + 1 < E:
                                spread(m, wB[(d // FC + 1) % 2], d // FC + 1, s).then_inc(z.spread, 1)

        @block.scalar
        def _(act):
            prime(act, z.gelu)
            nc.scalar.preload_act_table(ACT.Gelu)
            with act.Fori(0, PAIRS) as p2:
                for par in range(2):
                    s = 2 * p2 + par
                    base = CH * s
                    for c in range(CH):
                        act.wait_ge(z.scaled, PRIMED + base + max(0, c - XB + 1))
                        act.wait_ge(z.up, base + c + 1)
                        nc.scalar.activation(ge[:, c % XB, :], up[c % XB], ACT.Gelu, bias=up_b(c)).then_inc(z.gelu, 1)
                    act.wait_ge(z.sbd, 1)
                    act.wait_ge(z.added, PRIMED + 2 * p2)
                    act.wait_ge(z.used, PRIMED + base + CH)
                    nc.scalar.activation(yb[:, par, :], acc(par), ACT.Identity, bias=sbd).then_inc(z.biased, 1)

        @block.vector
        def _(dve):
            prime(dve, z.scaled, z.added)
            nc.vector.tensor_scalar(sbd, m.l("sbd"), SHARED, None, ALU.mult).then_inc(z.sbd, 1)

            def finish(s, par, p2):
                dve.wait_ge(z.biased, s + 1)
                apart(dve)
                x = m.xC[:, bass.ds(s * SUP, SUP)]
                nc.vector.scalar_tensor_tensor(out=x, in0=yb[:, par, :], scalar=m.gate[:, bass.ds((6 + 5) * B + p2, 1)],
                                               in1=x, op0=ALU.mult, op1=ALU.add).then_inc(z.added, 1)

            with dve.Fori(0, PAIRS) as p2:
                for par in range(2):
                    s = 2 * p2 + par
                    base = CH * s
                    for c in range(CH):
                        dve.wait_ge(z.used, PRIMED + base + max(0, c - XB + 1))
                        if c < E * FC:
                            dve.wait_ge(z.spread, E * s + c // FC + 1)
                        dve.wait_ge(z.gelu, PRIMED + base + c + 1)
                        if c < E * FC:
                            nc.vector.tensor_tensor(ie[:, c % XB, :], ge[:, c % XB, :], wB[(c // FC) % 2],
                                                    ALU.mult).then_inc(z.scaled, 1)
                        else:
                            nc.vector.tensor_scalar(ie[:, c % XB, :], ge[:, c % XB, :], SHARED, None,
                                                    ALU.mult).then_inc(z.scaled, 1)
                    finish(s, par, p2)

        @block.sync
        def _(sp):
            for s in range(NSUP):
                sp.wait_ge(z.added, PRIMED + s + 1)
                sp.dma_start(m.out[:, s * SUP:(s + 1) * SUP], m.xC[:, s * SUP:(s + 1) * SUP]).then_inc(z.stored, 16)
            sp.wait_ge(z.stored, 16 * NSUP)



def packed(inputs):
    g = {k: np.asarray(v) for k, v in inputs.items()}
    col = lambda v: v.reshape(-1, 1)
    halves = lambda w: w.reshape(HALVES, P, -1).transpose(1, 0, 2).reshape(P, -1)
    experts = lambda w: w.transpose(1, 0, 2).reshape(P, -1)
    att = {"wq": g["L0_attn_Wq"].T, "wk": g["L0_attn_Wk"].T, "wv": g["L0_attn_Wv"].T, "wo": g["L0_attn_Wo"].T,
           "wmod0": g["L0_wmod"], "wmod1": g["L1_wmod"], "c": np.concatenate([g["L0_c"].T, g["L1_c"].T], axis=1),
           "bq": col(g["L0_attn_bq"]), "bk": col(g["L0_attn_bk"]), "bv": col(g["L0_attn_bv"]), "bo": col(g["L0_attn_bo"]),
           "ln1w": col(g["L0_ffn_ln1_w"]), "ln1b": col(g["L0_ffn_ln1_b"]), "ln2w": col(g["L0_ffn_ln2_w"]),
           "ln2b": col(g["L0_ffn_ln2_b"]), "smha_sim": g["L0_ffn_smha_sim"], "moe_sim": g["L0_ffn_moe_sim"]}
    ffn = {"qp": experts(g["L0_ffn_q_proj"]), "kp": experts(g["L0_ffn_k_proj"]), "vp": experts(g["L0_ffn_v_proj"]),
           "op": experts(g["L0_ffn_o_proj"]), "w1": experts(g["L0_ffn_w1"]), "w2": experts(g["L0_ffn_w2"])}
    bd = np.concatenate([g["L1_ffn_bd"]] * NPART + [np.zeros((P - NPART * E, D), np.float32)])
    l1 = {"w_in": g["L1_attn_W_in"], "w_x": halves(g["L1_attn_W_x"]), "w_out": halves(g["L1_attn_W_out"]),
          "b_conv": halves(g["L1_attn_b_conv"]), "w_dt": halves(g["L1_attn_W_dt"][0]), "b_dt": halves(g["L1_attn_b_dt"]),
          "a_log": halves(g["L1_attn_A_log"]), "dskip": halves(g["L1_attn_D"]), "gate_w": g["L1_ffn_gate_w"].T,
          "wu": g["L1_ffn_Wu"].transpose(2, 0, 1).reshape(P, -1),
          "bu": g["L1_ffn_bu"].reshape(E, FC, P).transpose(2, 0, 1).reshape(P, -1),
          "wd": g["L1_ffn_Wd"].reshape(E, D, FC, P).transpose(3, 0, 2, 1).reshape(P, -1),
          "swu": g["L1_ffn_sWu"].T, "sbu": g["L1_ffn_sbu"].reshape(FC, P).T,
          "swd": g["L1_ffn_sWd"].reshape(D, FC, P).transpose(2, 1, 0).reshape(P, -1), "sbd": col(g["L1_ffn_sbd"]), "bd": bd}
    row = {"alpha": g["L0_attn_alpha"].reshape(1), "smha_gates": g["L0_ffn_smha_gates"], "moe_gates": g["L0_ffn_moe_gates"],
           "gate_bias": g["L1_ffn_gate_bias"], "w_conv": g["L1_attn_W_conv"][:, 0, :].T.reshape(-1)}
    side = lambda cols, parts: np.ascontiguousarray(np.concatenate([parts[k] for k in cols], axis=-1))
    return {"att_w": side(ATT_COLS, att), "ffn_w": side(FFN_COLS, ffn), "l1_w": side(L1_COLS, l1),
            "row_w": side(ROW_COLS, row).reshape(1, -1),
            "x_channels": np.ascontiguousarray(g["L0_attn_x"].reshape(N, D).T)}


def kernel(**inputs):
    import concourse.bacc as _bacc
    from concourse.bass_utils import run_bass_kernel_spmd as _run

    nc = _bacc.Bacc("TRN2", target_bir_lowering=False, num_devices=1)
    arrays = packed(inputs)
    args = {k: nc.dram_tensor(k, a.shape, mybir.dt.from_np(a.dtype), kind="ExternalInput").ap() for k, a in arrays.items()}
    out = nc.dram_tensor("out_channels", (P, N), F32, kind="ExternalOutput").ap()
    build(nc, args["att_w"], args["ffn_w"], args["l1_w"], args["row_w"], args["x_channels"], out)
    r = _run(nc, [arrays], core_ids=[0])
    return np.ascontiguousarray(r.results[0]["out_channels"].T).reshape(B, T, D)
```

```python
from collections import namedtuple
from contextlib import ExitStack

import numpy as np
import concourse.bass as bass
from concourse import mybir

F32 = mybir.dt.float32
BF16 = mybir.dt.bfloat16
ALU = mybir.AluOpType
ACT = mybir.ActivationFunctionType
AX = mybir.AxisListType

P = 128
B, T, D = 2, 1024, 128
N = B * T
SUP = 512
NSUP = N // SUP
SUPB = T // SUP
NBLK = N // P
BLKS = SUP // P
NH, HD = 16, 8
HG = 4
NG = NH // HG
QB = T // P
E = 8
DI, DS, KC = 256, 16, 4
HALVES = DI // P
F = 512
FC = F // P
EPS = 1e-5
NEG = -3.0e38
TILE = 32
NPART = 3
TERMS = NPART * NPART - 1
STACK = TERMS * HD

PRIMED = 1


def columns(parts):
    at, out = 0, {}
    for name, width in parts:
        out[name] = (at, width)
        at += width
    return out, at


ATT_COLS, ATT_W = columns([
    ("wq", D), ("wk", D), ("wv", D), ("wo", D), ("wmod0", 6 * D), ("wmod1", 6 * D), ("c", 2 * B),
    ("bq", 1), ("bk", 1), ("bv", 1), ("bo", 1), ("ln1w", 1), ("ln1b", 1), ("ln2w", 1), ("ln2b", 1),
    ("smha_sim", E), ("moe_sim", E)])
FFN_COLS, FFN_W = columns([
    ("qp", E * D), ("kp", E * D), ("vp", E * D), ("op", E * D), ("w1", E * D), ("w2", E * D)])
L1_COLS, L1_W = columns([
    ("w_in", 2 * DI), ("w_x", HALVES * (2 * DS + 1)), ("w_out", HALVES * D), ("b_conv", HALVES), ("w_dt", HALVES),
    ("b_dt", HALVES), ("a_log", HALVES * DS), ("dskip", HALVES), ("gate_w", E), ("wu", E * F), ("bu", E * FC),
    ("wd", E * F), ("swu", F), ("sbu", FC), ("swd", F), ("sbd", 1), ("bd", D)])
ROW_COLS, ROW_W = columns([("alpha", 1), ("smha_gates", E), ("moe_gates", E), ("gate_bias", E), ("w_conv", KC * DI)])


class Shared:
    pass


def semaphores(sem, prefix, names):
    return namedtuple("Semaphores", names)(*[sem(prefix + name) for name in names])


class Steps:

    def __init__(self, sem):
        self.sem, self.count = sem, 0

    def on(self, engine):
        def step(ins):
            self.count += 1
            ins.then_inc(self.sem, 1)
            engine.wait_ge(self.sem, self.count)
        return step


def apart(engine):
    engine.nop(nofuse=True)


def prime(engine, *sems, count=PRIMED):
    for sem in sems:
        engine.nop(nofuse=True).then_inc(sem, count)


def build(nc, att_in, ffn_in, l1_in, row_in, x_in, out):
    ctx = ExitStack()
    with ctx:
        def sb(name, shape, dt=F32):
            return ctx.enter_context(nc.sbuf_tensor(name, shape, dt))

        def sem(name):
            return ctx.enter_context(nc.semaphore(name))

        m = Shared()
        m.nc, m.sem, m.out = nc, sem, out
        m.xC = sb("xC", [P, N])
        m.att = sb("att_tile", [P, ATT_W])
        m.ffn = sb("ffn_tile", [P, FFN_W])
        m.late = sb("late", [P, L1_W])
        m.row = sb("row", [P, ROW_W])
        m.ident = sb("ident", [P, P])
        m.ones = sb("ones", [P, P])
        m.causal = sb("causal", [P, P])
        m.ident16 = sb("ident16", [P, P], BF16)
        m.countdown = sb("countdown", [P, E])
        m.one_at_e = sb("one_at_e", [P, TILE])
        m.sel_e = sb("sel_e", [NPART * E, E, P], BF16)
        m.mod = sb("mod", [P, 2 * 6 * B])
        m.gsign = sb("gsign", [P, 2 * 6 * B])
        m.gate = sb("gate", [P, 2 * 6 * B])
        m.small = sb("small", [P, 64])
        m.eps = m.small[:, 2:3]
        m.rowg = sb("rowg", [P, 2 * E])
        m.rwT = sb("rwT", [NPART * E, N], BF16)
        m.sel_n = sb("sel_n", [NPART * 2 * DS, 2 * DS, P], BF16)
        m.arena = sb("arena", [P, 25552])
        m.bank = [ctx.enter_context(nc.psum_tensor(f"bank{i}", [P, 2 * SUP], F32)) for i in range(4)]
        m.qk_parts = nc.dram_tensor("qk_parts", [2, NPART, D, N], BF16).ap()
        m.att_in, m.ffn_in, m.l1_in, m.row_in, m.x_in = att_in, ffn_in, l1_in, row_in, x_in
        m.dve = Steps(sem("dve_step"))
        m.act = Steps(sem("act_step"))
        m.pool = Steps(sem("pool_step"))
        m.att_loaded, m.ffn_loaded, m.l1_loaded = sem("att_loaded"), sem("ffn_loaded"), sem("l1_loaded")
        m.ln = semaphores(sem, "ln_", ("raw_T", "var", "std", "norm", "out_T"))
        m.gt = semaphores(sem, "gate_", ("sq", "simsq", "simstd", "sim", "logits", "saved", "turned", "act_out", "act_in", "split",
                                        "splitT"))
        m.ln_calls = m.gt_calls = 0

        def a(name):
            at, w = ATT_COLS[name]
            return m.att[:, at:at + w]

        def f(name):
            at, w = FFN_COLS[name]
            return m.ffn[:, at:at + w]

        def l(name):
            at, w = L1_COLS[name]
            return m.late[:, at:at + w]

        def r(name):
            at, w = ROW_COLS[name]
            return m.row[:, at:at + w]

        m.a, m.f, m.l, m.r = a, f, l, r
        ar = m.arena

        load_and_constants(m)
        modulation(m)
        hC = ar[:, 0:N]
        layer_norm(m, m.xC, lambda s: hC[:, s * SUP:(s + 1) * SUP], lambda s: m.scale1(0, 1, s), lambda s: m.shift(0, 0, s), tmp=2 * N,
                   meanwhile=lambda pool: zero_stacks(m, pool))
        head_projections(m, hC)
        decayed_attention(m)
        attention_output(m)
        feed_forward(m)
        mixer(m)
        experts(m)



def load_and_constants(m):
    nc = m.nc
    zeroed, lag_ready, negalpha = m.sem("zeroed"), m.sem("lag_ready"), m.sem("negalpha")
    t = attention_tiles(m)
    vaug, decay = t.vaug, t.decay
    m.decay_ready = m.sem("decay_ready")
    with nc.Block() as block:
        @block.sync
        def _(sp):
            sp.dma_start(m.att[:, :], m.att_in).then_inc(m.att_loaded, 16)
            sp.dma_start(m.row[:, :], m.row_in.partition_broadcast(P)).then_inc(m.att_loaded, 16)
            sp.dma_start(m.xC[:, :], m.x_in).then_inc(m.att_loaded, 16)
            sp.dma_start(m.ffn[:, :], m.ffn_in).then_inc(m.ffn_loaded, 16)
            sp.wait_ge(m.att_loaded, 48)

        @block.gpsimd
        def _(pool):
            step = m.pool.on(pool)
            nc.gpsimd.memset(m.ident[:, :], 0.0)
            nc.gpsimd.memset(m.causal[:, :], 0.0)
            nc.gpsimd.memset(m.sel_e[:, :, :], 0.0)
            nc.gpsimd.memset(m.ones[:, :], 1.0)
            nc.gpsimd.memset(m.eps, EPS)
            nc.gpsimd.memset(vaug[:, :, :, HD:HD + 1], 1.0)
            step(nc.gpsimd.memset(m.small[:, 3:4], 0.0))
            (nc.gpsimd.iota(decay[:, :], pattern=[[1, 2 * T - P]], base=-(T - P), channel_multiplier=-1,
                                allow_small_or_imprecise_dtypes=True)).then_inc(lag_ready, 1)
            nc.gpsimd.affine_select(out=m.ident[:, :], in_=m.ident[:, :], compare_op=ALU.not_equal, fill=1.0,
                                    base=0, pattern=[[-1, P]], channel_multiplier=1)
            nc.gpsimd.affine_select(out=m.causal[:, :], in_=m.causal[:, :], compare_op=ALU.is_ge, fill=NEG,
                                    base=0, pattern=[[-1, P]], channel_multiplier=1)
            for part in range(NPART):
                step(nc.gpsimd.affine_select(out=m.sel_e[:, :, :], in_=m.sel_e[:, :, :], compare_op=ALU.not_equal,
                                             fill=1.0, base=-part * E, pattern=[[-1, E], [0, P]],
                                             channel_multiplier=1))
            nc.gpsimd.iota(m.countdown[:, :], pattern=[[-1, E]], base=E, channel_multiplier=0,
                           allow_small_or_imprecise_dtypes=True)
            step(nc.gpsimd.memset(m.one_at_e[:, :], 0.0))
            nc.gpsimd.memset(m.one_at_e[:, E:E + 1], 1.0)
            step(nc.gpsimd.tensor_copy(m.ident16[:, :], m.ident[:, :]))

        @block.vector
        def _(dve):
            dve.wait_ge(m.att_loaded, 48)
            nc.vector.tensor_scalar(m.small[:, 0:1], m.r("alpha"), -1.0, None, ALU.mult).then_inc(negalpha, 1)

        @block.scalar
        def _(act):
            act.wait_ge(lag_ready, 1)
            step = m.act.on(act)
            step(nc.scalar.activation(decay[:, :], decay[:, :], ACT.Abs))
            act.wait_ge(negalpha, 1)
            nc.scalar.activation(decay[:, :], decay[:, :], ACT.Exp, scale=m.small[:, 0:1])
            nc.scalar.activation(m.rowg[:, 0:2 * E], m.row[:, ROW_COLS["smha_gates"][0]:ROW_COLS["smha_gates"][0] + 2 * E],
                                 ACT.Sigmoid)


def modulation(m):
    nc = m.nc
    silu_ready, mod_summed = m.sem("silu_ready"), m.sem("mod_summed")
    silu_c = m.small[:, 4:4 + 2 * B]
    ps = m.bank[0]
    W = 2 * 6 * B
    with nc.Block() as block:
        @block.scalar
        def _(act):
            nc.scalar.activation(silu_c, m.a("c"), ACT.Silu).then_inc(silu_ready, 1)

        @block.tensor
        def _(pe):
            pe.wait_ge(silu_ready, 1)
            for layer in range(2):
                w = m.a(f"wmod{layer}")
                for j in range(6):
                    at = (layer * 6 + j) * B
                    mm = nc.tensor.matmul(ps[:, at:at + B], w[:, j * D:(j + 1) * D],
                                          silu_c[:, layer * B:(layer + 1) * B], start=True, stop=True)
            mm.then_inc(mod_summed, 1)

        @block.vector
        def _(dve):
            step = m.dve.on(dve)
            dve.wait_ge(mod_summed, 1)
            step(nc.vector.tensor_copy(m.mod[:, :], ps[:, 0:W]))
            step(nc.vector.tensor_scalar(m.gsign[:, :], m.mod[:, :], 0.0, 2.0, ALU.is_ge, ALU.mult))
            step(nc.vector.scalar_tensor_tensor(out=m.gate[:, :], in0=m.mod[:, :], scalar=-1.0, in1=m.mod[:, :],
                                                op0=ALU.mult, op1=ALU.max))
            step(nc.vector.tensor_scalar(m.gate[:, :], m.gate[:, :], 0.25, None, ALU.max))
            step(nc.vector.scalar_tensor_tensor(out=m.gate[:, :], in0=m.gsign[:, :], scalar=-1.0, in1=m.gate[:, :],
                                                op0=ALU.add, op1=ALU.mult))
            step(nc.vector.tensor_scalar(m.gsign[:, :], m.mod[:, :], 1.0, None, ALU.add))
            step(nc.vector.tensor_scalar(m.small[:, 1:2], m.a("bq"), float(HD) ** -0.5, None, ALU.mult))

    def column(tile, layer, j, b):
        at = (layer * 6 + j) * B + b
        return tile[:, at:at + 1]

    m.scale1 = lambda layer, j, s: column(m.gsign, layer, j, s // SUPB)
    m.shift = lambda layer, j, s: column(m.mod, layer, j, s // SUPB)
    m.gated = lambda layer, j, s: column(m.gate, layer, j, s // SUPB)



def layer_norm(m, src, dst, scale, bias, tmp, meanwhile=None):
    nc, ln = m.nc, m.ln
    call = m.ln_calls
    m.ln_calls += 1
    c4, c1 = call * NSUP, call * NBLK
    t0 = tmp
    xn = m.arena[:, t0:t0 + NSUP * SUP].rearrange("p (s j c) -> p s j c", s=NSUP, j=BLKS)
    t1 = t0 + NSUP * SUP
    stats = m.arena[:, t1:t1 + 96].rearrange("p (k c) -> p k c", c=6)
    mv = m.arena[:, t1 + 96:t1 + 128].rearrange("p (k c) -> p k c", c=2)
    std = m.small[:, 8:8 + NBLK]
    rstd = m.small[:, 24:24 + NBLK]
    raw = lambda s: m.bank[s // 2][:, (s % 2) * SUP:(s % 2 + 1) * SUP]
    back = lambda s: m.bank[2 + s // 2][:, (s % 2) * SUP:(s % 2 + 1) * SUP]
    with nc.Block() as block:
        if meanwhile is not None:
            @block.gpsimd
            def _(pool):
                meanwhile(pool)

        @block.tensor
        def _(pe):
            for s in range(NSUP):
                for j in range(BLKS):
                    at = s * SUP + j * P
                    mm = nc.tensor.transpose(raw(s)[:, j * P:(j + 1) * P], src[:, at:at + P], m.ident[:, :])
                mm.then_inc(ln.raw_T, 1)
            for s in range(NSUP):
                pe.wait_ge(ln.norm, c4 + s + 1)
                for j in range(BLKS):
                    mm = nc.tensor.transpose(back(s)[:, j * P:(j + 1) * P], xn[:, s, j, :], m.ident[:, :])
                mm.then_inc(ln.out_T, 1)

        @block.vector
        def _(dve):
            step = m.dve.on(dve)

            def statistics(s):
                dve.wait_ge(ln.raw_T, c4 + s + 1)
                for j in range(BLKS):
                    ins = nc.vector.bn_stats(stats[:, s * BLKS + j, :], raw(s)[:, j * P:(j + 1) * P])
                step(ins)
                for j in range(BLKS):
                    ins = nc.vector.bn_aggr(mv[:, s * BLKS + j, :], stats[:, s * BLKS + j, :])
                ins.then_inc(ln.var, 1)

            def normalise(s):
                k0 = s * BLKS
                dve.wait_ge(ln.std, c4 + s + 1)
                step(nc.vector.reciprocal(rstd[:, k0:k0 + BLKS], std[:, k0:k0 + BLKS]))
                for j in range(BLKS):
                    k = k0 + j
                    ins = nc.vector.tensor_scalar(xn[:, s, j, :], raw(s)[:, j * P:(j + 1) * P], mv[:, k, 0:1],
                                                  rstd[:, k:k + 1], ALU.subtract, ALU.mult)
                ins.then_inc(ln.norm, 1)

            statistics(0)
            for s in range(1, NSUP):
                statistics(s)
                normalise(s - 1)
            normalise(NSUP - 1)

        @block.scalar
        def _(act):
            for s in range(NSUP):
                k0 = s * BLKS
                act.wait_ge(ln.var, c4 + s + 1)
                nc.scalar.activation(std[:, k0:k0 + BLKS], mv[:, k0:k0 + BLKS, 1], ACT.Sqrt,
                                     bias=m.eps[:, 0:1]).then_inc(ln.std, 1)
            for s in range(NSUP):
                act.wait_ge(ln.out_T, c4 + s + 1)
                nc.scalar.activation(dst(s), back(s), ACT.Identity, bias=bias(s), scale=scale(s))



def attention_tiles(m):
    ar = m.arena
    t = Shared()
    at = 0

    def take(width):
        nonlocal at
        at += width
        return ar[:, at - width:at]

    t.qpair = take(2 * 2 * T // 2).bitcast(BF16).rearrange("p (u h q) -> p u h q", u=2, h=2)
    t.weighted = take(4 * T).rearrange("p (u k) -> p u k", u=4)
    t.probsT = take(2 * HG * QB * P).rearrange("p (u h k q) -> p u h k q", u=2, h=HG, k=QB)
    t.vstat = take(2 * QB * HG * 32).rearrange("p (u k h c) -> p u k h c", u=2, k=QB, h=HG)
    m.heads_end = at
    t.kpad = take(2 * HG * T // 2).bitcast(BF16).rearrange("p (u h k) -> p u h k", u=2, h=HG)
    t.vaug = take(NBLK * NH * (HD + 1)).rearrange("p (k h c) -> p k h c", k=NBLK, h=NH)
    t.decay = take(2 * T - P)
    assert at <= ar.shape[1], at
    t.raw = m.late[:, 0:B * NG * QB * P].rearrange("p (n q) -> p n q", q=P)
    return t


def zero_stacks(m, pool):
    t, step = attention_tiles(m), m.pool.on(pool)
    step(m.nc.gpsimd.memset(t.kpad[0:STACK, :, 1:HG:2, :], 0.0))
    step(m.nc.gpsimd.memset(t.kpad[STACK:P, :, 0:HG:2, :], 0.0))


def head_projections(m, hC):
    nc, t = m.nc, attention_tiles(m)
    s_q, s_k, s_v = m.sem("q_summed"), m.sem("k_summed"), m.sem("v_summed")
    s_first, s_second, s_third = m.sem("part1_ready"), m.sem("part2_ready"), m.sem("part3_ready")
    s_rest, s_qk_free, s_v_free = m.sem("rest_ready"), m.sem("qk_free"), m.sem("v_free")
    parts_stored = m.sem("parts_stored")
    base = N
    full = [m.arena[:, base + i * N:base + (i + 1) * N] for i in range(2)]
    rest = [m.arena[:, base + (2 + i) * N:base + (3 + i) * N] for i in range(2)]
    all_parts = m.arena[:, base + 4 * N:base + 4 * N + 2 * NPART * N // 2].bitcast(BF16).rearrange(
        "p (i a t) -> p i a t", i=2, a=NPART)
    parts = [[all_parts[:, i, j, :] for j in range(NPART)] for i in range(2)]
    assert base + 4 * N + 2 * NPART * N // 2 <= m.heads_end
    sup = lambda tile, s: tile[:, s * SUP:(s + 1) * SUP]
    half = lambda tile, s: tile[:, (s % 2) * SUP:(s % 2 + 1) * SUP]
    with nc.Block() as block:
        @block.tensor
        def _(pe):
            for s in range(NSUP):
                if s >= 2:
                    pe.wait_ge(s_qk_free, 2 * (s - 1))
                    pe.wait_ge(s_v_free, s - 1)
                nc.tensor.matmul(half(m.bank[0], s), m.a("wq"), sup(hC, s), start=True, stop=True).then_inc(s_q, 1)
                nc.tensor.matmul(half(m.bank[1], s), m.a("wk"), sup(hC, s), start=True, stop=True).then_inc(s_k, 1)
                for j in range(BLKS):
                    at = s * SUP + j * P
                    mm = nc.tensor.matmul(half(m.bank[2], s)[:, j * P:(j + 1) * P], hC[:, at:at + P], m.a("wv"),
                                          start=True, stop=True)
                mm.then_inc(s_v, 1)

        @block.scalar
        def _(act):
            for s in range(NSUP):
                act.wait_ge(s_q, s + 1)
                nc.scalar.activation(sup(full[0], s), half(m.bank[0], s), ACT.Identity, bias=m.small[:, 1:2],
                                     scale=float(HD) ** -0.5)
                nc.scalar.activation(sup(parts[0][0], s), half(m.bank[0], s), ACT.Identity, bias=m.small[:, 1:2],
                                     scale=float(HD) ** -0.5).then_inc(s_qk_free, 1)
                act.wait_ge(s_k, s + 1)
                nc.scalar.activation(sup(full[1], s), half(m.bank[1], s), ACT.Identity, bias=m.a("bk"))
                nc.scalar.activation(sup(parts[1][0], s), half(m.bank[1], s), ACT.Identity,
                                     bias=m.a("bk")).then_inc(s_qk_free, 1)
                for i in range(2):
                    act.wait_ge(s_rest, 2 * s + i + 1)
                    nc.scalar.activation(sup(parts[i][1], s), sup(rest[i], s), ACT.Copy).then_inc(s_second, 1)

        @block.vector
        def _(dve):
            for s in range(NSUP):
                for i in range(2):
                    dve.wait_ge(s_qk_free, 2 * s + i + 1)
                    nc.vector.tensor_tensor(sup(rest[i], s), sup(full[i], s), sup(parts[i][0], s),
                                            ALU.subtract).then_inc(s_rest, 1)
                dve.wait_ge(s_v, s + 1)
                nc.vector.tensor_copy(
                    t.vaug[:, s * BLKS:(s + 1) * BLKS, :, 0:HD].rearrange("p k h c -> p (k h) c"),
                    half(m.bank[2], s).rearrange("p (k c) -> p k c", c=HD)).then_inc(s_v_free, 1)
                for i in range(2):
                    dve.wait_ge(s_second, 2 * s + i + 1)
                    nc.vector.tensor_tensor(sup(parts[i][2], s), sup(rest[i], s), sup(parts[i][1], s),
                                            ALU.subtract).then_inc(s_third, 1)

        @block.gpsimd
        def _(pool):
            step = m.pool.on(pool)
            step(nc.gpsimd.memset(m.sel_n[:, :, :], 0.0))
            for part in range(NPART):
                step(nc.gpsimd.affine_select(out=m.sel_n[:, :, :], in_=m.sel_n[:, :, :], compare_op=ALU.not_equal, fill=1.0,
                                             base=-part * 2 * DS, pattern=[[-1, 2 * DS], [0, P]], channel_multiplier=1))

        @block.sync
        def _(sp):
            for s in range(NSUP):
                sp.wait_ge(s_third, 2 * (s + 1))
                for i in range(2):
                    sp.dma_start(m.qk_parts[i].rearrange("a d t -> d a t")[:, :, s * SUP:(s + 1) * SUP],
                                 all_parts[:, i, :, s * SUP:(s + 1) * SUP]).then_inc(parts_stored, 16)
            sp.wait_ge(parts_stored, 16 * 2 * NSUP)


def decayed_attention(m):
    nc, t = m.nc, attention_tiles(m)
    names = ("scored", "weighted", "negmax", "exped", "turnedA", "turnedB", "copiedA", "copiedB", "pv_done",
             "raw_saved", "v_early", "v_late", "tiles_zeroed")
    z = semaphores(m.sem, "att_", names)
    head_loaded = [m.sem(f"att_head_loaded{h}") for h in range(HG)]
    negm = m.small[:, 8:16]
    rowmax = m.small[:, 16:24]
    score = [m.bank[0], m.bank[1]]
    turnA, turnB = m.bank[2][:, 0:SUP], m.bank[2][:, SUP:2 * SUP]
    pv = [m.bank[3][:, 0:P], m.bank[3][:, SUP:SUP + P]]
    KB = QB // 2
    GROUPS = B * NG
    LOADED = 16 * 2 * NPART

    def every_group(engine, steps):
        steps(0)
        with engine.Fori(1, GROUPS - 1) as g:
            steps(g)
        steps(GROUPS - 1)

    with nc.Block() as block:
        @block.sync
        def _(sp):
            for g in range(GROUPS):
                b, hg, u = g // NG, g % NG, g % 2
                if g >= 2:
                    sp.wait_ge(z.scored, HG * QB * (g - 1))
                for head in range(HG):
                    if g:
                        sp.wait_ge(head_loaded[head], LOADED * g)
                    j, w = head // 2, head % 2
                    for i, tile in enumerate((t.qpair[:, u, j, :], t.kpad[:, u, head, :])):
                        src = m.qk_parts[i][:, :, b * T:(b + 1) * T].rearrange("a (h d) t -> h a d t", d=HD)[hg * HG + head]
                        for a in range(NPART):
                            n = NPART if a < NPART - 1 else NPART - 1
                            at = w * STACK + a * NPART * HD
                            rows = src[a].unsqueeze(0).broadcast_to([n, HD, T]) if i == 0 else src[0:n]
                            sp.dma_start(tile[at:at + n * HD], rows).then_inc(head_loaded[head], 16)

        @block.gpsimd
        def _(pool):
            nc.gpsimd.memset(t.vstat[:, :, :, :, :], 0.0).then_inc(z.tiles_zeroed, 1)
            pool.wait_ge(z.tiles_zeroed, 1)

            def steps(g):
                vg = t.vaug[:, bass.ds(((g >> 2) & (B - 1)) * QB, QB), bass.ds((g & (NG - 1)) * HG, HG), :]
                for i in range(QB):
                    n = QB * g + i
                    for u in range(HG):
                        k = HG * n + u
                        if i == 0 and u == 2:
                            after(pool, z.pv_done, n - 1)
                            apart(pool)
                            nc.gpsimd.tensor_copy(t.vstat[:, 0, :, :, 0:HD + 1], vg).then_inc(z.v_early, 1)
                        if i == 2 and u == 2:
                            after(pool, z.pv_done, n - 2)
                            apart(pool)
                            nc.gpsimd.tensor_copy(t.vstat[:, 1, :, :, 0:HD + 1], vg).then_inc(z.v_late, 1)
                        slot = k_slot(i, u)
                        after(pool, z.weighted, k + 1)
                        after(pool, z.exped, k - 7)
                        apart(pool)
                        nc.gpsimd.tensor_scalar(negm[:, slot:slot + 1], rowmax[:, slot:slot + 1], -1.0, None,
                                                ALU.mult).then_inc(z.negmax, 1)

            every_group(pool, steps)

        @block.tensor
        def _(pe):
            def scores(g, i, u):
                n = QB * g + i
                if i == 0:
                    for head in (u, u + 1) if u % 2 == 0 else (u,):
                        after(pe, head_loaded[head], LOADED * (g + 1))
                after(pe, z.weighted, HG * n + u - 1)
                for h in range(2):
                    mm = nc.tensor.matmul(score[u % 2][:, h * SUP:(h + 1) * SUP],
                                          t.qpair[:, g & 1, u // 2, i * P:(i + 1) * P],
                                          t.kpad[:, g & 1, u, h * SUP:(h + 1) * SUP], start=True, stop=True)
                mm.then_inc(z.scored, 1)

            def turn(g, i, u):
                k = HG * (QB * g + i) + u
                after(pe, z.exped, k + 1)
                for turned, bank, copied, k0 in ((z.turnedA, turnA, z.copiedA, 0), (z.turnedB, turnB, z.copiedB, KB)):
                    after(pe, copied, k)
                    for j in range(KB):
                        mm = nc.tensor.transpose(bank[:, j * P:(j + 1) * P], t.weighted[:, u, (k0 + j) * P:(k0 + j + 1) * P],
                                                 m.ident[:, :])
                    mm.then_inc(turned, 1)

            def values(g, i, u):
                n, par = QB * g + i, i % 2
                if u == 0:
                    after(pe, z.copiedA, HG * (n + 1))
                    after(pe, z.copiedB, HG * (n + 1))
                    if i == QB - 1:
                        after(pe, z.v_late, g + 1)
                    elif i == 0:
                        after(pe, z.v_early, g + 1)
                    after(pe, z.raw_saved, n - 1)
                for kb in (2 * u, 2 * u + 1):
                    for h in range(HG):
                        mm = nc.tensor.matmul(pv[par][32 * h:32 * (h + 1), :], t.vstat[:, i // (QB - 1), kb, h, :],
                                              t.probsT[:, par, h, kb, :], start=(kb == 0), stop=(kb == QB - 1))
                if u == HG - 1:
                    mm.then_inc(z.pv_done, 1)

            def steps(g):
                first, last = type(g) is int and g == 0, type(g) is int and g == GROUPS - 1
                for i in range(QB):
                    for u in range(HG):
                        if u < 2:
                            scores(g, i, u + 2)
                        elif i < QB - 1:
                            scores(g, i + 1, u - 2)
                        elif not last:
                            scores(g + 1, 0, u - 2)
                        turn(g, i, u)
                        if i:
                            values(g, i - 1, u)
                        elif not first:
                            values(g - 1, QB - 1, u)

            scores(0, 0, 0)
            scores(0, 0, 1)
            every_group(pe, steps)
            for u in range(HG):
                values(GROUPS - 1, QB - 1, u)

        @block.vector
        def _(dve):
            def copy_a(g, i, u):
                n, par = QB * g + i, i % 2
                if u == 0:
                    after(dve, z.pv_done, n - 1)
                after(dve, z.turnedA, HG * n + u + 1)
                nc.vector.tensor_copy(t.probsT[:, par, u, 0:KB, :].rearrange("p k q -> p (k q)"), turnA).then_inc(z.copiedA, 1)

            def steps(g):
                for i in range(QB):
                    for u in range(HG):
                        k, slot = HG * (QB * g + i) + u, k_slot(i, u)
                        after(dve, z.turnedB, k - 3)
                        after(dve, z.scored, k + 1)
                        start = (QB - 1 - i) * P
                        apart(dve)
                        nc.vector.tensor_tensor_reduce(t.weighted[:, u, :], score[u % 2][:, :],
                                                       t.decay[:, start:start + T], 1.0, NEG, ALU.mult, ALU.max,
                                                       rowmax[:, slot:slot + 1]).then_inc(z.weighted, 1)
                        if u >= 2:
                            copy_a(g, i, u - 2)
                        elif i:
                            copy_a(g, i - 1, u + 2)
                        elif not (type(g) is int and g == 0):
                            copy_a(g - 1, QB - 1, u + 2)

            every_group(dve, steps)
            copy_a(GROUPS - 1, QB - 1, HG - 2)
            copy_a(GROUPS - 1, QB - 1, HG - 1)

        @block.scalar
        def _(act):
            def copy_b(g, i, u):
                n, par = QB * g + i, i % 2
                if u == 0:
                    after(act, z.pv_done, n - 1)
                after(act, z.turnedB, HG * n + u + 1)
                nc.scalar.activation(t.probsT[:, par, u, KB:QB, :].rearrange("p k q -> p (k q)"), turnB,
                                     ACT.Copy).then_inc(z.copiedB, 1)

            def save(g, i):
                n = QB * g + i
                after(act, z.pv_done, n + 1)
                nc.scalar.activation(t.raw[:, n, :], pv[i % 2], ACT.Copy).then_inc(z.raw_saved, 1)

            def steps(g):
                first = type(g) is int and g == 0
                for i in range(QB):
                    for u in range(HG):
                        k, slot = HG * (QB * g + i) + u, k_slot(i, u)
                        after(act, z.negmax, k + 1)
                        nc.scalar.activation(t.weighted[:, u, :], t.weighted[:, u, :], ACT.Exp,
                                             bias=negm[:, slot:slot + 1]).then_inc(z.exped, 1)
                        unit_before(g, i, u, copy_b)
                        if u == 1:
                            if i >= 2:
                                save(g, i - 2)
                            elif not first:
                                save(g - 1, QB - 2 + i)

            nc.scalar.preload_act_table(ACT.Exp)
            every_group(act, steps)
            copy_b(GROUPS - 1, QB - 1, HG - 1)
            save(GROUPS - 1, QB - 2)
            save(GROUPS - 1, QB - 1)


def k_slot(i, u):
    return (HG * i + u) % 8


def unit_before(g, i, u, do):
    if u:
        do(g, i, u - 1)
    elif i:
        do(g, i - 1, HG - 1)
    elif not (type(g) is int and g == 0):
        do(g - 1, QB - 1, HG - 1)


def after(engine, sem, count):
    if type(count) is not int:
        engine.wait_ge(sem, count)
    elif count > 0:
        engine.wait_ge(sem, count)


def attention_output(m):
    nc, t = m.nc, attention_tiles(m)
    names = ("turned", "rec", "normed", "turned_back", "biased", "wo_summed", "wo_biased", "x_added")
    z = semaphores(m.sem, "ao_", names)
    rec = m.arena[:, 0:2 * NH].rearrange("p (u h) -> p u h", u=2)
    on = m.arena[:, 64:64 + 4 * D].rearrange("p (u c) -> p u c", u=4)
    oC = m.arena[:, 1024:1024 + N]
    yC = m.arena[:, 1024 + N:1024 + N + 2 * SUP].rearrange("p (u c) -> p u c", u=2)
    raw_bank = lambda k: m.bank[0][:, (k % 2) * SUP:(k % 2 + 1) * SUP]
    half = lambda tile, s: tile[:, (s % 2) * SUP:(s % 2 + 1) * SUP]
    with nc.Block() as block:
        @block.tensor
        def _(pe):
            def turn(k):
                if k >= 2:
                    pe.wait_ge(z.normed, k - 1)
                b, i = divmod(k, QB)
                for hg in range(NG):
                    mm = nc.tensor.transpose(raw_bank(k)[:, hg * P:(hg + 1) * P], t.raw[:, (b * NG + hg) * QB + i, :],
                                             m.ident[:, :])
                mm.then_inc(z.turned, 1)

            def back(k):
                s, j = divmod(k, BLKS)
                pe.wait_ge(z.normed, k + 1)
                if j == 0 and s >= 2:
                    pe.wait_ge(z.biased, s - 1)
                mm = nc.tensor.transpose(half(m.bank[1], s)[:, j * P:(j + 1) * P], on[:, k % 4, :], m.ident[:, :])
                mm.then_inc(z.turned_back, 1)
                if j == BLKS - 1:
                    pe.wait_ge(z.biased, s + 1)
                    if s >= 2:
                        pe.wait_ge(z.wo_biased, s - 1)
                    nc.tensor.matmul(half(m.bank[2], s), m.a("wo"), oC[:, s * SUP:(s + 1) * SUP], start=True,
                                     stop=True).then_inc(z.wo_summed, 1)

            turn(0)
            for k in range(NBLK):
                if k + 1 < NBLK:
                    turn(k + 1)
                back(k)

        @block.vector
        def _(dve):
            for k in range(NBLK):
                raw = raw_bank(k).rearrange("p (h c) -> p h c", c=32)
                dve.wait_ge(z.turned, k + 1)
                nc.vector.reciprocal(rec[:, k % 2, :], raw[:, :, HD]).then_inc(z.rec, 1)
                dve.wait_ge(z.rec, k + 1)
                if k >= 4:
                    dve.wait_ge(z.turned_back, k - 3)
                nc.vector.tensor_tensor(on[:, k % 4, :].rearrange("p (h c) -> p h c", c=HD), raw[:, :, 0:HD],
                                        rec[:, k % 2, :].unsqueeze(2).broadcast_to([P, NH, HD]), ALU.mult).then_inc(z.normed, 1)
            for s in range(NSUP):
                xs = m.xC[:, s * SUP:(s + 1) * SUP]
                dve.wait_ge(z.wo_biased, s + 1)
                nc.vector.scalar_tensor_tensor(out=xs, in0=yC[:, s % 2, :], scalar=m.gated(0, 2, s), in1=xs,
                                               op0=ALU.mult, op1=ALU.add).then_inc(z.x_added, 1)

        @block.scalar
        def _(act):
            for s in range(NSUP):
                act.wait_ge(z.turned_back, BLKS * (s + 1))
                nc.scalar.activation(oC[:, s * SUP:(s + 1) * SUP], half(m.bank[1], s), ACT.Identity,
                                     bias=m.a("bv")).then_inc(z.biased, 1)
                act.wait_ge(z.wo_summed, s + 1)
                if s >= 2:
                    act.wait_ge(z.x_added, s - 1)
                nc.scalar.activation(yC[:, s % 2, :], half(m.bank[2], s), ACT.Identity,
                                     bias=m.a("bo")).then_inc(z.wo_biased, 1)



def take_first(m, step, chosen, score, highest, tmp):
    nc = m.nc
    order, pick = tmp[:, 0:NBLK * E].rearrange("p (k e) -> p k e", e=E), tmp[:, NBLK * E:NBLK * E + NBLK]
    over = lambda v: v.unsqueeze(2).broadcast_to([P, NBLK, E])
    step(nc.vector.tensor_tensor(order, score, over(highest), ALU.is_equal))
    step(nc.vector.tensor_tensor(order, order, m.countdown[:, :].unsqueeze(1).broadcast_to([P, NBLK, E]), ALU.mult))
    step(nc.vector.tensor_reduce(pick, order, AX.X, ALU.max))
    step(nc.vector.tensor_tensor(chosen, order, over(pick), ALU.is_equal))


def top_two(m, step, score, highest, tmp):
    nc = m.nc
    ke = lambda i: tmp[:, i * NBLK * E:(i + 1) * NBLK * E].rearrange("p (k e) -> p k e", e=E)
    first, second, rest = ke(0), ke(1), ke(2)
    low, work = tmp[:, 3 * NBLK * E:3 * NBLK * E + NBLK], tmp[:, 4 * NBLK * E:6 * NBLK * E]
    take_first(m, step, first, score, highest, work)
    step(nc.vector.scalar_tensor_tensor(out=rest, in0=first, scalar=NEG, in1=score, op0=ALU.mult, op1=ALU.add))
    step(nc.vector.tensor_reduce(low, rest, AX.X, ALU.max))
    take_first(m, step, second, rest, low, work)
    step(nc.vector.tensor_tensor(first, first, second, ALU.add))
    return first


def split_weights(m, step, rw, parts, rest):
    nc = m.nc
    step(nc.vector.tensor_copy(parts[:, :, 0, :], rw))
    step(nc.vector.tensor_tensor(rest, rw, parts[:, :, 0, :], ALU.subtract))
    step(nc.vector.tensor_copy(parts[:, :, 1, :], rest))
    nc.vector.tensor_tensor(parts[:, :, 2, :], rest, parts[:, :, 1, :], ALU.subtract).then_inc(m.gt.split, 1)


def turned_parts(m, s):
    return m.bank[s].bitcast(BF16)[0:NPART * E, 0:SUP]


def turn_weights(m, pe, parts, call):
    pe.wait_ge(m.gt.split, call + 1)
    for s in range(NSUP):
        for j in range(BLKS):
            mm = m.nc.tensor.transpose(turned_parts(m, s)[:, j * P:(j + 1) * P],
                                       parts[:, s * BLKS + j].rearrange("p a e -> p (a e)"), m.ident16[:, :])
        mm.then_inc(m.gt.splitT, 1)


def copy_weights(m, act, call, also=None):
    for s in range(NSUP):
        act.wait_ge(m.gt.splitT, call * NSUP + s + 1)
        m.nc.scalar.activation(m.rwT[:, s * SUP:(s + 1) * SUP], turned_parts(m, s), ACT.Copy)
        if also is not None:
            m.nc.scalar.activation(also[:, s * SUP:(s + 1) * SUP], turned_parts(m, s), ACT.Copy)


def gate_products(m, pe, nC, weights, sq, call):
    nc, g = m.nc, m.gt
    wide = m.bank[0][:, 0:SUP]
    for s in range(NSUP):
        mm = nc.tensor.matmul(wide[TILE * s:TILE * (s + 1), :], weights, nC[:, s * SUP:(s + 1) * SUP], start=True,
                              stop=sq is None)
    if sq is not None:
        for s in range(NSUP):
            pe.wait_ge(g.sq, call * NSUP + s + 1)
            mm = nc.tensor.matmul(wide[TILE * s:TILE * (s + 1), :], m.one_at_e[:, :], sq[:, s * SUP:(s + 1) * SUP],
                                  start=False, stop=True)
    mm.then_inc(g.logits, 1)
    pe.wait_ge(g.saved, call + 1)
    for j in range(BLKS):
        mm = nc.tensor.transpose(m.bank[1][:, j * P:(j + 1) * P], m.gate_rows[:, j * P:(j + 1) * P], m.ident[:, :])
    mm.then_inc(g.turned, 1)


def save_products(m, act, call):
    act.wait_ge(m.gt.logits, call + 1)
    m.nc.scalar.activation(m.gate_rows[:, :], m.bank[0][:, 0:SUP], ACT.Copy).then_inc(m.gt.saved, 1)


def by_token(m):
    return m.bank[1][:, 0:SUP].rearrange("p (j s c) -> p s j c", j=BLKS, s=NSUP)


def similarity_gating(m, nC, sim, gates, tmp):
    nc, g = m.nc, m.gt
    call = m.gt_calls
    m.gt_calls += 1
    at = 0

    def take(width):
        nonlocal at
        at += width
        return tmp[:, at - width:at]

    sq = take(N)
    m.gate_rows = take(SUP)
    simsq, simstd, simn = take(E), take(E), take(TILE)
    KE = NBLK * E
    std, lg, gated, mask, rw = take(NBLK), take(KE), take(KE), take(KE), take(KE)
    mx, top, put = take(NBLK), take(NBLK), take(NBLK)
    parts = take(NPART * KE // 2).bitcast(BF16).rearrange("p (k a e) -> p k a e", k=NBLK, a=NPART)
    rest = take(KE)
    top_tmp = take(6 * KE)
    ke = lambda v: v.rearrange("p (k e) -> p k e", e=E)
    sje = lambda v: v.rearrange("p (s j e) -> p s j e", s=NSUP, j=BLKS)
    over = lambda v: v.unsqueeze(2).broadcast_to([P, NBLK, E])
    simss = m.bank[2][:, 0:E]
    with nc.Block() as block:
        @block.scalar
        def _(act):
            for s in range(NSUP):
                nc.scalar.activation(sq[:, s * SUP:(s + 1) * SUP], nC[:, s * SUP:(s + 1) * SUP], ACT.Square).then_inc(g.sq, 1)
            act.wait_ge(g.simsq, 2 * call + 2)
            nc.scalar.activation(simstd, simss, ACT.Sqrt).then_inc(g.simstd, 1)
            save_products(m, act, call)
            act.wait_ge(g.turned, call + 1)
            nc.scalar.activation(std.rearrange("p (s j) -> p s j", j=BLKS), by_token(m)[:, :, :, E],
                                 ACT.Sqrt).then_inc(g.act_out, 1)
            nc.scalar.preload_act_table(ACT.Exp)
            act.wait_ge(g.act_in, call + 1)
            nc.scalar.activation(rw, gated, ACT.Exp).then_inc(g.act_out, 1)
            copy_weights(m, act, call)

        @block.tensor
        def _(pe):
            pe.wait_ge(g.simsq, 2 * call + 1)
            nc.tensor.matmul(simss, m.ones[:, :], simsq, start=True, stop=True).then_inc(g.simsq, 1)
            pe.wait_ge(g.sim, call + 1)
            gate_products(m, pe, nC, simn, sq, call)
            turn_weights(m, pe, parts, call)

        @block.vector
        def _(dve):
            step = m.dve.on(dve)
            nc.vector.memset(simn, 0.0)
            nc.vector.tensor_tensor(simsq, sim, sim, ALU.mult).then_inc(g.simsq, 1)
            dve.wait_ge(g.simstd, call + 1)
            step(nc.vector.tensor_scalar(simstd, simstd, 1e-12, None, ALU.max))
            step(nc.vector.reciprocal(simstd, simstd))
            nc.vector.tensor_tensor(simn[:, 0:E], sim, simstd, ALU.mult).then_inc(g.sim, 1)
            dve.wait_ge(g.act_out, 2 * call + 1)
            step(nc.vector.tensor_scalar(std, std, 1e-12, None, ALU.max))
            step(nc.vector.reciprocal(std, std))
            rstd = std.rearrange("p (s j) -> p s j", j=BLKS).unsqueeze(3).broadcast_to([P, NSUP, BLKS, E])
            step(nc.vector.tensor_tensor(sje(lg), by_token(m)[:, :, :, 0:E], rstd, ALU.mult))
            step(nc.vector.tensor_tensor(ke(lg), ke(lg), gates.unsqueeze(1).broadcast_to([P, NBLK, E]), ALU.subtract))
            step(nc.vector.tensor_reduce(mx, ke(lg), AX.X, ALU.max))
            step(nc.vector.tensor_scalar(gated, lg, 0.0, None, ALU.max))
            step(nc.vector.tensor_scalar(top, mx, 0.0, None, ALU.max))
            nc.vector.tensor_tensor(ke(gated), ke(gated), over(top), ALU.subtract).then_inc(g.act_in, 1)
            chosen = top_two(m, step, ke(lg), mx, top_tmp)
            step(nc.vector.tensor_scalar(mask, lg, 0.0, None, ALU.is_gt))
            step(nc.vector.tensor_scalar(put, mx, 0.0, None, ALU.is_le))
            step(nc.vector.tensor_tensor(chosen, chosen, over(put), ALU.mult))
            step(nc.vector.tensor_tensor(ke(mask), ke(mask), chosen, ALU.max))
            dve.wait_ge(g.act_out, 2 * call + 2)
            step(nc.vector.tensor_tensor(rw, rw, mask, ALU.mult))
            step(nc.vector.tensor_reduce(mx, ke(rw), AX.X, ALU.add))
            step(nc.vector.reciprocal(mx, mx))
            step(nc.vector.tensor_tensor(ke(rw), ke(rw), over(mx), ALU.mult))
            split_weights(m, step, ke(rw), parts, ke(rest))



def feed_forward(m):
    ar = m.arena
    at = 0

    def take(width):
        nonlocal at
        at += width
        return ar[:, at - width:at]

    m.nC, m.hC, m.qT, m.kT, m.vS, m.aC = (take(N) for _ in range(6))
    tmp = ar[:, at:ar.shape[1]]
    sup = lambda tile: (lambda s: tile[:, s * SUP:(s + 1) * SUP])
    layer_norm(m, m.xC, sup(m.hC), lambda s: m.scale1(0, 4, s), lambda s: m.shift(0, 3, s), tmp=at)
    load_layer1(m)
    layer_norm(m, m.hC, sup(m.nC), lambda s: m.a("ln1w"), lambda s: m.a("ln1b"), tmp=at)
    similarity_gating(m, m.nC, m.a("smha_sim"), m.rowg[:, 0:E], tmp)
    routed_projections(m, tmp)
    causal_attention(m, tmp)
    routed_output(m, tmp)
    layer_norm(m, m.hC, sup(m.nC), lambda s: m.a("ln2w"), lambda s: m.a("ln2b"), tmp=at)
    similarity_gating(m, m.nC, m.a("moe_sim"), m.rowg[:, E:2 * E], tmp)
    routed_mlp(m, tmp)


def load_layer1(m):
    with m.nc.Block() as block:
        @block.sync
        def _(sp):
            sp.dma_start(m.late[:, :], m.l1_in).then_inc(m.l1_loaded, 16)
            sp.wait_ge(m.ffn_loaded, 16)


def spread(m, out, e, s):
    return m.nc.tensor.matmul(out, m.sel_e[:, e, :], m.rwT[:, bass.ds(s * SUP, SUP)], start=True, stop=True)


def routed_projections(m, tmp):
    nc = m.nc
    names = ("spread", "scaled", "used", "q_done", "k_done", "v_done", "q_free", "k_free", "v_free")
    z = semaphores(m.sem, "rp_", names)
    XB = 4
    xe = tmp[:, 0:XB * SUP].rearrange("p (u c) -> p u c", u=XB)
    wB = [m.bank[0][:, 0:SUP], m.bank[0][:, SUP:2 * SUP]]
    acc = lambda i, par: m.bank[1 + i][:, par * SUP:(par + 1) * SUP]
    PAIRS = NSUP // 2
    with nc.Block() as block:
        @block.tensor
        def _(pe):
            prime(pe, z.used)
            with pe.Fori(0, PAIRS) as p2:
                for par in range(2):
                    s = 2 * p2 + par
                    pe.wait_ge(z.scaled, PRIMED + E * s)
                    apart(pe)
                    spread(m, wB[0], 0, s).then_inc(z.spread, 1)
                    for e in range(E):
                        if e + 1 < E:
                            if e >= 1:
                                pe.wait_ge(z.scaled, PRIMED + E * s + e)
                                apart(pe)
                            spread(m, wB[(e + 1) % 2], e + 1, s).then_inc(z.spread, 1)
                        x = xe[:, e % XB, :]
                        pe.wait_ge(z.scaled, PRIMED + E * s + e + 1)
                        if e == 0:
                            pe.wait_ge(z.q_free, PRIMED + 2 * p2)
                            pe.wait_ge(z.k_free, PRIMED + 2 * p2)
                            pe.wait_ge(z.v_free, PRIMED + 2 * p2)
                        ws = slice(e * D, (e + 1) * D)
                        q = nc.tensor.matmul(acc(0, par), m.f("qp")[:, ws], x, start=(e == 0), stop=(e == E - 1))
                        k = nc.tensor.matmul(acc(1, par), m.f("kp")[:, ws], x, start=(e == 0), stop=(e == E - 1))
                        for j in range(BLKS):
                            v = nc.tensor.matmul(acc(2, par)[:, j * P:(j + 1) * P], x[:, j * P:(j + 1) * P],
                                                 m.f("vp")[:, ws], start=(e == 0 and j == 0), stop=(e == E - 1),
                                                 skip_group_check=True)
                        v.then_inc(z.used, 1)
                        if e == E - 1:
                            q.then_inc(z.q_done, 1)
                            k.then_inc(z.k_done, 1)

        @block.vector
        def _(dve):
            prime(dve, z.scaled, z.v_free)
            with dve.Fori(0, PAIRS) as p2:
                for par in range(2):
                    s = 2 * p2 + par
                    for e in range(E):
                        if e >= XB:
                            dve.wait_ge(z.used, PRIMED + E * s + e - XB + 1)
                        else:
                            dve.wait_ge(z.used, PRIMED + E * s)
                        dve.wait_ge(z.spread, E * s + e + 1)
                        apart(dve)
                        nc.vector.tensor_tensor(xe[:, e % XB, :], m.nC[:, bass.ds(s * SUP, SUP)], wB[e % 2],
                                                ALU.mult).then_inc(z.scaled, 1)
                    dve.wait_ge(z.used, PRIMED + E * (s + 1))
                    apart(dve)
                    nc.vector.tensor_copy(m.vS[:, bass.ds(s * SUP, SUP)], acc(2, par)).then_inc(z.v_free, 1)

        @block.scalar
        def _(act):
            prime(act, z.q_free, z.k_free)
            with act.Fori(0, PAIRS) as p2:
                for par in range(2):
                    s = 2 * p2 + par
                    act.wait_ge(z.q_done, s + 1)
                    apart(act)
                    nc.scalar.activation(m.qT[:, bass.ds(s * SUP, SUP)], acc(0, par), ACT.Copy).then_inc(z.q_free, 1)
                    act.wait_ge(z.k_done, s + 1)
                    apart(act)
                    nc.scalar.activation(m.kT[:, bass.ds(s * SUP, SUP)], acc(1, par), ACT.Copy).then_inc(z.k_free, 1)


def causal_attention(m, tmp):
    nc = m.nc
    names = ("scored", "maxed", "negmax", "exped", "normed", "turned", "copied", "summed", "saved", "masked")
    z = semaphores(m.sem, "ca_", names)
    p = tmp[:, 0:2 * T].rearrange("p (u k) -> p u k", u=2)
    pT = tmp[:, 2 * T:4 * T].rearrange("p (u k) -> p u k", u=2)
    col = tmp[:, 4 * T:4 * T + 8]
    mx, nm, l, rl = (col[:, 2 * i:2 * i + 2] for i in range(4))
    scale = float(D) ** -0.5
    score = lambda n: m.bank[n % 2]
    turn = m.bank[2]
    out = lambda n: m.bank[3][:, (n % 2) * SUP:(n % 2) * SUP + P]
    halves_of = lambda w: [(a, min(a + SUP, w)) for a in range(0, w, SUP)]
    copies = [0]
    for n in range(NBLK):
        copies.append(copies[-1] + len(halves_of((n % QB + 1) * P)))
    with nc.Block() as block:
        @block.tensor
        def _(pe):
            def scores(n):
                b, i = divmod(n, QB)
                if n >= 2:
                    pe.wait_ge(z.exped, n - 1)
                for a, c in halves_of((i + 1) * P):
                    mm = nc.tensor.matmul(score(n)[:, a:c], m.qT[:, n * P:(n + 1) * P], m.kT[:, b * T + a:b * T + c],
                                          start=True, stop=True)
                mm.then_inc(z.scored, 1)

            def turns(n):
                b, i = divmod(n, QB)
                pe.wait_ge(z.normed, n + 1)
                for h, (a, c) in enumerate(halves_of((i + 1) * P)):
                    if n:
                        last = copies[n] if h == 0 or copies[n] - copies[n - 1] == 2 else copies[n]
                        pe.wait_ge(z.copied, last)
                    for k in range(a, c, P):
                        mm = nc.tensor.transpose(turn[:, k:k + P], p[:, n % 2, k:k + P], m.ident[:, :])
                    mm.then_inc(z.turned, 1)

            def values(n):
                b, i = divmod(n, QB)
                pe.wait_ge(z.copied, copies[n + 1])
                if n >= 2:
                    pe.wait_ge(z.saved, n - 1)
                for kb in range(i + 1):
                    mm = nc.tensor.matmul(out(n), m.vS[:, (b * QB + kb) * P:(b * QB + kb + 1) * P],
                                          pT[:, n % 2, kb * P:(kb + 1) * P], start=(kb == 0), stop=(kb == i))
                mm.then_inc(z.summed, 1)

            scores(0)
            for n in range(NBLK):
                if n + 1 < NBLK:
                    scores(n + 1)
                turns(n)
                if n:
                    values(n - 1)
            values(NBLK - 1)

        @block.vector
        def _(dve):
            def top(n):
                i = n % QB
                w = (i + 1) * P
                dve.wait_ge(z.scored, n + 1)
                nc.vector.tensor_tensor(score(n)[:, i * P:w], score(n)[:, i * P:w], m.causal[:, :],
                                        ALU.add).then_inc(z.masked, 1)
                dve.wait_ge(z.masked, n + 1)
                nc.vector.tensor_reduce(mx[:, n % 2:n % 2 + 1], score(n)[:, 0:w], AX.X, ALU.max).then_inc(z.maxed, 1)
                dve.wait_ge(z.maxed, n + 1)
                nc.vector.tensor_scalar(nm[:, n % 2:n % 2 + 1], mx[:, n % 2:n % 2 + 1], -scale, None,
                                        ALU.mult).then_inc(z.negmax, 1)

            step = m.dve.on(dve)
            top(0)
            for n in range(NBLK):
                w = (n % QB + 1) * P
                if n + 1 < NBLK:
                    top(n + 1)
                dve.wait_ge(z.exped, n + 1)
                step(nc.vector.reciprocal(rl[:, n % 2:n % 2 + 1], l[:, n % 2:n % 2 + 1]))
                nc.vector.tensor_scalar(p[:, n % 2, 0:w], p[:, n % 2, 0:w], rl[:, n % 2:n % 2 + 1], None,
                                        ALU.mult).then_inc(z.normed, 1)

        @block.scalar
        def _(act):
            def exps(n):
                w = (n % QB + 1) * P
                act.wait_ge(z.negmax, n + 1)
                if n >= 2:
                    act.wait_ge(z.turned, copies[n - 1])
                nc.scalar.activation(p[:, n % 2, 0:w], score(n)[:, 0:w], ACT.Exp, bias=nm[:, n % 2:n % 2 + 1],
                                     scale=scale, accum_out=l[:, n % 2:n % 2 + 1]).then_inc(z.exped, 1)

            def copy(n):
                if n >= 2:
                    act.wait_ge(z.summed, n - 1)
                for h, (a, c) in enumerate(halves_of((n % QB + 1) * P)):
                    act.wait_ge(z.turned, copies[n] + h + 1)
                    nc.scalar.activation(pT[:, n % 2, a:c], turn[:, a:c], ACT.Copy).then_inc(z.copied, 1)

            def save(n):
                act.wait_ge(z.summed, n + 1)
                nc.scalar.activation(m.aC[:, n * P:(n + 1) * P], out(n), ACT.Copy).then_inc(z.saved, 1)

            exps(0)
            for n in range(NBLK):
                if n + 1 < NBLK:
                    exps(n + 1)
                copy(n)
                if n:
                    save(n - 1)
            save(NBLK - 1)


def routed_output(m, tmp):
    nc = m.nc
    names = ("spread", "scaled", "used", "added")
    z = semaphores(m.sem, "ro_", names)
    XB = 4
    xe = tmp[:, 0:XB * SUP].rearrange("p (u c) -> p u c", u=XB)
    wB = [m.bank[0][:, 0:SUP], m.bank[0][:, SUP:2 * SUP]]
    acc = lambda par: m.bank[1][:, par * SUP:(par + 1) * SUP]
    PAIRS = NSUP // 2
    with nc.Block() as block:
        @block.tensor
        def _(pe):
            prime(pe, z.used)
            with pe.Fori(0, PAIRS) as p2:
                for par in range(2):
                    s = 2 * p2 + par
                    pe.wait_ge(z.scaled, PRIMED + E * s)
                    apart(pe)
                    spread(m, wB[0], 0, s).then_inc(z.spread, 1)
                    for e in range(E):
                        if e + 1 < E:
                            if e >= 1:
                                pe.wait_ge(z.scaled, PRIMED + E * s + e)
                                apart(pe)
                            spread(m, wB[(e + 1) % 2], e + 1, s).then_inc(z.spread, 1)
                        pe.wait_ge(z.scaled, PRIMED + E * s + e + 1)
                        if e == 0:
                            pe.wait_ge(z.added, PRIMED + 2 * p2)
                        nc.tensor.matmul(acc(par), m.f("op")[:, e * D:(e + 1) * D], xe[:, e % XB, :], start=(e == 0),
                                         stop=(e == E - 1)).then_inc(z.used, 1)

        @block.vector
        def _(dve):
            prime(dve, z.scaled, z.added)
            with dve.Fori(0, PAIRS) as p2:
                for par in range(2):
                    s = 2 * p2 + par
                    for e in range(E):
                        dve.wait_ge(z.used, PRIMED + E * s + max(0, e - XB + 1))
                        dve.wait_ge(z.spread, E * s + e + 1)
                        apart(dve)
                        nc.vector.tensor_tensor(xe[:, e % XB, :], m.aC[:, bass.ds(s * SUP, SUP)], wB[e % 2],
                                                ALU.mult).then_inc(z.scaled, 1)
                    dve.wait_ge(z.used, PRIMED + E * (s + 1))
                    apart(dve)
                    h = m.hC[:, bass.ds(s * SUP, SUP)]
                    nc.vector.tensor_tensor(h, h, acc(par), ALU.add).then_inc(z.added, 1)


def routed_mlp(m, tmp):
    nc = m.nc
    names = ("up", "gelu", "spread", "scaled", "used", "summed", "added")
    z = semaphores(m.sem, "rm_", names)
    XB = 4
    ge = tmp[:, 0:XB * SUP].rearrange("p (u c) -> p u c", u=XB)
    ie = tmp[:, XB * SUP:2 * XB * SUP].rearrange("p (u c) -> p u c", u=XB)
    yh = tmp[:, 2 * XB * SUP:2 * XB * SUP + 2 * SUP].rearrange("p (u c) -> p u c", u=2)
    wB = [m.bank[0][:, 0:SUP], m.bank[0][:, SUP:2 * SUP]]
    up = [m.bank[2][:, 0:SUP], m.bank[2][:, SUP:2 * SUP]]
    acc = lambda par: m.bank[1][:, par * SUP:(par + 1) * SUP]
    PAIRS = NSUP // 2
    with nc.Block() as block:
        @block.tensor
        def _(pe):
            prime(pe, z.used)
            with pe.Fori(0, PAIRS) as p2:
                for par in range(2):
                    s = 2 * p2 + par

                    def rise(e):
                        pe.wait_ge(z.scaled, PRIMED + E * s + max(0, e - 1))
                        pe.wait_ge(z.gelu, PRIMED + E * s + max(0, e - 1))
                        apart(pe)
                        spread(m, wB[e % 2], e, s).then_inc(z.spread, 1)
                        nc.tensor.matmul(up[e % 2], m.f("w1")[:, e * D:(e + 1) * D], m.nC[:, bass.ds(s * SUP, SUP)],
                                         start=True, stop=True).then_inc(z.up, 1)

                    rise(0)
                    rise(1)
                    for e in range(E):
                        pe.wait_ge(z.scaled, PRIMED + E * s + e + 1)
                        if e == 0:
                            pe.wait_ge(z.added, PRIMED + 2 * p2)
                        nc.tensor.matmul(acc(par), m.f("w2")[:, e * D:(e + 1) * D], ie[:, e % XB, :], start=(e == 0),
                                         stop=(e == E - 1)).then_inc(z.used, 1)
                        if e + 2 < E:
                            rise(e + 2)

        @block.scalar
        def _(act):
            prime(act, z.gelu)
            nc.scalar.preload_act_table(ACT.Gelu)
            with act.Fori(0, PAIRS) as p2:
                for par in range(2):
                    s = 2 * p2 + par
                    for e in range(E):
                        act.wait_ge(z.scaled, PRIMED + E * s + max(0, e - XB + 1))
                        act.wait_ge(z.up, E * s + e + 1)
                        nc.scalar.activation(ge[:, e % XB, :], up[e % 2], ACT.Gelu).then_inc(z.gelu, 1)

        @block.vector
        def _(dve):
            prime(dve, z.scaled, z.added)
            with dve.Fori(0, PAIRS) as p2:
                for par in range(2):
                    s = 2 * p2 + par
                    for e in range(E):
                        dve.wait_ge(z.used, PRIMED + E * s + max(0, e - XB + 1))
                        dve.wait_ge(z.spread, E * s + e + 1)
                        dve.wait_ge(z.gelu, PRIMED + E * s + e + 1)
                        nc.vector.tensor_tensor(ie[:, e % XB, :], ge[:, e % XB, :], wB[e % 2],
                                                ALU.mult).then_inc(z.scaled, 1)
                    dve.wait_ge(z.used, PRIMED + E * (s + 1))
                    apart(dve)
                    nc.vector.tensor_tensor(yh[:, par, :], acc(par), m.hC[:, bass.ds(s * SUP, SUP)],
                                            ALU.add).then_inc(z.summed, 1)
                    dve.wait_ge(z.summed, s + 1)
                    apart(dve)
                    x = m.xC[:, bass.ds(s * SUP, SUP)]
                    nc.vector.scalar_tensor_tensor(out=x, in0=yh[:, par, :], scalar=m.gate[:, bass.ds(5 * B + p2, 1)], in1=x,
                                                   op0=ALU.mult, op1=ALU.add).then_inc(z.added, 1)



def mixer(m):
    nc, ar, fr = m.nc, m.arena, m.ffn
    PAD = 4
    W = PAD + T
    at = 0

    def take(width):
        nonlocal at
        at += width
        return ar[:, at - width:at]

    halves = lambda v: v.rearrange("p (h t) -> p h t", h=HALVES)
    t = Shared()
    t.W, t.PAD = W, PAD
    t.hP = take(B * W).rearrange("p (b t) -> p b t", b=B)
    t.xs, t.sz, t.dt, t.u = (halves(take(HALVES * N)) for _ in range(4))
    t.dA = take(HALVES * T).rearrange("p (h t) -> p h t", h=HALVES)
    t.g = take(2 * HALVES * T).rearrange("p (u h t) -> p u h t", u=2, h=HALVES)
    t.scratch = ar[:, at - 6 * T:at]
    t.A, t.wrep, t.diag = take(HALVES * DS), take(HALVES * P), take(HALVES * P)
    assert at <= ar.shape[1], at
    t.sel = m.sel_n
    t.stack = fr[0:NPART * 2 * DS, 2048:2048 + N // 2].bitcast(BF16)
    t.Cs = fr[:, 3072:3072 + 2 * T].rearrange("p (u t) -> p u t", u=2)
    t.wtap = t.scratch[:, 0:KC * DI].rearrange("p (k d) -> p k d", k=KC)
    t.tmp = 2 * N

    mixer_constants(m, t)
    layer_norm(m, m.xC, lambda s: t.hP[:, s // SUPB, PAD + (s % SUPB) * SUP:PAD + (s % SUPB + 1) * SUP],
               lambda s: m.scale1(1, 1, s), lambda s: m.shift(1, 0, s), tmp=t.tmp + 4096)
    mixer_input(m, t)
    mixer_steps(m, t)
    selective_scan(m, t)
    mixer_output(m, t)


def mixer_constants(m, t):
    nc = m.nc
    exped = m.sem("a_exped")
    with nc.Block() as block:
        @block.gpsimd
        def _(pool):
            nc.gpsimd.memset(t.hP[:, :, 0:t.PAD], 0.0)

        @block.scalar
        def _(act):
            act.wait_ge(m.l1_loaded, 16)
            nc.scalar.activation(t.A, m.l("a_log"), ACT.Exp).then_inc(exped, 1)

        @block.vector
        def _(dve):
            dve.wait_ge(m.l1_loaded, 16)
            for k in range(KC):
                nc.vector.tensor_tensor(t.wtap[:, k, :], m.l("w_in")[:, 0:DI], m.r("w_conv")[:, k * DI:(k + 1) * DI],
                                        ALU.mult)
            for h in range(HALVES):
                nc.vector.tensor_copy(t.wrep[:, h * P:(h + 1) * P],
                                      m.l("w_x")[:, h * (2 * DS + 1):h * (2 * DS + 1) + 1].broadcast_to([P, P]))
                nc.vector.tensor_scalar(t.diag[:, h * P:(h + 1) * P], m.ident[:, :], m.l("dskip")[:, h:h + 1], None,
                                        ALU.mult)
            dve.wait_ge(exped, 1)
            nc.vector.tensor_scalar(t.A, t.A, -1.0, None, ALU.mult)


def mixer_input(m, t):
    nc = m.nc
    z = semaphores(m.sem, "mi_", ("x_done", "z_done", "freed"))
    ps = lambda i, par: m.bank[i][:, par * SUP:(par + 1) * SUP]
    with nc.Block() as block:
        @block.tensor
        def _(pe):
            with pe.Fori(0, B) as b:
                for par in range(SUPB):
                    pe.wait_ge(z.freed, PRIMED + 4 * b)
                    pe.wait_ge(z.freed, PRIMED + 8 * b)
                    for h in range(HALVES):
                        for k in range(KC):
                            at = t.PAD - (KC - 1) + k + par * SUP
                            mm = nc.tensor.matmul(ps(h, par), t.wtap[:, k, h * P:(h + 1) * P], t.hP[:, b, at:at + SUP],
                                                  start=(k == 0), stop=(k == KC - 1))
                        mm.then_inc(z.x_done, 1)
                    for h in range(HALVES):
                        at = t.PAD + par * SUP
                        nc.tensor.matmul(ps(2 + h, par), m.l("w_in")[:, DI + h * P:DI + (h + 1) * P], t.hP[:, b, at:at + SUP],
                                         start=True, stop=True).then_inc(z.z_done, 1)

        @block.scalar
        def _(act):
            prime(act, z.freed)
            nc.scalar.preload_act_table(ACT.Silu)
            with act.Fori(0, B) as b:
                for par in range(SUPB):
                    s = b * SUPB + par
                    for h in range(HALVES):
                        act.wait_ge(z.x_done, HALVES * s + h + 1)
                        apart(act)
                        nc.scalar.activation(t.xs[:, h, bass.ds(s * SUP, SUP)], ps(h, par), ACT.Silu,
                                             bias=m.l("b_conv")[:, h:h + 1]).then_inc(z.freed, 1)
                    for h in range(HALVES):
                        act.wait_ge(z.z_done, HALVES * s + h + 1)
                        apart(act)
                        nc.scalar.activation(t.sz[:, h, bass.ds(s * SUP, SUP)], ps(2 + h, par),
                                             ACT.Silu).then_inc(z.freed, 1)


def mixer_steps(m, t):
    nc = m.nc
    names = ("dt_raw", "affine", "abs", "logged", "bc_done", "first", "rest", "second", "third", "dt_free")
    z = semaphores(m.sem, "ms_", names)
    ps = lambda i, par: m.bank[i][:, par * SUP:(par + 1) * SUP]
    v = t.scratch[:, 0:HALVES * SUP * 2].rearrange("p (u h c) -> p u h c", u=2, h=HALVES)
    low = t.scratch[0:2 * DS, 2048:2048 + 2048]
    rest, part2, part3 = low[:, 0:SUP], low[:, SUP:SUP + SUP // 2].bitcast(BF16), low[:, 2 * SUP:2 * SUP + SUP // 2].bitcast(BF16)
    R = 2 * DS
    sup = lambda tile, s: tile[:, s * SUP:(s + 1) * SUP]
    with nc.Block() as block:
        @block.tensor
        def _(pe):
            for s in range(NSUP):
                par = s % 2
                if s >= 2:
                    pe.wait_ge(z.affine, s - 1)
                    pe.wait_ge(z.rest, s - 1)
                for h in range(HALVES):
                    mm = nc.tensor.matmul(ps(0, par), t.wrep[:, h * P:(h + 1) * P], sup(t.xs[:, h], s), start=(h == 0),
                                          stop=(h == HALVES - 1))
                mm.then_inc(z.dt_raw, 1)
                for h in range(HALVES):
                    c = h * (R + 1) + 1
                    mm = nc.tensor.matmul(ps(1, par)[0:R, :], m.l("w_x")[:, c:c + R], sup(t.xs[:, h], s), start=(h == 0),
                                          stop=(h == HALVES - 1))
                mm.then_inc(z.bc_done, 1)

        @block.vector
        def _(dve):
            for s in range(NSUP):
                par = s % 2
                dve.wait_ge(z.dt_raw, s + 1)
                for h in range(HALVES):
                    ins = nc.vector.tensor_scalar(sup(t.dt[:, h], s), ps(0, par), m.l("w_dt")[:, h:h + 1],
                                                  m.l("b_dt")[:, h:h + 1], ALU.mult, ALU.add)
                ins.then_inc(z.affine, 1)
                dve.wait_ge(z.bc_done, s + 1)
                if s:
                    dve.wait_ge(z.third, 2 * s)
                nc.vector.tensor_copy(sup(t.stack[0:R], s), ps(1, par)[0:R, :]).then_inc(z.first, 1)
                dve.wait_ge(z.first, s + 1)
                nc.vector.tensor_tensor(rest, ps(1, par)[0:R, :], sup(t.stack[0:R], s), ALU.subtract).then_inc(z.rest, 1)
                dve.wait_ge(z.rest, s + 1)
                nc.vector.tensor_copy(part2, rest).then_inc(z.second, 1)
                dve.wait_ge(z.second, 2 * s + 1)
                nc.vector.tensor_tensor(part3, rest, part2, ALU.subtract).then_inc(z.second, 1)
                dve.wait_ge(z.logged, s + 1)
                d = t.dt[:, :, s * SUP:(s + 1) * SUP]
                nc.vector.scalar_tensor_tensor(out=d, in0=d, scalar=0.0, in1=v[:, par], op0=ALU.max,
                                               op1=ALU.add).then_inc(z.dt_free, 1)
                dve.wait_ge(z.dt_free, s + 1)
                nc.vector.tensor_tensor(t.u[:, :, s * SUP:(s + 1) * SUP], d, t.xs[:, :, s * SUP:(s + 1) * SUP], ALU.mult)

        @block.scalar
        def _(act):
            nc.scalar.preload_act_table_set("natural_log_exp_and_others")
            for s in range(NSUP):
                par = s % 2
                d = t.dt[:, :, s * SUP:(s + 1) * SUP]
                step = m.act.on(act)
                act.wait_ge(z.affine, s + 1)
                if s >= 2:
                    act.wait_ge(z.dt_free, s - 1)
                step(nc.scalar.activation(v[:, par], d, ACT.Abs))
                step(nc.scalar.activation(v[:, par], v[:, par], ACT.Exp, scale=-1.0))
                nc.scalar.activation(v[:, par], v[:, par], ACT.Ln, bias=m.ones[:, 0:1]).then_inc(z.logged, 1)
                act.wait_ge(z.second, 2 * s + 2)
                nc.scalar.activation(sup(t.stack[R:2 * R], s), part2, ACT.Copy).then_inc(z.third, 1)
                nc.scalar.activation(sup(t.stack[2 * R:3 * R], s), part3, ACT.Copy).then_inc(z.third, 1)


def selective_scan(m, t):
    nc = m.nc
    names = ("b_spread", "c_spread", "b_used", "c_saved", "decayed", "scanned", "weighted", "y_added", "driven",
             "y_gated")
    z = semaphores(m.sem, "ss_", names)
    psB, psC = m.bank[0], m.bank[1]
    y = [m.bank[2], m.bank[3]]
    PAIRS = DS // 2
    halves_of = [(h, h * SUP, (h + 1) * SUP) for h in range(SUPB)]
    AHEAD = 4
    with nc.Block() as block:
        @block.tensor
        def _(pe):
            for b in range(B):
                def spread_b(b, n):
                    k = b * DS + n
                    pe.wait_ge(z.b_used, AHEAD + 2 * k)
                    apart(pe)
                    for _, a, c in halves_of:
                        mm = nc.tensor.matmul(psB[:, a:c], t.sel[:, n, :], t.stack[:, b * T + a:b * T + c], start=True, stop=True)
                    mm.then_inc(z.b_spread, 1)

                def spread_c(b, n):
                    k = b * DS + n
                    pe.wait_ge(z.c_saved, AHEAD + k)
                    apart(pe)
                    for _, a, c in halves_of:
                        mm = nc.tensor.matmul(psC[:, a:c], t.sel[:, n + DS, :], t.stack[:, b * T + a:b * T + c], start=True,
                                              stop=True)
                    mm.then_inc(z.c_spread, 1)

                def add_y(n, par, h, last=False):
                    pe.wait_ge(z.weighted, AHEAD + 2 * (b * DS + n) + h + 1)
                    for _, a, c in halves_of:
                        mm = nc.tensor.matmul(y[h][:, a:c], m.ident[:, :], t.g[:, par, h, a:c], start=False, stop=last)
                    mm.then_inc(z.y_added, 1)

                if b:
                    pe.wait_ge(z.y_gated, HALVES * b)
                else:
                    for n in range(2):
                        spread_b(b, n)
                        spread_c(b, n)
                for h in range(HALVES):
                    for _, a, c in halves_of:
                        nc.tensor.matmul(y[h][:, a:c], t.diag[:, h * P:(h + 1) * P], t.xs[:, h, b * T + a:b * T + c],
                                         start=True, stop=False)
                with pe.Fori(0, PAIRS - 1) as mm_:
                    for par in range(2):
                        n = 2 * mm_ + par
                        add_y(n, par, 0)
                        spread_b(b, n + 2)
                        spread_c(b, n + 2)
                        add_y(n, par, 1)
                for par in range(2):
                    last = par == 1
                    add_y(DS - 2 + par, par, 0, last)
                    if b + 1 < B:
                        spread_b(b + 1, par)
                        spread_c(b + 1, par)
                    add_y(DS - 2 + par, par, 1, last)

        @block.scalar
        def _(act):
            prime(act, z.c_saved, count=AHEAD)
            nc.scalar.preload_act_table(ACT.Exp)
            for b in range(B):
                with act.Fori(0, PAIRS) as mm_:
                    for par in range(2):
                        n = 2 * mm_ + par
                        k = b * DS + n
                        for h in range(HALVES):
                            act.wait_ge(z.scanned, AHEAD + 2 * k - 1 + h)
                            apart(act)
                            nc.scalar.activation(t.dA[:, h, :], t.dt[:, h, b * T:(b + 1) * T], ACT.Exp,
                                                 scale=t.A[:, bass.ds(h * DS + n, 1)]).then_inc(z.decayed, 1)
                            if h == 0:
                                act.wait_ge(z.c_spread, k + 1)
                                act.wait_ge(z.weighted, AHEAD + 2 * k - 2)
                                nc.scalar.activation(t.Cs[:, par, :], psC[:, :], ACT.Copy).then_inc(z.c_saved, 1)

        @block.vector
        def _(dve):
            prime(dve, z.b_used, z.scanned, count=AHEAD)

            def state(b, n, par):
                k = b * DS + n
                for h in range(HALVES):
                    dve.wait_ge(z.y_added, AHEAD + 2 * k + h - 3)
                    dve.wait_ge(z.b_spread, k + 1)
                    nc.vector.tensor_tensor(t.g[:, par, h, :], psB[:, :], t.u[:, h, b * T:(b + 1) * T],
                                            ALU.mult).then_inc(z.b_used, 1)
                for h in range(HALVES):
                    g = t.g[:, par, h, :]
                    dve.wait_ge(z.b_used, AHEAD + 2 * k + h + 1)
                    dve.wait_ge(z.decayed, 2 * k + h + 1)
                    nc.vector.tensor_tensor_scan(g, t.dA[:, h, :], g, 0.0, ALU.mult, ALU.add).then_inc(z.scanned, 1)

            def gate_y(b):
                for h in range(HALVES):
                    szb = t.sz[:, h, b * T:(b + 1) * T]
                    dve.wait_ge(z.y_added, AHEAD + HALVES * DS * (b + 1))
                    nc.vector.tensor_tensor(szb, y[h][:, :], szb, ALU.mult).then_inc(z.y_gated, 1)

            for b in range(B):
                if b:
                    state(b, 0, 0)
                    gate_y(b - 1)
                    state(b, 1, 1)
                with dve.Fori(1 if b else 0, PAIRS) as mm_:
                    for par in range(2):
                        state(b, 2 * mm_ + par, par)
            gate_y(B - 1)

        @block.gpsimd
        def _(pool):
            prime(pool, z.weighted, z.y_added, count=AHEAD)
            for b in range(B):
                with pool.Fori(0, PAIRS) as mm_:
                    for par in range(2):
                        k = b * DS + 2 * mm_ + par
                        for h in range(HALVES):
                            g = t.g[:, par, h, :]
                            pool.wait_ge(z.c_saved, AHEAD + k + 1)
                            pool.wait_ge(z.scanned, AHEAD + 2 * k + h + 1)
                            nc.gpsimd.tensor_tensor(g, g, t.Cs[:, par, :], ALU.mult).then_inc(z.weighted, 1)


def mixer_output(m, t):
    nc = m.nc
    z = semaphores(m.sem, "mo_", ("summed", "added"))
    with nc.Block() as block:
        @block.tensor
        def _(pe):
            for s in range(NSUP):
                for h in range(HALVES):
                    mm = nc.tensor.matmul(m.bank[s][:, 0:SUP], m.l("w_out")[:, h * D:(h + 1) * D],
                                          t.sz[:, h, s * SUP:(s + 1) * SUP], start=(h == 0), stop=(h == HALVES - 1))
                mm.then_inc(z.summed, 1)

        @block.vector
        def _(dve):
            for s in range(NSUP):
                x = m.xC[:, s * SUP:(s + 1) * SUP]
                dve.wait_ge(z.summed, s + 1)
                nc.vector.scalar_tensor_tensor(out=x, in0=m.bank[s][:, 0:SUP], scalar=m.gated(1, 2, s), in1=x,
                                               op0=ALU.mult, op1=ALU.add).then_inc(z.added, 1)



def experts(m):
    ar = m.arena
    m.hC = ar[:, 0:N]
    layer_norm(m, m.xC, lambda s: m.hC[:, s * SUP:(s + 1) * SUP], lambda s: m.scale1(1, 4, s), lambda s: m.shift(1, 3, s),
               tmp=N)
    top_two_gating(m, ar[:, N:ar.shape[1]])
    expert_sums(m, ar[:, N:ar.shape[1]])


def top_two_gating(m, tmp):
    nc, g = m.nc, m.gt
    call = m.gt_calls
    m.gt_calls += 1
    m.rwTf = m.ffn[0:NPART * E, 0:N]
    KE = NBLK * E
    at = 0

    def take(width):
        nonlocal at
        at += width
        return tmp[:, at - width:at]

    m.gate_rows = take(SUP)
    gw, sc, rw, total, mx, rest = take(TILE), take(KE), take(KE), take(NBLK), take(NBLK), take(KE)
    parts = take(NPART * KE // 2).bitcast(BF16).rearrange("p (k a e) -> p k a e", k=NBLK, a=NPART)
    top_tmp = take(6 * KE)
    ke = lambda v: v.rearrange("p (k e) -> p k e", e=E)
    with nc.Block() as block:
        @block.tensor
        def _(pe):
            pe.wait_ge(g.sim, call + 1)
            gate_products(m, pe, m.hC, gw, None, call)
            turn_weights(m, pe, parts, call)

        @block.scalar
        def _(act):
            nc.scalar.preload_act_table(ACT.Sigmoid)
            save_products(m, act, call)
            act.wait_ge(g.act_in, call + 1)
            nc.scalar.activation(sc, sc, ACT.Sigmoid).then_inc(g.act_out, 1)
            copy_weights(m, act, call, also=m.rwTf)

        @block.vector
        def _(dve):
            step = m.dve.on(dve)
            step(nc.vector.memset(gw, 0.0))
            nc.vector.tensor_copy(gw[:, 0:E], m.l("gate_w")).then_inc(g.sim, 1)
            dve.wait_ge(g.turned, call + 1)
            bias = m.r("gate_bias").unsqueeze(1).unsqueeze(1).broadcast_to([P, NSUP, BLKS, E])
            nc.vector.tensor_tensor(sc.rearrange("p (s j e) -> p s j e", s=NSUP, j=BLKS), by_token(m)[:, :, :, 0:E], bias,
                                    ALU.add).then_inc(g.act_in, 1)
            dve.wait_ge(g.act_out, 2 * call + 1)
            step(nc.vector.tensor_reduce(mx, ke(sc), AX.X, ALU.max))
            chosen = top_two(m, step, ke(sc), mx, top_tmp)
            step(nc.vector.tensor_tensor(ke(rw), ke(sc), chosen, ALU.mult))
            step(nc.vector.tensor_reduce(total, ke(rw), AX.X, ALU.add))
            step(nc.vector.tensor_scalar(total, total, 1e-6, None, ALU.add))
            step(nc.vector.reciprocal(total, total))
            step(nc.vector.tensor_tensor(ke(rw), ke(rw), total.unsqueeze(2).broadcast_to([P, NBLK, E]), ALU.mult))
            split_weights(m, step, ke(rw), parts, ke(rest))


def expert_sums(m, tmp):
    nc = m.nc
    names = ("up", "gelu", "spread", "scaled", "used", "biased", "added", "stored", "sbd")
    z = semaphores(m.sem, "ex_", names)
    XB = 4
    CH = (E + 1) * FC
    LAG = 3
    SHARED = 0.1
    ge = tmp[:, 0:XB * SUP].rearrange("p (u c) -> p u c", u=XB)
    ie = tmp[:, XB * SUP:2 * XB * SUP].rearrange("p (u c) -> p u c", u=XB)
    yb = tmp[:, 2 * XB * SUP:2 * XB * SUP + 2 * SUP].rearrange("p (u c) -> p u c", u=2)
    sbd = m.small[:, 40:41]
    up = [m.bank[i // 2][:, (i % 2) * SUP:(i % 2 + 1) * SUP] for i in range(4)]
    wB = [m.bank[2][:, 0:SUP], m.bank[2][:, SUP:2 * SUP]]
    acc = lambda par: m.bank[3][:, par * SUP:(par + 1) * SUP]
    up_w = lambda c: m.l("wu")[:, c * P:(c + 1) * P] if c < E * FC else m.l("swu")[:, (c - E * FC) * P:(c - E * FC + 1) * P]
    down_w = lambda c: m.l("wd")[:, c * P:(c + 1) * P] if c < E * FC else m.l("swd")[:, (c - E * FC) * P:(c - E * FC + 1) * P]
    up_b = lambda c: m.l("bu")[:, c:c + 1] if c < E * FC else m.l("sbu")[:, c - E * FC:c - E * FC + 1]
    PAIRS = NSUP // 2
    with nc.Block() as block:
        @block.tensor
        def _(pe):
            prime(pe, z.used)
            with pe.Fori(0, PAIRS) as p2:
                for par in range(2):
                    s = 2 * p2 + par
                    base = CH * s
                    h = m.hC[:, bass.ds(s * SUP, SUP)]
                    pe.wait_ge(z.scaled, PRIMED + base)
                    apart(pe)
                    spread(m, wB[0], 0, s).then_inc(z.spread, 1)
                    pe.wait_ge(z.added, PRIMED + 2 * p2)
                    apart(pe)
                    nc.tensor.matmul(acc(par), m.l("bd")[0:NPART * E, :], m.rwTf[:, bass.ds(s * SUP, SUP)], start=True, stop=False)
                    for c in range(CH + LAG):
                        if c < CH:
                            pe.wait_ge(z.gelu, PRIMED + base + max(0, c - XB + 1))
                            apart(pe)
                            nc.tensor.matmul(up[c % XB], up_w(c), h, start=True, stop=True).then_inc(z.up, 1)
                        if c >= LAG:
                            d = c - LAG
                            pe.wait_ge(z.scaled, PRIMED + base + d + 1)
                            nc.tensor.matmul(acc(par), down_w(d), ie[:, d % XB, :], start=False,
                                             stop=(d == CH - 1)).then_inc(z.used, 1)
                            if d % FC == 0 and d // FC + 1 < E:
                                spread(m, wB[(d // FC + 1) % 2], d // FC + 1, s).then_inc(z.spread, 1)

        @block.scalar
        def _(act):
            prime(act, z.gelu)
            nc.scalar.preload_act_table(ACT.Gelu)
            with act.Fori(0, PAIRS) as p2:
                for par in range(2):
                    s = 2 * p2 + par
                    base = CH * s
                    for c in range(CH):
                        act.wait_ge(z.scaled, PRIMED + base + max(0, c - XB + 1))
                        act.wait_ge(z.up, base + c + 1)
                        nc.scalar.activation(ge[:, c % XB, :], up[c % XB], ACT.Gelu, bias=up_b(c)).then_inc(z.gelu, 1)
                    act.wait_ge(z.sbd, 1)
                    act.wait_ge(z.added, PRIMED + 2 * p2)
                    act.wait_ge(z.used, PRIMED + base + CH)
                    nc.scalar.activation(yb[:, par, :], acc(par), ACT.Identity, bias=sbd).then_inc(z.biased, 1)

        @block.vector
        def _(dve):
            prime(dve, z.scaled, z.added)
            nc.vector.tensor_scalar(sbd, m.l("sbd"), SHARED, None, ALU.mult).then_inc(z.sbd, 1)

            def finish(s, par, p2):
                dve.wait_ge(z.biased, s + 1)
                apart(dve)
                x = m.xC[:, bass.ds(s * SUP, SUP)]
                nc.vector.scalar_tensor_tensor(out=x, in0=yb[:, par, :], scalar=m.gate[:, bass.ds((6 + 5) * B + p2, 1)],
                                               in1=x, op0=ALU.mult, op1=ALU.add).then_inc(z.added, 1)

            with dve.Fori(0, PAIRS) as p2:
                for par in range(2):
                    s = 2 * p2 + par
                    base = CH * s
                    for c in range(CH):
                        dve.wait_ge(z.used, PRIMED + base + max(0, c - XB + 1))
                        if c < E * FC:
                            dve.wait_ge(z.spread, E * s + c // FC + 1)
                        dve.wait_ge(z.gelu, PRIMED + base + c + 1)
                        if c < E * FC:
                            nc.vector.tensor_tensor(ie[:, c % XB, :], ge[:, c % XB, :], wB[(c // FC) % 2],
                                                    ALU.mult).then_inc(z.scaled, 1)
                        else:
                            nc.vector.tensor_scalar(ie[:, c % XB, :], ge[:, c % XB, :], SHARED, None,
                                                    ALU.mult).then_inc(z.scaled, 1)
                    finish(s, par, p2)

        @block.sync
        def _(sp):
            for s in range(NSUP):
                sp.wait_ge(z.added, PRIMED + s + 1)
                sp.dma_start(m.out[:, s * SUP:(s + 1) * SUP], m.xC[:, s * SUP:(s + 1) * SUP]).then_inc(z.stored, 16)
            sp.wait_ge(z.stored, 16 * NSUP)



def packed(inputs):
    g = {k: np.asarray(v) for k, v in inputs.items()}
    col = lambda v: v.reshape(-1, 1)
    halves = lambda w: w.reshape(HALVES, P, -1).transpose(1, 0, 2).reshape(P, -1)
    experts = lambda w: w.transpose(1, 0, 2).reshape(P, -1)
    att = {"wq": g["L0_attn_Wq"].T, "wk": g["L0_attn_Wk"].T, "wv": g["L0_attn_Wv"].T, "wo": g["L0_attn_Wo"].T,
           "wmod0": g["L0_wmod"], "wmod1": g["L1_wmod"], "c": np.concatenate([g["L0_c"].T, g["L1_c"].T], axis=1),
           "bq": col(g["L0_attn_bq"]), "bk": col(g["L0_attn_bk"]), "bv": col(g["L0_attn_bv"]), "bo": col(g["L0_attn_bo"]),
           "ln1w": col(g["L0_ffn_ln1_w"]), "ln1b": col(g["L0_ffn_ln1_b"]), "ln2w": col(g["L0_ffn_ln2_w"]),
           "ln2b": col(g["L0_ffn_ln2_b"]), "smha_sim": g["L0_ffn_smha_sim"], "moe_sim": g["L0_ffn_moe_sim"]}
    ffn = {"qp": experts(g["L0_ffn_q_proj"]), "kp": experts(g["L0_ffn_k_proj"]), "vp": experts(g["L0_ffn_v_proj"]),
           "op": experts(g["L0_ffn_o_proj"]), "w1": experts(g["L0_ffn_w1"]), "w2": experts(g["L0_ffn_w2"])}
    bd = np.concatenate([g["L1_ffn_bd"]] * NPART + [np.zeros((P - NPART * E, D), np.float32)])
    l1 = {"w_in": g["L1_attn_W_in"], "w_x": halves(g["L1_attn_W_x"]), "w_out": halves(g["L1_attn_W_out"]),
          "b_conv": halves(g["L1_attn_b_conv"]), "w_dt": halves(g["L1_attn_W_dt"][0]), "b_dt": halves(g["L1_attn_b_dt"]),
          "a_log": halves(g["L1_attn_A_log"]), "dskip": halves(g["L1_attn_D"]), "gate_w": g["L1_ffn_gate_w"].T,
          "wu": g["L1_ffn_Wu"].transpose(2, 0, 1).reshape(P, -1),
          "bu": g["L1_ffn_bu"].reshape(E, FC, P).transpose(2, 0, 1).reshape(P, -1),
          "wd": g["L1_ffn_Wd"].reshape(E, D, FC, P).transpose(3, 0, 2, 1).reshape(P, -1),
          "swu": g["L1_ffn_sWu"].T, "sbu": g["L1_ffn_sbu"].reshape(FC, P).T,
          "swd": g["L1_ffn_sWd"].reshape(D, FC, P).transpose(2, 1, 0).reshape(P, -1), "sbd": col(g["L1_ffn_sbd"]), "bd": bd}
    row = {"alpha": g["L0_attn_alpha"].reshape(1), "smha_gates": g["L0_ffn_smha_gates"], "moe_gates": g["L0_ffn_moe_gates"],
           "gate_bias": g["L1_ffn_gate_bias"], "w_conv": g["L1_attn_W_conv"][:, 0, :].T.reshape(-1)}
    side = lambda cols, parts: np.ascontiguousarray(np.concatenate([parts[k] for k in cols], axis=-1))
    return {"att_w": side(ATT_COLS, att), "ffn_w": side(FFN_COLS, ffn), "l1_w": side(L1_COLS, l1),
            "row_w": side(ROW_COLS, row).reshape(1, -1),
            "x_channels": np.ascontiguousarray(g["L0_attn_x"].reshape(N, D).T)}


def kernel(**inputs):
    import concourse.bacc as _bacc
    from concourse.bass_utils import run_bass_kernel_spmd as _run

    nc = _bacc.Bacc("TRN2", target_bir_lowering=False, num_devices=1)
    arrays = packed(inputs)
    args = {k: nc.dram_tensor(k, a.shape, mybir.dt.from_np(a.dtype), kind="ExternalInput").ap() for k, a in arrays.items()}
    out = nc.dram_tensor("out_channels", (P, N), F32, kind="ExternalOutput").ap()
    build(nc, args["att_w"], args["ffn_w"], args["l1_w"], args["row_w"], args["x_channels"], out)
    r = _run(nc, [arrays], core_ids=[0])
    return np.ascontiguousarray(r.results[0]["out_channels"].T).reshape(B, T, D)
```

```python
from collections import namedtuple
from contextlib import ExitStack

import numpy as np
import concourse.bass as bass
from concourse import mybir

F32 = mybir.dt.float32
BF16 = mybir.dt.bfloat16
F32R = mybir.dt.float32r
ALU = mybir.AluOpType
ACT = mybir.ActivationFunctionType
AX = mybir.AxisListType

P = 128
B, T, D = 2, 1024, 128
N = B * T
SUP = 512
NSUP = N // SUP
SUPB = T // SUP
NBLK = N // P
BLKS = SUP // P
NH, HD = 16, 8
HG = 4
NG = NH // HG
QB = T // P
E = 8
DI, DS, KC = 256, 16, 4
HALVES = DI // P
F = 512
FC = F // P
EPS = 1e-5
NEG = -3.0e38
TILE = 32
NPART = 3
TERMS = NPART * NPART - 1
STACK = TERMS * HD

PRIMED = 1


def columns(parts):
    at, out = 0, {}
    for name, width in parts:
        out[name] = (at, width)
        at += width
    return out, at


ATT_COLS, ATT_W = columns([
    ("wq", D), ("wk", D), ("wv", D), ("wo", D), ("wmod0", 6 * D), ("wmod1", 6 * D), ("c", 2 * B),
    ("bq", 1), ("bk", 1), ("bv", 1), ("bo", 1), ("ln1w", 1), ("ln1b", 1), ("ln2w", 1), ("ln2b", 1),
    ("smha_sim", E), ("moe_sim", E)])
FFN_COLS, FFN_W = columns([
    ("qp", E * D), ("kp", E * D), ("vp", E * D), ("w1", E * D), ("w2", E * D), ("op", E * D)])
SPLIT = ("qp", "kp", "vp", "w1", "w2")
L1_COLS, L1_W = columns([
    ("w_in", 2 * DI), ("w_x", HALVES * (2 * DS + 1)), ("w_out", HALVES * D), ("b_conv", HALVES), ("w_conv", HALVES * KC), ("w_dt", HALVES),
    ("b_dt", HALVES), ("a_log", HALVES * DS), ("dskip", HALVES), ("gate_w", E), ("up", (E + 1) * F),
    ("down", (E + 1) * F), ("up_bias", (E + 1) * FC), ("sbd", 1), ("bd", D)])
ROW_COLS, ROW_W = columns([("alpha", 1), ("smha_gates", E), ("moe_gates", E), ("gate_bias", E)])


class Shared:
    pass


def semaphores(sem, prefix, names):
    return namedtuple("Semaphores", names)(*[sem(prefix + name) for name in names])


class Steps:

    def __init__(self, sem):
        self.sem, self.count = sem, 0

    def on(self, engine):
        def step(ins):
            self.count += 1
            ins.then_inc(self.sem, 1)
            engine.wait_ge(self.sem, self.count)
        return step


def apart(engine):
    engine.nop(nofuse=True)


def prime(engine, *sems, count=PRIMED):
    for sem in sems:
        engine.nop(nofuse=True).then_inc(sem, count)


def three_passes(m, out, w_high, w_low, x_high, x_low, start, stop):
    m.nc.tensor.matmul(out, w_high, x_low, start=start, stop=False)
    m.nc.tensor.matmul(out, w_high, x_high, start=False, stop=False)
    return m.nc.tensor.matmul(out, w_low, x_high, start=False, stop=stop)


def build(nc, att_in, ffn_in, l1_in, row_in, x_in, out):
    ctx = ExitStack()
    with ctx:
        def sb(name, shape, dt=F32):
            return ctx.enter_context(nc.sbuf_tensor(name, shape, dt))

        def sem(name):
            return ctx.enter_context(nc.semaphore(name))

        m = Shared()
        m.nc, m.sem, m.out = nc, sem, out
        m.xC = sb("xC", [P, N])
        m.att = sb("att_tile", [P, ATT_W])
        m.late = sb("late", [P, L1_W])
        m.row = sb("row", [P, ROW_W])
        m.ident = sb("ident", [P, P])
        m.ones = sb("ones", [P, P])
        m.causal = sb("causal", [P, P])
        m.ident16 = sb("ident16", [P, P], BF16)
        m.causal16 = sb("causal16", [P, P], BF16)
        m.countdown = sb("countdown", [P, E])
        m.sims = sb("sims", [P, 2 * TILE])
        m.one_at_e = sb("one_at_e", [P, TILE])
        m.sel_e = sb("sel_e", [NPART * E, E, P], BF16)
        m.mod = sb("mod", [P, 2 * 6 * B])
        m.gsign = sb("gsign", [P, 2 * 6 * B])
        m.gate = sb("gate", [P, 2 * 6 * B])
        m.small = sb("small", [P, 64])
        m.eps = m.small[:, 2:3]
        m.rowg = sb("rowg", [P, 2 * E])
        m.rwT = sb("rwT", [NPART * E, N], BF16)
        m.sel_n = sb("sel_n", [NPART * 2 * DS, 2 * DS, P], BF16)
        m.sb = sb
        m.bank = [ctx.enter_context(nc.psum_tensor(f"bank{i}", [P, 2 * SUP], F32)) for i in range(4)]
        m.qk_parts = nc.dram_tensor("qk_parts", [2, NPART, D, N], BF16).ap()
        m.att_in, m.ffn_in, m.l1_in, m.row_in, m.x_in = att_in, ffn_in, l1_in, row_in, x_in
        m.dve = Steps(sem("dve_step"))
        m.act = Steps(sem("act_step"))
        m.pool = Steps(sem("pool_step"))
        m.att_loaded, m.ffn_loaded, m.l1_loaded = sem("att_loaded"), sem("ffn_loaded"), sem("l1_loaded")
        m.ln = semaphores(sem, "ln_", ("raw_T", "var", "std", "shift", "norm", "norm_act", "out_T"))
        m.gt = semaphores(sem, "gate_", ("sq", "weights", "logits", "saved", "turned", "act_out", "act_in", "split",
                                        "splitT"))
        m.ln_calls = m.gt_calls = 0

        def a(name):
            at, w = ATT_COLS[name]
            return m.att[:, at:at + w]

        def l(name):
            at, w = L1_COLS[name]
            return m.late[:, at:at + w]

        def r(name):
            at, w = ROW_COLS[name]
            return m.row[:, at:at + w]

        m.a, m.l, m.r = a, l, r
        m.raw = m.late[:, 0:B * NG * QB * P].rearrange("p (n q) -> p n q", q=P)
        with nc.sbuf_tensor("ffn_tile", [P, FFN_W], F32) as m.ffn:
            with nc.sbuf_tensor("attention_arena", [P, 24704], F32) as m.arena:
                load_and_constants(m)
                modulation(m)
                hC = m.arena[:, 0:N]
                layer_norm(m, m.xC, lambda s: hC[:, s * SUP:(s + 1) * SUP], lambda s: m.scale1(0, 1, s),
                           lambda s: m.shift(0, 0, s), tmp=2 * N, meanwhile=lambda pool: zero_stacks(m, pool))
                head_projections(m, hC)
                decayed_attention(m)
            feed_forward(m)
        with nc.sbuf_tensor("mixer_arena", [P, 31696], F32) as m.arena:
            mixer(m)
        experts(m)



def load_and_constants(m):
    nc = m.nc
    lag_ready = m.sem("lag_ready")
    t = attention_tiles(m)
    vaug, decay = t.vaug, t.decay
    with nc.Block() as block:
        @block.sync
        def _(sp):
            sp.dma_start(m.att[:, :], m.att_in).then_inc(m.att_loaded, 16)
            sp.dma_start(m.row[:, :], m.row_in.partition_broadcast(P)).then_inc(m.att_loaded, 16)
            sp.dma_start(m.xC[:, :], m.x_in).then_inc(m.att_loaded, 16)
            sp.dma_start(m.ffn[:, :], m.ffn_in).then_inc(m.ffn_loaded, 16)
            sp.wait_ge(m.att_loaded, 48)

        @block.gpsimd
        def _(pool):
            step = m.pool.on(pool)
            nc.gpsimd.memset(m.ident[:, :], 0.0)
            nc.gpsimd.memset(m.causal[:, :], 0.0)
            nc.gpsimd.memset(m.sel_e[:, :, :], 0.0)
            nc.gpsimd.memset(m.ones[:, :], 1.0)
            nc.gpsimd.memset(m.eps, EPS)
            nc.gpsimd.memset(vaug[:, :, :, HD:HD + 1], 1.0)
            step(nc.gpsimd.memset(m.small[:, 3:4], 0.0))
            (nc.gpsimd.iota(decay[:, :], pattern=[[1, 2 * T - P]], base=-(T - P), channel_multiplier=-1,
                                allow_small_or_imprecise_dtypes=True)).then_inc(lag_ready, 1)
            nc.gpsimd.affine_select(out=m.ident[:, :], in_=m.ident[:, :], compare_op=ALU.not_equal, fill=1.0,
                                    base=0, pattern=[[-1, P]], channel_multiplier=1)
            nc.gpsimd.affine_select(out=m.causal[:, :], in_=m.causal[:, :], compare_op=ALU.is_ge, fill=NEG,
                                    base=0, pattern=[[-1, P]], channel_multiplier=1)
            for part in range(NPART):
                step(nc.gpsimd.affine_select(out=m.sel_e[:, :, :], in_=m.sel_e[:, :, :], compare_op=ALU.not_equal,
                                             fill=1.0, base=-part * E, pattern=[[-1, E], [0, P]],
                                             channel_multiplier=1))
            nc.gpsimd.iota(m.countdown[:, :], pattern=[[-1, E]], base=E, channel_multiplier=0,
                           allow_small_or_imprecise_dtypes=True)
            step(nc.gpsimd.memset(m.one_at_e[:, :], 0.0))
            nc.gpsimd.memset(m.one_at_e[:, E:E + 1], 1.0)
            step(nc.gpsimd.tensor_copy(m.ident16[:, :], m.ident[:, :]))
            nc.gpsimd.tensor_copy(m.causal16[:, :], m.causal[:, :])

        @block.vector
        def _(dve):
            dve.wait_ge(m.att_loaded, 48)
            nc.vector.tensor_scalar(m.small[:, 0:1], m.r("alpha"), -1.0, None, ALU.mult)

        @block.scalar
        def _(act):
            act.wait_ge(lag_ready, 1)
            nc.scalar.activation(decay[:, :], decay[:, :], ACT.Abs)


def modulation(m):
    nc = m.nc
    silu_ready, mod_summed = m.sem("silu_ready"), m.sem("mod_summed")
    sim_squared, sim_summed, sim_rooted = m.sem("sim_squared"), m.sem("sim_summed"), m.sem("sim_rooted")
    at = ATT_COLS["smha_sim"][0]
    sims, squares, roots = m.att[:, at:at + 2 * E], m.small[:, 8:8 + 2 * E], m.small[:, 24:24 + 2 * E]
    silu_c = m.small[:, 4:4 + 2 * B]
    ps = m.bank[0]
    W = 2 * 6 * B
    with nc.Block() as block:
        @block.scalar
        def _(act):
            nc.scalar.activation(silu_c, m.a("c"), ACT.Silu).then_inc(silu_ready, 1)
            act.wait_ge(sim_summed, 1)
            nc.scalar.activation(roots, m.bank[1][:, 0:2 * E], ACT.Sqrt).then_inc(sim_rooted, 1)

        @block.tensor
        def _(pe):
            pe.wait_ge(sim_squared, 1)
            nc.tensor.matmul(m.bank[1][:, 0:2 * E], m.ones[:, :], squares, start=True, stop=True).then_inc(sim_summed, 1)
            pe.wait_ge(silu_ready, 1)
            for layer in range(2):
                w = m.a(f"wmod{layer}")
                for j in range(6):
                    at = (layer * 6 + j) * B
                    mm = nc.tensor.matmul(ps[:, at:at + B], w[:, j * D:(j + 1) * D],
                                          silu_c[:, layer * B:(layer + 1) * B], start=True, stop=True)
            mm.then_inc(mod_summed, 1)

        @block.vector
        def _(dve):
            step = m.dve.on(dve)
            nc.vector.memset(m.sims[:, :], 0.0)
            nc.vector.tensor_tensor(squares, sims, sims, ALU.mult).then_inc(sim_squared, 1)
            dve.wait_ge(mod_summed, 1)
            step(nc.vector.tensor_copy(m.mod[:, :], ps[:, 0:W]))
            step(nc.vector.tensor_scalar(m.gsign[:, :], m.mod[:, :], 0.0, 2.0, ALU.is_ge, ALU.mult))
            step(nc.vector.scalar_tensor_tensor(out=m.gate[:, :], in0=m.mod[:, :], scalar=-1.0, in1=m.mod[:, :],
                                                op0=ALU.mult, op1=ALU.max))
            step(nc.vector.tensor_scalar(m.gate[:, :], m.gate[:, :], 0.25, None, ALU.max))
            step(nc.vector.scalar_tensor_tensor(out=m.gate[:, :], in0=m.gsign[:, :], scalar=-1.0, in1=m.gate[:, :],
                                                op0=ALU.add, op1=ALU.mult))
            step(nc.vector.tensor_scalar(m.gsign[:, :], m.mod[:, :], 1.0, None, ALU.add))
            dve.wait_ge(sim_rooted, 1)
            step(nc.vector.tensor_scalar(roots, roots, 1e-12, None, ALU.max))
            step(nc.vector.reciprocal(roots, roots))
            step(nc.vector.tensor_tensor(m.sims[:, :].rearrange("p (i c) -> p i c", i=2)[:, :, 0:E],
                                         sims.rearrange("p (i e) -> p i e", i=2), roots.rearrange("p (i e) -> p i e", i=2),
                                         ALU.mult))
            step(nc.vector.tensor_scalar(m.small[:, 1:2], m.a("bq"), float(HD) ** -0.5, None, ALU.mult))

    def column(tile, layer, j, b):
        at = (layer * 6 + j) * B + b
        return tile[:, at:at + 1]

    m.scale1 = lambda layer, j, s: column(m.gsign, layer, j, s // SUPB)
    m.shift = lambda layer, j, s: column(m.mod, layer, j, s // SUPB)
    m.gated = lambda layer, j, s: column(m.gate, layer, j, s // SUPB)



def layer_norm(m, src, dst, scale, bias, tmp, meanwhile=None, act_first=None, high=None,
               queue=None):
    nc, ln = m.nc, m.ln
    call = m.ln_calls
    m.ln_calls += 1
    c4, c1 = call * NSUP, call * NBLK
    t0 = tmp
    xn = m.arena[:, t0:t0 + NSUP * SUP].rearrange("p (s j c) -> p s j c", s=NSUP, j=BLKS)
    t1 = t0 + NSUP * SUP
    stats = m.arena[:, t1:t1 + 96].rearrange("p (k c) -> p k c", c=6)
    mv = m.arena[:, t1 + 96:t1 + 128].rearrange("p (k c) -> p k c", c=2)
    std = m.small[:, 8:8 + NBLK]
    rstd = m.small[:, 24:24 + NBLK]
    shift = m.small[:, 44:44 + NBLK]
    c2 = call * NSUP // 2
    raw = lambda s: m.bank[s // 2][:, (s % 2) * SUP:(s % 2 + 1) * SUP]
    back = lambda s: m.bank[2 + s // 2][:, (s % 2) * SUP:(s % 2 + 1) * SUP]
    assert NSUP == 4
    with nc.Block() as block:
        if queue is not None:
            @block.sync
            def _(sp):
                queue(sp)

        if meanwhile is not None:
            @block.gpsimd
            def _(pool):
                meanwhile(pool)

        @block.tensor
        def _(pe):
            for s in range(NSUP):
                for j in range(BLKS):
                    at = s * SUP + j * P
                    mm = nc.tensor.transpose(raw(s)[:, j * P:(j + 1) * P], src[:, at:at + P], m.ident[:, :])
                mm.then_inc(ln.raw_T, 1)
            for s in range(NSUP):
                pe.wait_ge(ln.norm_act if s % 2 else ln.norm, c2 + s // 2 + 1)
                for j in range(BLKS):
                    mm = nc.tensor.transpose(back(s)[:, j * P:(j + 1) * P], xn[:, s, j, :], m.ident[:, :])
                mm.then_inc(ln.out_T, 1)

        @block.vector
        def _(dve):
            step = m.dve.on(dve)

            def statistics(s):
                dve.wait_ge(ln.raw_T, c4 + s + 1)
                for j in range(BLKS):
                    ins = nc.vector.bn_stats(stats[:, s * BLKS + j, :], raw(s)[:, j * P:(j + 1) * P])
                step(ins)
                for j in range(BLKS):
                    ins = nc.vector.bn_aggr(mv[:, s * BLKS + j, :], stats[:, s * BLKS + j, :])
                ins.then_inc(ln.var, 1)

            def invert(s):
                k0 = s * BLKS
                dve.wait_ge(ln.std, c4 + s + 1)
                step(nc.vector.reciprocal(rstd[:, k0:k0 + BLKS], std[:, k0:k0 + BLKS]))
                if s % 2:
                    nc.vector.scalar_tensor_tensor(out=shift[:, k0:k0 + BLKS], in0=mv[:, k0:k0 + BLKS, 0], scalar=-1.0,
                                                   in1=rstd[:, k0:k0 + BLKS], op0=ALU.mult, op1=ALU.mult).then_inc(ln.shift, 1)

            def normalise(s):
                for j in range(BLKS):
                    k = s * BLKS + j
                    ins = nc.vector.tensor_scalar(xn[:, s, j, :], raw(s)[:, j * P:(j + 1) * P], mv[:, k, 0:1],
                                                  rstd[:, k:k + 1], ALU.subtract, ALU.mult)
                ins.then_inc(ln.norm, 1)

            def put(s):
                dve.wait_ge(ln.out_T, c4 + s + 1)
                for out in (dst,) if high is None else (dst, high):
                    nc.vector.tensor_scalar(out(s), back(s), scale(s), bias(s), ALU.mult, ALU.add)

            statistics(0)
            statistics(1)
            invert(0)
            normalise(0)
            invert(1)
            statistics(2)
            statistics(3)
            invert(3)
            invert(2)
            normalise(2)
            put(2)

        @block.scalar
        def _(act):
            if act_first is not None:
                act_first(act)
            def root(s):
                k0 = s * BLKS
                act.wait_ge(ln.var, c4 + s + 1)
                nc.scalar.activation(std[:, k0:k0 + BLKS], mv[:, k0:k0 + BLKS, 1], ACT.Sqrt,
                                     bias=m.eps[:, 0:1]).then_inc(ln.std, 1)

            def normalise(s):
                act.wait_ge(ln.shift, c2 + s // 2 + 1)
                for j in range(BLKS):
                    k = s * BLKS + j
                    ins = nc.scalar.activation(xn[:, s, j, :], raw(s)[:, j * P:(j + 1) * P], ACT.Identity,
                                               bias=shift[:, k:k + 1], scale=rstd[:, k:k + 1])
                ins.then_inc(ln.norm_act, 1)

            def put(s):
                act.wait_ge(ln.out_T, c4 + s + 1)
                for out in (dst,) if high is None else (dst, high):
                    nc.scalar.activation(out(s), back(s), ACT.Identity, bias=bias(s), scale=scale(s))

            root(0)
            root(1)
            normalise(1)
            root(2)
            root(3)
            put(0)
            normalise(3)
            put(1)
            put(3)



def attention_tiles(m):
    ar = m.arena
    t = Shared()
    at = 0

    def take(width):
        nonlocal at
        at += width
        return ar[:, at - width:at]

    t.qpair = take(2 * 2 * T // 2).bitcast(BF16).rearrange("p (u h q) -> p u h q", u=2, h=2)
    t.weighted = take(4 * T).rearrange("p (u k) -> p u k", u=4)
    t.probsT = take(2 * HG * QB * P).rearrange("p (u h k q) -> p u h k q", u=2, h=HG, k=QB)
    t.vstat = take(2 * QB * HG * 32).rearrange("p (u k h c) -> p u k h c", u=2, k=QB, h=HG)
    m.heads_end = at
    t.kpad = take(2 * HG * T // 2).bitcast(BF16).rearrange("p (u h k) -> p u h k", u=2, h=HG)
    t.vaug = take(NBLK * NH * (HD + 1)).rearrange("p (k h c) -> p k h c", k=NBLK, h=NH)
    t.decay = take(2 * T - P)
    assert at <= ar.shape[1], at
    return t


def zero_stacks(m, pool):
    t, step = attention_tiles(m), m.pool.on(pool)
    step(m.nc.gpsimd.memset(t.kpad[0:STACK, :, 1:HG:2, :], 0.0))
    step(m.nc.gpsimd.memset(t.kpad[STACK:P, :, 0:HG:2, :], 0.0))


def head_projections(m, hC):
    nc, t = m.nc, attention_tiles(m)
    s_q, s_k, s_v = m.sem("q_summed"), m.sem("k_summed"), m.sem("v_summed")
    s_first, s_second, s_third = m.sem("part1_ready"), m.sem("part2_ready"), m.sem("part3_ready")
    s_rest, s_qk_free, s_v_free = m.sem("rest_ready"), m.sem("qk_free"), m.sem("v_free")
    parts_stored = m.sem("parts_stored")
    base = N
    full = [m.arena[:, base + i * N:base + (i + 1) * N] for i in range(2)]
    rest = [m.arena[:, base + (2 + i) * N:base + (3 + i) * N] for i in range(2)]
    all_parts = m.arena[:, base + 4 * N:base + 4 * N + 2 * NPART * N // 2].bitcast(BF16).rearrange(
        "p (i a t) -> p i a t", i=2, a=NPART)
    parts = [[all_parts[:, i, j, :] for j in range(NPART)] for i in range(2)]
    assert base + 4 * N + 2 * NPART * N // 2 <= m.heads_end
    sup = lambda tile, s: tile[:, s * SUP:(s + 1) * SUP]
    half = lambda tile, s: tile[:, (s % 2) * SUP:(s % 2 + 1) * SUP]
    with nc.Block() as block:
        @block.tensor
        def _(pe):
            for s in range(NSUP):
                if s >= 2:
                    pe.wait_ge(s_qk_free, 2 * (s - 1))
                    pe.wait_ge(s_v_free, s - 1)
                nc.tensor.matmul(half(m.bank[0], s), m.a("wq"), sup(hC, s), start=True, stop=True).then_inc(s_q, 1)
                nc.tensor.matmul(half(m.bank[1], s), m.a("wk"), sup(hC, s), start=True, stop=True).then_inc(s_k, 1)
                for j in range(BLKS):
                    at = s * SUP + j * P
                    mm = nc.tensor.matmul(half(m.bank[2], s)[:, j * P:(j + 1) * P], hC[:, at:at + P], m.a("wv"),
                                          start=True, stop=True)
                mm.then_inc(s_v, 1)

        @block.scalar
        def _(act):
            for s in range(NSUP):
                act.wait_ge(s_q, s + 1)
                nc.scalar.activation(sup(full[0], s), half(m.bank[0], s), ACT.Identity, bias=m.small[:, 1:2],
                                     scale=float(HD) ** -0.5)
                nc.scalar.activation(sup(parts[0][0], s), half(m.bank[0], s), ACT.Identity, bias=m.small[:, 1:2],
                                     scale=float(HD) ** -0.5).then_inc(s_qk_free, 1)
                act.wait_ge(s_k, s + 1)
                nc.scalar.activation(sup(full[1], s), half(m.bank[1], s), ACT.Identity, bias=m.a("bk"))
                nc.scalar.activation(sup(parts[1][0], s), half(m.bank[1], s), ACT.Identity,
                                     bias=m.a("bk")).then_inc(s_qk_free, 1)
                for i in range(2):
                    act.wait_ge(s_rest, 2 * s + i + 1)
                    nc.scalar.activation(sup(parts[i][1], s), sup(rest[i], s), ACT.Copy).then_inc(s_second, 1)

        @block.vector
        def _(dve):
            for s in range(NSUP):
                for i in range(2):
                    dve.wait_ge(s_qk_free, 2 * s + i + 1)
                    nc.vector.tensor_tensor(sup(rest[i], s), sup(full[i], s), sup(parts[i][0], s),
                                            ALU.subtract).then_inc(s_rest, 1)
                dve.wait_ge(s_v, s + 1)
                nc.vector.tensor_copy(
                    t.vaug[:, s * BLKS:(s + 1) * BLKS, :, 0:HD].rearrange("p k h c -> p (k h) c"),
                    half(m.bank[2], s).rearrange("p (k c) -> p k c", c=HD)).then_inc(s_v_free, 1)
                for i in range(2):
                    dve.wait_ge(s_second, 2 * s + i + 1)
                    nc.vector.tensor_tensor(sup(parts[i][2], s), sup(rest[i], s), sup(parts[i][1], s),
                                            ALU.subtract).then_inc(s_third, 1)

        @block.gpsimd
        def _(pool):
            step = m.pool.on(pool)
            step(nc.gpsimd.memset(m.sel_n[:, :, :], 0.0))
            for part in range(NPART):
                step(nc.gpsimd.affine_select(out=m.sel_n[:, :, :], in_=m.sel_n[:, :, :], compare_op=ALU.not_equal, fill=1.0,
                                             base=-part * 2 * DS, pattern=[[-1, 2 * DS], [0, P]], channel_multiplier=1))

        @block.sync
        def _(sp):
            for s in range(NSUP):
                sp.wait_ge(s_third, 2 * (s + 1))
                for i in range(2):
                    sp.dma_start(m.qk_parts[i].rearrange("a d t -> d a t")[:, :, s * SUP:(s + 1) * SUP],
                                 all_parts[:, i, :, s * SUP:(s + 1) * SUP]).then_inc(parts_stored, 16)
            sp.wait_ge(parts_stored, 16 * 2 * NSUP)


def decayed_attention(m):
    nc, t = m.nc, attention_tiles(m)
    names = ("scored", "weighted", "negmax", "exped", "turnedA", "turnedB", "copiedA", "copiedB", "pv_done",
             "raw_saved", "v_early", "v_late", "tiles_zeroed", "decay_ready")
    z = semaphores(m.sem, "att_", names)
    head_loaded = [m.sem(f"att_head_loaded{h}") for h in range(HG)]
    negm = m.small[:, 8:16]
    rowmax = m.small[:, 16:24]
    score = [m.bank[0], m.bank[1]]
    turnA, turnB = m.bank[2][:, 0:SUP], m.bank[2][:, SUP:2 * SUP]
    pv = [m.bank[3][:, 0:P], m.bank[3][:, SUP:SUP + P]]
    KB = QB // 2
    GROUPS = B * NG
    LOADED = 16 * 2 * NPART

    def every_group(engine, steps):
        steps(0)
        with engine.Fori(1, GROUPS - 1) as g:
            steps(g)
        steps(GROUPS - 1)

    with nc.Block() as block:
        @block.sync
        def _(sp):
            for g in range(GROUPS):
                b, hg, u = g // NG, g % NG, g % 2
                if g >= 2:
                    sp.wait_ge(z.scored, HG * QB * (g - 1))
                for head in range(HG):
                    if g:
                        sp.wait_ge(head_loaded[head], LOADED * g)
                    j, w = head // 2, head % 2
                    for i, tile in enumerate((t.qpair[:, u, j, :], t.kpad[:, u, head, :])):
                        src = m.qk_parts[i][:, :, b * T:(b + 1) * T].rearrange("a (h d) t -> h a d t", d=HD)[hg * HG + head]
                        for a in range(NPART):
                            n = NPART if a < NPART - 1 else NPART - 1
                            at = w * STACK + a * NPART * HD
                            rows = src[a].unsqueeze(0).broadcast_to([n, HD, T]) if i == 0 else src[0:n]
                            sp.dma_start(tile[at:at + n * HD], rows).then_inc(head_loaded[head], 16)

        @block.gpsimd
        def _(pool):
            nc.gpsimd.memset(t.vstat[:, :, :, :, :], 0.0).then_inc(z.tiles_zeroed, 1)
            pool.wait_ge(z.tiles_zeroed, 1)

            def steps(g):
                vg = t.vaug[:, bass.ds(((g >> 2) & (B - 1)) * QB, QB), bass.ds((g & (NG - 1)) * HG, HG), :]
                for i in range(QB):
                    n = QB * g + i
                    for u in range(HG):
                        k = HG * n + u
                        if i == 0 and u == 2:
                            after(pool, z.pv_done, n - 1)
                            apart(pool)
                            nc.gpsimd.tensor_copy(t.vstat[:, 0, :, :, 0:HD + 1], vg).then_inc(z.v_early, 1)
                        if i == 2 and u == 2:
                            after(pool, z.pv_done, n - 2)
                            apart(pool)
                            nc.gpsimd.tensor_copy(t.vstat[:, 1, :, :, 0:HD + 1], vg).then_inc(z.v_late, 1)
                        slot = k_slot(i, u)
                        after(pool, z.weighted, k + 1)
                        after(pool, z.exped, k - 7)
                        apart(pool)
                        nc.gpsimd.tensor_scalar(negm[:, slot:slot + 1], rowmax[:, slot:slot + 1], -1.0, None,
                                                ALU.mult).then_inc(z.negmax, 1)

            every_group(pool, steps)

        @block.tensor
        def _(pe):
            def scores(g, i, u):
                n = QB * g + i
                if i == 0:
                    for head in (u, u + 1) if u % 2 == 0 else (u,):
                        after(pe, head_loaded[head], LOADED * (g + 1))
                after(pe, z.weighted, HG * n + u - 1)
                for h in range(2):
                    mm = nc.tensor.matmul(score[u % 2][:, h * SUP:(h + 1) * SUP],
                                          t.qpair[:, g & 1, u // 2, i * P:(i + 1) * P],
                                          t.kpad[:, g & 1, u, h * SUP:(h + 1) * SUP], start=True, stop=True)
                mm.then_inc(z.scored, 1)

            def turn(g, i, u):
                k = HG * (QB * g + i) + u
                after(pe, z.exped, k + 1)
                for turned, bank, copied, k0 in ((z.turnedA, turnA, z.copiedA, 0), (z.turnedB, turnB, z.copiedB, KB)):
                    after(pe, copied, k)
                    for j in range(KB):
                        mm = nc.tensor.transpose(bank[:, j * P:(j + 1) * P], t.weighted[:, u, (k0 + j) * P:(k0 + j + 1) * P],
                                                 m.ident[:, :])
                    mm.then_inc(turned, 1)

            def values(g, i, u):
                n, par = QB * g + i, i % 2
                if u == 0:
                    after(pe, z.copiedA, HG * (n + 1))
                    after(pe, z.copiedB, HG * (n + 1))
                    if i == QB - 1:
                        after(pe, z.v_late, g + 1)
                    elif i == 0:
                        after(pe, z.v_early, g + 1)
                    after(pe, z.raw_saved, n - 1)
                for kb in (2 * u, 2 * u + 1):
                    for h in range(HG):
                        mm = nc.tensor.matmul(pv[par][32 * h:32 * (h + 1), :], t.vstat[:, i // (QB - 1), kb, h, :],
                                              t.probsT[:, par, h, kb, :], start=(kb == 0), stop=(kb == QB - 1))
                if u == HG - 1:
                    mm.then_inc(z.pv_done, 1)

            def steps(g):
                first, last = type(g) is int and g == 0, type(g) is int and g == GROUPS - 1
                for i in range(QB):
                    for u in range(HG):
                        turn(g, i, u)
                        if u == 0:
                            scores(g, i, 3)
                        elif i < QB - 1:
                            scores(g, i + 1, u - 1)
                        elif not last:
                            scores(g + 1, 0, u - 1)
                        if i:
                            values(g, i - 1, u)
                        elif not first:
                            values(g - 1, QB - 1, u)

            scores(0, 0, 0)
            scores(0, 0, 1)
            scores(0, 0, 2)
            every_group(pe, steps)
            for u in range(HG):
                values(GROUPS - 1, QB - 1, u)

        @block.vector
        def _(dve):
            def copy_a(g, i, u):
                n, par = QB * g + i, i % 2
                if u == 0:
                    after(dve, z.pv_done, n - 1)
                after(dve, z.turnedA, HG * n + u + 1)
                nc.vector.tensor_copy(t.probsT[:, par, u, 0:KB, :].rearrange("p k q -> p (k q)"), turnA).then_inc(z.copiedA, 1)

            def steps(g):
                for i in range(QB):
                    for u in range(HG):
                        k, slot = HG * (QB * g + i) + u, k_slot(i, u)
                        after(dve, z.turnedB, k - 3)
                        after(dve, z.scored, k + 1)
                        start = (QB - 1 - i) * P
                        apart(dve)
                        nc.vector.tensor_tensor_reduce(t.weighted[:, u, :], score[u % 2][:, :],
                                                       t.decay[:, start:start + T], 1.0, NEG, ALU.mult, ALU.max,
                                                       rowmax[:, slot:slot + 1]).then_inc(z.weighted, 1)
                        if u >= 2:
                            copy_a(g, i, u - 2)
                        elif i:
                            copy_a(g, i - 1, u + 2)
                        elif not (type(g) is int and g == 0):
                            copy_a(g - 1, QB - 1, u + 2)

            dve.wait_ge(z.decay_ready, 1)
            every_group(dve, steps)
            copy_a(GROUPS - 1, QB - 1, HG - 2)
            copy_a(GROUPS - 1, QB - 1, HG - 1)

        @block.scalar
        def _(act):
            def copy_b(g, i, u):
                n, par = QB * g + i, i % 2
                if u == 0:
                    after(act, z.pv_done, n - 1)
                after(act, z.turnedB, HG * n + u + 1)
                nc.scalar.activation(t.probsT[:, par, u, KB:QB, :].rearrange("p k q -> p (k q)"), turnB,
                                     ACT.Copy).then_inc(z.copiedB, 1)

            def save(g, i):
                n = QB * g + i
                after(act, z.pv_done, n + 1)
                nc.scalar.activation(m.raw[:, n, :], pv[i % 2], ACT.Copy).then_inc(z.raw_saved, 1)

            def steps(g):
                first = type(g) is int and g == 0
                for i in range(QB):
                    for u in range(HG):
                        k, slot = HG * (QB * g + i) + u, k_slot(i, u)
                        after(act, z.negmax, k + 1)
                        nc.scalar.activation(t.weighted[:, u, :], t.weighted[:, u, :], ACT.Exp,
                                             bias=negm[:, slot:slot + 1]).then_inc(z.exped, 1)
                        unit_before(g, i, u, copy_b)
                        if u == 1:
                            if i >= 2:
                                save(g, i - 2)
                            elif not first:
                                save(g - 1, QB - 2 + i)

            at = ROW_COLS["smha_gates"][0]
            nc.scalar.activation(m.rowg[:, 0:2 * E], m.row[:, at:at + 2 * E], ACT.Sigmoid)
            nc.scalar.preload_act_table(ACT.Exp)
            nc.scalar.activation(t.decay[:, :], t.decay[:, :], ACT.Exp, scale=m.small[:, 0:1]).then_inc(z.decay_ready, 1)
            every_group(act, steps)
            copy_b(GROUPS - 1, QB - 1, HG - 1)
            save(GROUPS - 1, QB - 2)
            save(GROUPS - 1, QB - 1)


def k_slot(i, u):
    return (HG * i + u) % 8


def unit_before(g, i, u, do):
    if u:
        do(g, i, u - 1)
    elif i:
        do(g, i - 1, HG - 1)
    elif not (type(g) is int and g == 0):
        do(g - 1, QB - 1, HG - 1)


def after(engine, sem, count):
    if type(count) is not int:
        engine.wait_ge(sem, count)
    elif count > 0:
        engine.wait_ge(sem, count)


def attention_output(m, tmp):
    nc = m.nc
    names = ("turned", "rec", "normed", "turned_back", "biased", "wo_summed", "wo_biased", "x_added", "w_high")
    z = semaphores(m.sem, "ao_", names)
    rec = tmp[:, 0:2 * NH].rearrange("p (u h) -> p u h", u=2)
    on = tmp[:, 64:64 + 4 * D].rearrange("p (u c) -> p u c", u=4)
    oC = tmp[:, 1024:1024 + N]
    yC = tmp[:, 1024 + N:1024 + N + 2 * SUP].rearrange("p (u c) -> p u c", u=2)
    raw_bank = lambda k: m.bank[0][:, (k % 2) * SUP:(k % 2 + 1) * SUP]
    half = lambda tile, s: tile[:, (s % 2) * SUP:(s % 2 + 1) * SUP]
    with nc.Block() as block:
        @block.gpsimd
        def _(pool):
            for i, name in enumerate(SPLIT):
                pool.wait_ge(z.w_high, i + 1)
                nc.gpsimd.tensor_tensor(m.ffn_low[name][:, :], ffn_columns(m, name), m.ffn_high[name][:, :], ALU.subtract)

        @block.tensor
        def _(pe):
            def turn(k):
                if k >= 2:
                    pe.wait_ge(z.normed, k - 1)
                b, i = divmod(k, QB)
                for hg in range(NG):
                    mm = nc.tensor.transpose(raw_bank(k)[:, hg * P:(hg + 1) * P], m.raw[:, (b * NG + hg) * QB + i, :],
                                             m.ident[:, :])
                mm.then_inc(z.turned, 1)

            def back(k):
                s, j = divmod(k, BLKS)
                pe.wait_ge(z.normed, k + 1)
                if j == 0 and s >= 2:
                    pe.wait_ge(z.biased, s - 1)
                mm = nc.tensor.transpose(half(m.bank[1], s)[:, j * P:(j + 1) * P], on[:, k % 4, :], m.ident[:, :])
                mm.then_inc(z.turned_back, 1)
                if j == BLKS - 1:
                    pe.wait_ge(z.biased, s + 1)
                    if s >= 2:
                        pe.wait_ge(z.wo_biased, s - 1)
                    nc.tensor.matmul(half(m.bank[2], s), m.a("wo"), oC[:, s * SUP:(s + 1) * SUP], start=True,
                                     stop=True).then_inc(z.wo_summed, 1)

            turn(0)
            for k in range(NBLK):
                if k + 1 < NBLK:
                    turn(k + 1)
                back(k)

        @block.vector
        def _(dve):
            for k in range(NBLK):
                raw = raw_bank(k).rearrange("p (h c) -> p h c", c=32)
                dve.wait_ge(z.turned, k + 1)
                nc.vector.reciprocal(rec[:, k % 2, :], raw[:, :, HD]).then_inc(z.rec, 1)
                dve.wait_ge(z.rec, k + 1)
                if k >= 4:
                    dve.wait_ge(z.turned_back, k - 3)
                nc.vector.tensor_tensor(on[:, k % 4, :].rearrange("p (h c) -> p h c", c=HD), raw[:, :, 0:HD],
                                        rec[:, k % 2, :].unsqueeze(2).broadcast_to([P, NH, HD]), ALU.mult).then_inc(z.normed, 1)
            for s in range(NSUP):
                xs = m.xC[:, s * SUP:(s + 1) * SUP]
                dve.wait_ge(z.wo_biased, s + 1)
                nc.vector.scalar_tensor_tensor(out=xs, in0=yC[:, s % 2, :], scalar=m.gated(0, 2, s), in1=xs,
                                               op0=ALU.mult, op1=ALU.add).then_inc(z.x_added, 1)

        @block.scalar
        def _(act):
            act.wait_ge(m.ffn_loaded, 16)
            for name in SPLIT:
                nc.scalar.activation(m.ffn_high[name][:, :], ffn_columns(m, name), ACT.Copy).then_inc(z.w_high, 1)
            for s in range(NSUP):
                act.wait_ge(z.turned_back, BLKS * (s + 1))
                nc.scalar.activation(oC[:, s * SUP:(s + 1) * SUP], half(m.bank[1], s), ACT.Identity,
                                     bias=m.a("bv")).then_inc(z.biased, 1)
                act.wait_ge(z.wo_summed, s + 1)
                if s >= 2:
                    act.wait_ge(z.x_added, s - 1)
                nc.scalar.activation(yC[:, s % 2, :], half(m.bank[2], s), ACT.Identity,
                                     bias=m.a("bo")).then_inc(z.wo_biased, 1)



def take_first(m, step, chosen, score, highest, tmp):
    nc = m.nc
    order, pick = tmp[:, 0:NBLK * E].rearrange("p (k e) -> p k e", e=E), tmp[:, NBLK * E:NBLK * E + NBLK]
    over = lambda v: v.unsqueeze(2).broadcast_to([P, NBLK, E])
    step(nc.vector.tensor_tensor(order, score, over(highest), ALU.is_equal))
    step(nc.vector.tensor_tensor(order, order, m.countdown[:, :].unsqueeze(1).broadcast_to([P, NBLK, E]), ALU.mult))
    step(nc.vector.tensor_reduce(pick, order, AX.X, ALU.max))
    step(nc.vector.tensor_tensor(chosen, order, over(pick), ALU.is_equal))


def top_two(m, step, score, highest, tmp):
    nc = m.nc
    ke = lambda i: tmp[:, i * NBLK * E:(i + 1) * NBLK * E].rearrange("p (k e) -> p k e", e=E)
    first, second, rest = ke(0), ke(1), ke(2)
    low, work = tmp[:, 3 * NBLK * E:3 * NBLK * E + NBLK], tmp[:, 4 * NBLK * E:6 * NBLK * E]
    take_first(m, step, first, score, highest, work)
    step(nc.vector.scalar_tensor_tensor(out=rest, in0=first, scalar=NEG, in1=score, op0=ALU.mult, op1=ALU.add))
    step(nc.vector.tensor_reduce(low, rest, AX.X, ALU.max))
    take_first(m, step, second, rest, low, work)
    step(nc.vector.tensor_tensor(first, first, second, ALU.add))
    return first


def split_weights(m, step, rw, parts, rest):
    nc = m.nc
    step(nc.vector.tensor_copy(parts[:, :, 0, :], rw))
    step(nc.vector.tensor_tensor(rest, rw, parts[:, :, 0, :], ALU.subtract))
    step(nc.vector.tensor_copy(parts[:, :, 1, :], rest))
    nc.vector.tensor_tensor(parts[:, :, 2, :], rest, parts[:, :, 1, :], ALU.subtract).then_inc(m.gt.split, 1)


def turned_parts(m, s):
    return m.bank[s].bitcast(BF16)[0:NPART * E, 0:SUP]


def turn_weights(m, pe, parts, call):
    pe.wait_ge(m.gt.split, call + 1)
    for s in range(NSUP):
        for j in range(BLKS):
            mm = m.nc.tensor.transpose(turned_parts(m, s)[:, j * P:(j + 1) * P],
                                       parts[:, s * BLKS + j].rearrange("p a e -> p (a e)"), m.ident16[:, :])
        mm.then_inc(m.gt.splitT, 1)


def copy_weights(m, act, call, also=None):
    for s in range(NSUP):
        act.wait_ge(m.gt.splitT, call * NSUP + s + 1)
        m.nc.scalar.activation(m.rwT[:, s * SUP:(s + 1) * SUP], turned_parts(m, s), ACT.Copy)
        if also is not None:
            m.nc.scalar.activation(also[:, s * SUP:(s + 1) * SUP], turned_parts(m, s), ACT.Copy)


def gate_products(m, pe, nC, weights, sq, call):
    nc, g = m.nc, m.gt
    wide = m.bank[0][:, 0:SUP]
    for s in range(NSUP):
        mm = nc.tensor.matmul(wide[TILE * s:TILE * (s + 1), :], weights, nC[:, s * SUP:(s + 1) * SUP], start=True,
                              stop=sq is None)
    if sq is not None:
        for s in range(NSUP):
            pe.wait_ge(g.sq, call * NSUP + s + 1)
            mm = nc.tensor.matmul(wide[TILE * s:TILE * (s + 1), :], m.one_at_e[:, :], sq[:, s * SUP:(s + 1) * SUP],
                                  start=False, stop=True)
    mm.then_inc(g.logits, 1)
    pe.wait_ge(g.saved, call + 1)
    for j in range(BLKS):
        mm = nc.tensor.transpose(m.bank[1][:, j * P:(j + 1) * P], m.gate_rows[:, j * P:(j + 1) * P], m.ident[:, :])
    mm.then_inc(g.turned, 1)


def save_products(m, act, call):
    act.wait_ge(m.gt.logits, call + 1)
    m.nc.scalar.activation(m.gate_rows[:, :], m.bank[0][:, 0:SUP], ACT.Copy).then_inc(m.gt.saved, 1)


def by_token(m):
    return m.bank[1][:, 0:SUP].rearrange("p (j s c) -> p s j c", j=BLKS, s=NSUP)


def similarity_gating(m, nC, simn, gates, tmp, meanwhile=None):
    nc, g = m.nc, m.gt
    call = m.gt_calls
    m.gt_calls += 1
    at = 0

    def take(width):
        nonlocal at
        at += width
        return tmp[:, at - width:at]

    sq = take(N)
    m.gate_rows = take(SUP)
    KE = NBLK * E
    std, lg, gated, mask, rw = take(NBLK), take(KE), take(KE), take(KE), take(KE)
    mx, top, put = take(NBLK), take(NBLK), take(NBLK)
    parts = take(NPART * KE // 2).bitcast(BF16).rearrange("p (k a e) -> p k a e", k=NBLK, a=NPART)
    rest = take(KE)
    top_tmp = take(6 * KE)
    ke = lambda v: v.rearrange("p (k e) -> p k e", e=E)
    sje = lambda v: v.rearrange("p (s j e) -> p s j e", s=NSUP, j=BLKS)
    over = lambda v: v.unsqueeze(2).broadcast_to([P, NBLK, E])
    with nc.Block() as block:
        @block.scalar
        def _(act):
            for s in range(NSUP):
                nc.scalar.activation(sq[:, s * SUP:(s + 1) * SUP], nC[:, s * SUP:(s + 1) * SUP], ACT.Square).then_inc(g.sq, 1)
            save_products(m, act, call)
            act.wait_ge(g.turned, call + 1)
            nc.scalar.activation(std.rearrange("p (s j) -> p s j", j=BLKS), by_token(m)[:, :, :, E],
                                 ACT.Sqrt).then_inc(g.act_out, 1)
            nc.scalar.preload_act_table(ACT.Exp)
            act.wait_ge(g.act_in, call + 1)
            nc.scalar.activation(rw, gated, ACT.Exp).then_inc(g.act_out, 1)
            copy_weights(m, act, call)

        @block.tensor
        def _(pe):
            gate_products(m, pe, nC, simn, sq, call)
            turn_weights(m, pe, parts, call)

        @block.vector
        def _(dve):
            step = m.dve.on(dve)
            if meanwhile is not None:
                meanwhile(dve)
            dve.wait_ge(g.act_out, 2 * call + 1)
            step(nc.vector.tensor_scalar(std, std, 1e-12, None, ALU.max))
            step(nc.vector.reciprocal(std, std))
            rstd = std.rearrange("p (s j) -> p s j", j=BLKS).unsqueeze(3).broadcast_to([P, NSUP, BLKS, E])
            step(nc.vector.tensor_tensor(sje(lg), by_token(m)[:, :, :, 0:E], rstd, ALU.mult))
            step(nc.vector.tensor_tensor(ke(lg), ke(lg), gates.unsqueeze(1).broadcast_to([P, NBLK, E]), ALU.subtract))
            step(nc.vector.tensor_reduce(mx, ke(lg), AX.X, ALU.max))
            step(nc.vector.tensor_scalar(gated, lg, 0.0, None, ALU.max))
            step(nc.vector.tensor_scalar(top, mx, 0.0, None, ALU.max))
            nc.vector.tensor_tensor(ke(gated), ke(gated), over(top), ALU.subtract).then_inc(g.act_in, 1)
            chosen = top_two(m, step, ke(lg), mx, top_tmp)
            step(nc.vector.tensor_scalar(mask, lg, 0.0, None, ALU.is_gt))
            step(nc.vector.tensor_scalar(put, mx, 0.0, None, ALU.is_le))
            step(nc.vector.tensor_tensor(chosen, chosen, over(put), ALU.mult))
            step(nc.vector.tensor_tensor(ke(mask), ke(mask), chosen, ALU.max))
            dve.wait_ge(g.act_out, 2 * call + 2)
            step(nc.vector.tensor_tensor(rw, rw, mask, ALU.mult))
            step(nc.vector.tensor_reduce(mx, ke(rw), AX.X, ALU.add))
            step(nc.vector.reciprocal(mx, mx))
            step(nc.vector.tensor_tensor(ke(rw), ke(rw), over(mx), ALU.mult))
            split_weights(m, step, ke(rw), parts, ke(rest))



def ffn_columns(m, name):
    at, w = FFN_COLS[name]
    return m.ffn[:, at:at + w]


def feed_forward(m):
    nc = m.nc
    sup = lambda tile: (lambda s: tile[:, s * SUP:(s + 1) * SUP])

    def tile(stack, name, width, dt=F32):
        return stack.enter_context(nc.sbuf_tensor(name, [P, width], dt))

    m.ffn_high, m.ffn_low = {}, {}

    def take_parts(stack, names):
        for name in names:
            m.ffn_high[name] = tile(stack, name + "_high", E * D, F32R)
            m.ffn_low[name] = tile(stack, name + "_low", E * D, F32R)

    def parts(name, e):
        return m.ffn_high[name][:, e * D:(e + 1) * D], m.ffn_low[name][:, e * D:(e + 1) * D]

    m.f_parts = parts
    tmp = m.ffn[:, 0:FFN_COLS["op"][0]]
    with ExitStack() as outer:
        m.hC = tile(outer, "ffn_h", N)
        take_parts(outer, ("w1", "w2"))
        with ExitStack() as attention:
            qkv = tile(attention, "ffn_qkv", 3 * N)
            m.qT, m.kT, m.vS = (qkv[:, i * N:(i + 1) * N] for i in range(3))
            with ExitStack() as projections:
                m.nC = tile(projections, "ffn_n1", N)
                take_parts(projections, ("qp", "kp", "vp"))
                XB = 3
                x_parts = [tile(projections, name, XB * SUP, F32R) for name in ("scaled_n1_high", "scaled_n1_low")]
                attention_output(m, qkv)
                m.arena = tmp
                layer_norm(m, m.xC, sup(m.hC), lambda s: m.scale1(0, 4, s), lambda s: m.shift(0, 3, s), tmp=0)
                layer_norm(m, m.hC, sup(m.nC), lambda s: m.a("ln1w"), lambda s: m.a("ln1b"), tmp=0,
                           queue=lambda sp: load_layer1(m, sp))
                similarity_gating(m, m.nC, m.sims[:, 0:TILE], m.rowg[:, 0:E], tmp)
                routed_projections(m, tmp, XB, *x_parts)
            with nc.sbuf_tensor("ffn_a", [P, N], F32) as m.aC:
                causal_attention(m, tmp)
                routed_output(m, tmp)
        m.nC = tile(outer, "ffn_n2", N)
        n_high, n_low = tile(outer, "n2_high", N, F32R), tile(outer, "n2_low", N, F32R)
        XB = 4
        x_parts = [tile(outer, name, XB * SUP, F32R) for name in ("scaled_high", "scaled_low")]
        layer_norm(m, m.hC, sup(m.nC), lambda s: m.a("ln2w"), lambda s: m.a("ln2b"), tmp=0, high=sup(n_high))
        similarity_gating(m, m.nC, m.sims[:, TILE:2 * TILE], m.rowg[:, E:2 * E], tmp,
                          lambda dve: nc.vector.tensor_tensor(n_low[:, :], m.nC[:, :], n_high[:, :], ALU.subtract))
        routed_mlp(m, n_high, n_low, tmp, XB, *x_parts)


def load_layer1(m, sp):
    sp.dma_start(m.late[:, :], m.l1_in).then_inc(m.l1_loaded, 16)


def spread(m, out, e, s):
    return m.nc.tensor.matmul(out, m.sel_e[:, e, :], m.rwT[:, bass.ds(s * SUP, SUP)], start=True, stop=True)


def routed_projections(m, tmp, XB, x_high, x_low):
    nc = m.nc
    names = ("spread", "scaled", "high", "low", "used", "q_done", "k_done", "q_free", "k_free", "v_saved", "v_turned",
             "v_free")
    z = semaphores(m.sem, "rp_", names)
    xe, high, low = (v[:, 0:XB * SUP].rearrange("p (u c) -> p u c", u=XB) for v in (tmp, x_high, x_low))
    vT = tmp[:, XB * SUP:(XB + 2) * SUP].rearrange("p (u c) -> p u c", u=2)
    wB = [m.bank[0][:, 0:SUP], m.bank[0][:, SUP:2 * SUP]]
    acc = lambda i, s: m.bank[1 + i][:, (s % 2) * SUP:(s % 2 + 1) * SUP]
    sup = lambda tile, s: tile[:, s * SUP:(s + 1) * SUP]
    STEPS = NSUP * E
    with nc.Block() as block:
        @block.tensor
        def _(pe):
            def spread_for(c):
                if c >= 2:
                    pe.wait_ge(z.scaled, c - 1)
                spread(m, wB[c % 2], c % E, c // E).then_inc(z.spread, 1)

            def turn_v(s):
                pe.wait_ge(z.v_saved, s + 1)
                for j in range(BLKS):
                    mm = nc.tensor.transpose(acc(2, s)[:, j * P:(j + 1) * P], vT[:, s % 2, j * P:(j + 1) * P], m.ident[:, :])
                mm.then_inc(z.v_turned, 1)

            spread_for(0)
            spread_for(1)
            for c in range(STEPS):
                s, e = divmod(c, E)
                if e == 0 and s >= 2:
                    pe.wait_ge(z.q_free, s - 1)
                    pe.wait_ge(z.k_free, s - 1)
                    pe.wait_ge(z.v_free, s - 1)
                pe.wait_ge(z.low, c + 1)
                first, last = e == 0, e == E - 1
                if c + 2 < STEPS:
                    spread_for(c + 2)
                x = (high[:, c % XB, :], low[:, c % XB, :])
                q = three_passes(m, acc(0, s), *m.f_parts("qp", e), *x, first, last)
                k = three_passes(m, acc(1, s), *m.f_parts("kp", e), *x, first, last)
                if last:
                    q.then_inc(z.q_done, 1)
                    k.then_inc(z.k_done, 1)
                three_passes(m, acc(2, s), *m.f_parts("vp", e), *x, first, last).then_inc(z.used, 1)
                if s and e == 2:
                    turn_v(s - 1)
            turn_v(NSUP - 1)

        @block.vector
        def _(dve):
            def copy_out(s):
                dve.wait_ge(z.q_done, s + 1)
                nc.vector.tensor_copy(sup(m.qT, s), acc(0, s)).then_inc(z.q_free, 1)

            def copy_v(s):
                dve.wait_ge(z.v_turned, s + 1)
                nc.vector.tensor_copy(sup(m.vS, s), acc(2, s)).then_inc(z.v_free, 1)

            for c in range(STEPS + 1):
                s, e = divmod(c, E)
                if c < STEPS:
                    dve.wait_ge(z.spread, c + 1)
                    if c >= XB:
                        dve.wait_ge(z.high, c - XB + 1)
                    nc.vector.tensor_tensor(xe[:, c % XB, :], sup(m.nC, s), wB[c % 2], ALU.mult).then_inc(z.scaled, 1)
                if c:
                    d = c - 1
                    dve.wait_ge(z.high, d + 1)
                    nc.vector.tensor_tensor(low[:, d % XB, :], xe[:, d % XB, :], high[:, d % XB, :],
                                            ALU.subtract).then_inc(z.low, 1)
                if s and s < NSUP and e == 2:
                    copy_out(s - 1)
                if s and s < NSUP and e == 5:
                    copy_v(s - 1)
            copy_out(NSUP - 1)
            copy_v(NSUP - 1)

        @block.scalar
        def _(act):
            def copy_out(s):
                act.wait_ge(z.used, E * (s + 1))
                nc.scalar.activation(vT[:, s % 2, :], acc(2, s), ACT.Copy).then_inc(z.v_saved, 1)
                act.wait_ge(z.k_done, s + 1)
                nc.scalar.activation(sup(m.kT, s), acc(1, s), ACT.Copy).then_inc(z.k_free, 1)

            for c in range(STEPS):
                s, e = divmod(c, E)
                if c >= XB:
                    act.wait_ge(z.used, c - XB + 1)
                act.wait_ge(z.scaled, c + 1)
                nc.scalar.activation(high[:, c % XB, :], xe[:, c % XB, :], ACT.Copy).then_inc(z.high, 1)
                if s and e == 1:
                    copy_out(s - 1)
            copy_out(NSUP - 1)


def causal_attention(m, tmp):
    nc = m.nc
    names = ("scored", "maxed", "negmax", "exped", "normed", "turned", "copied", "summed", "saved")
    z = semaphores(m.sem, "ca_", names)
    p = tmp[:, 0:2 * T].rearrange("p (u k) -> p u k", u=2)
    pT = tmp[:, 2 * T:4 * T].rearrange("p (u k) -> p u k", u=2)
    col = tmp[:, 4 * T:4 * T + 8]
    mx, nm, l, rl = (col[:, 2 * i:2 * i + 2] for i in range(4))
    scale = float(D) ** -0.5
    score = lambda n: m.bank[n % 2]
    turn = m.bank[2]
    out = lambda n: m.bank[3][:, (n % 2) * SUP:(n % 2) * SUP + P]
    halves_of = lambda w: [(a, min(a + SUP, w)) for a in range(0, w, SUP)]
    copies = [0]
    for n in range(NBLK):
        copies.append(copies[-1] + len(halves_of((n % QB + 1) * P)))
    with nc.Block() as block:
        @block.tensor
        def _(pe):
            def scores(n):
                b, i = divmod(n, QB)
                if n >= 2:
                    pe.wait_ge(z.exped, n - 1)
                for a, c in halves_of((i + 1) * P):
                    mm = nc.tensor.matmul(score(n)[:, a:c], m.qT[:, n * P:(n + 1) * P], m.kT[:, b * T + a:b * T + c],
                                          start=True, stop=True)
                mm = nc.tensor.matmul(score(n)[:, i * P:(i + 1) * P], m.ident16[:, :], m.causal16[:, :], start=False, stop=True,
                                      skip_group_check=True)
                mm.then_inc(z.scored, 1)

            def turns(n):
                b, i = divmod(n, QB)
                pe.wait_ge(z.normed, n + 1)
                for h, (a, c) in enumerate(halves_of((i + 1) * P)):
                    if n:
                        last = copies[n] if h == 0 or copies[n] - copies[n - 1] == 2 else copies[n]
                        pe.wait_ge(z.copied, last)
                    for k in range(a, c, P):
                        mm = nc.tensor.transpose(turn[:, k:k + P], p[:, n % 2, k:k + P], m.ident[:, :])
                    mm.then_inc(z.turned, 1)

            def values(n):
                b, i = divmod(n, QB)
                pe.wait_ge(z.copied, copies[n + 1])
                if n >= 2:
                    pe.wait_ge(z.saved, n - 1)
                for kb in range(i + 1):
                    mm = nc.tensor.matmul(out(n), m.vS[:, (b * QB + kb) * P:(b * QB + kb + 1) * P],
                                          pT[:, n % 2, kb * P:(kb + 1) * P], start=(kb == 0), stop=(kb == i))
                mm.then_inc(z.summed, 1)

            scores(0)
            scores(1)
            for n in range(NBLK):
                if n + 2 < NBLK:
                    scores(n + 2)
                turns(n)
                if n:
                    values(n - 1)
            values(NBLK - 1)

        @block.vector
        def _(dve):
            def top(n):
                w = (n % QB + 1) * P
                dve.wait_ge(z.scored, n + 1)
                nc.vector.tensor_reduce(mx[:, n % 2:n % 2 + 1], score(n)[:, 0:w], AX.X, ALU.max).then_inc(z.maxed, 1)
                dve.wait_ge(z.maxed, n + 1)
                nc.vector.tensor_scalar(nm[:, n % 2:n % 2 + 1], mx[:, n % 2:n % 2 + 1], -scale, None,
                                        ALU.mult).then_inc(z.negmax, 1)

            step = m.dve.on(dve)
            top(0)
            for n in range(NBLK):
                w = (n % QB + 1) * P
                if n + 1 < NBLK:
                    top(n + 1)
                dve.wait_ge(z.exped, n + 1)
                step(nc.vector.reciprocal(rl[:, n % 2:n % 2 + 1], l[:, n % 2:n % 2 + 1]))
                nc.vector.tensor_scalar(p[:, n % 2, 0:w], p[:, n % 2, 0:w], rl[:, n % 2:n % 2 + 1], None,
                                        ALU.mult).then_inc(z.normed, 1)

        @block.scalar
        def _(act):
            def exps(n):
                w = (n % QB + 1) * P
                act.wait_ge(z.negmax, n + 1)
                if n >= 2:
                    act.wait_ge(z.turned, copies[n - 1])
                nc.scalar.activation(p[:, n % 2, 0:w], score(n)[:, 0:w], ACT.Exp, bias=nm[:, n % 2:n % 2 + 1],
                                     scale=scale, accum_out=l[:, n % 2:n % 2 + 1]).then_inc(z.exped, 1)

            def copy(n):
                if n >= 2:
                    act.wait_ge(z.summed, n - 1)
                for h, (a, c) in enumerate(halves_of((n % QB + 1) * P)):
                    act.wait_ge(z.turned, copies[n] + h + 1)
                    nc.scalar.activation(pT[:, n % 2, a:c], turn[:, a:c], ACT.Copy).then_inc(z.copied, 1)

            def save(n):
                act.wait_ge(z.summed, n + 1)
                nc.scalar.activation(m.aC[:, n * P:(n + 1) * P], out(n), ACT.Copy).then_inc(z.saved, 1)

            exps(0)
            for n in range(NBLK):
                if n + 1 < NBLK:
                    exps(n + 1)
                copy(n)
                if n:
                    save(n - 1)
            save(NBLK - 1)


def routed_output(m, tmp):
    nc = m.nc
    z = semaphores(m.sem, "ro_", ("spread", "scaled", "used", "added"))
    XB = 4
    xe = tmp[:, 0:XB * SUP].rearrange("p (u c) -> p u c", u=XB)
    wB = [m.bank[i // 2][:, (i % 2) * SUP:(i % 2 + 1) * SUP] for i in range(XB)]
    acc = lambda s: m.bank[2][:, (s % 2) * SUP:(s % 2 + 1) * SUP]
    sup = lambda tile, s: tile[:, s * SUP:(s + 1) * SUP]
    STEPS = NSUP * E
    with nc.Block() as block:
        @block.tensor
        def _(pe):
            def spread_for(c):
                if c >= XB:
                    pe.wait_ge(z.scaled, c - XB + 1)
                spread(m, wB[c % XB], c % E, c // E).then_inc(z.spread, 1)

            spread_for(0)
            spread_for(1)
            for c in range(STEPS):
                s, e = divmod(c, E)
                if c + 2 < STEPS:
                    spread_for(c + 2)
                pe.wait_ge(z.scaled, c + 1)
                if e == 0 and s >= 2:
                    pe.wait_ge(z.added, s - 1)
                nc.tensor.matmul(acc(s), ffn_columns(m, "op")[:, e * D:(e + 1) * D], xe[:, c % XB, :], start=(e == 0),
                                 stop=(e == E - 1)).then_inc(z.used, 1)

        @block.vector
        def _(dve):
            def add(s):
                dve.wait_ge(z.used, E * (s + 1))
                nc.vector.tensor_tensor(sup(m.hC, s), sup(m.hC, s), acc(s), ALU.add).then_inc(z.added, 1)

            for c in range(STEPS):
                s, e = divmod(c, E)
                if c >= XB:
                    dve.wait_ge(z.used, c - XB + 1)
                dve.wait_ge(z.spread, c + 1)
                nc.vector.tensor_tensor(xe[:, c % XB, :], sup(m.aC, s), wB[c % XB], ALU.mult).then_inc(z.scaled, 1)
                if s and e == 3:
                    add(s - 1)
            add(NSUP - 1)


def routed_mlp(m, n_high, n_low, tmp, XB, x_high, x_low):
    nc = m.nc
    names = ("up", "gelu", "spread", "scaled", "high", "low", "used", "summed", "added")
    z = semaphores(m.sem, "rm_", names)
    LAG = 3
    gelu, scaled, high, low = (v[:, 0:XB * SUP].rearrange("p (u c) -> p u c", u=XB)
                               for v in (tmp, tmp[:, XB * SUP:2 * XB * SUP], x_high, x_low))
    yh = tmp[:, 2 * XB * SUP:(2 * XB + 2) * SUP].rearrange("p (u c) -> p u c", u=2)
    wB = [m.bank[i // 2][:, (i % 2) * SUP:(i % 2 + 1) * SUP] for i in range(2)]
    up = [m.bank[1][:, 0:SUP], m.bank[1][:, SUP:2 * SUP], m.bank[2][:, 0:SUP]]
    UB = len(up)
    acc = lambda s: m.bank[3][:, (s % 2) * SUP:(s % 2 + 1) * SUP]
    sup = lambda tile, s: tile[:, s * SUP:(s + 1) * SUP]
    STEPS = NSUP * E
    with nc.Block() as block:
        @block.tensor
        def _(pe):
            for c in range(STEPS + LAG):
                if c < STEPS:
                    s, e = divmod(c, E)
                    if c >= 2:
                        pe.wait_ge(z.scaled, c - 1)
                    spread(m, wB[c % 2], e, s).then_inc(z.spread, 1)
                    if c >= UB:
                        pe.wait_ge(z.gelu, c - UB + 1)
                    three_passes(m, up[c % UB], *m.f_parts("w1", e), sup(n_high, s), sup(n_low, s), True,
                                 True).then_inc(z.up, 1)
                if c >= LAG:
                    d = c - LAG
                    s, e = divmod(d, E)
                    pe.wait_ge(z.low, d + 1)
                    if e == 0 and s >= 2:
                        pe.wait_ge(z.summed, s - 1)
                    three_passes(m, acc(s), *m.f_parts("w2", e), high[:, d % XB, :], low[:, d % XB, :], e == 0,
                                 e == E - 1).then_inc(z.used, 1)

        @block.scalar
        def _(act):
            nc.scalar.preload_act_table(ACT.Gelu)
            for c in range(STEPS + 1):
                if c < STEPS:
                    if c >= XB:
                        act.wait_ge(z.scaled, c - XB + 1)
                    act.wait_ge(z.up, c + 1)
                    nc.scalar.activation(gelu[:, c % XB, :], up[c % UB], ACT.Gelu).then_inc(z.gelu, 1)
                if c:
                    d = c - 1
                    if d >= XB:
                        act.wait_ge(z.used, d - XB + 1)
                    act.wait_ge(z.scaled, d + 1)
                    nc.scalar.activation(high[:, d % XB, :], scaled[:, d % XB, :], ACT.Copy).then_inc(z.high, 1)

        @block.vector
        def _(dve):
            def finish(s):
                dve.wait_ge(z.used, E * (s + 1))
                nc.vector.tensor_tensor(yh[:, s % 2, :], acc(s), sup(m.hC, s), ALU.add).then_inc(z.summed, 1)
                dve.wait_ge(z.summed, s + 1)
                nc.vector.scalar_tensor_tensor(out=sup(m.xC, s), in0=yh[:, s % 2, :], scalar=m.gated(0, 5, s),
                                               in1=sup(m.xC, s), op0=ALU.mult, op1=ALU.add).then_inc(z.added, 1)

            for c in range(STEPS + 1):
                s, e = divmod(c, E)
                if c < STEPS:
                    dve.wait_ge(z.spread, c + 1)
                    dve.wait_ge(z.gelu, c + 1)
                    nc.vector.tensor_tensor(scaled[:, c % XB, :], gelu[:, c % XB, :], wB[c % 2], ALU.mult).then_inc(z.scaled, 1)
                if c:
                    d = c - 1
                    dve.wait_ge(z.high, d + 1)
                    nc.vector.tensor_tensor(low[:, d % XB, :], scaled[:, d % XB, :], high[:, d % XB, :],
                                            ALU.subtract).then_inc(z.low, 1)
                if s and s < NSUP and e == 4:
                    finish(s - 1)
            finish(NSUP - 1)



def mixer(m):
    nc, ar = m.nc, m.arena
    fr = ar[:, 25552:]
    PAD = 4
    W = PAD + T
    at = 0

    def take(width):
        nonlocal at
        at += width
        return ar[:, at - width:at]

    halves = lambda v: v.rearrange("p (h t) -> p h t", h=HALVES)
    t = Shared()
    t.W, t.PAD = W, PAD
    t.h = take(N)
    t.xs, t.sz, t.dt, t.u = (halves(take(HALVES * N)) for _ in range(4))
    t.dA = take(HALVES * T).rearrange("p (h t) -> p h t", h=HALVES)
    t.g = take(2 * HALVES * T).rearrange("p (u h t) -> p u h t", u=2, h=HALVES)
    t.scratch = ar[:, at - 6 * T:at]
    t.A, t.wrep, t.diag = take(HALVES * DS), take(HALVES * P), take(HALVES * P)
    assert at <= ar.shape[1], at
    t.sel = m.sel_n
    t.stack = fr[0:NPART * 2 * DS, 2048:2048 + N // 2].bitcast(BF16)
    t.Cs = fr[:, 3072:3072 + 2 * T].rearrange("p (u t) -> p u t", u=2)
    t.xpad = t.scratch[:, 0:B * HALVES * W].rearrange("p (b h t) -> p b h t", b=B, h=HALVES)
    t.tmp = 2 * N

    mixer_constants(m, t)
    layer_norm(m, m.xC, lambda s: t.h[:, s * SUP:(s + 1) * SUP],
               lambda s: m.scale1(1, 1, s), lambda s: m.shift(1, 0, s), tmp=t.tmp + 4096)
    mixer_input(m, t)
    mixer_steps(m, t)
    selective_scan(m, t)
    mixer_output(m, t)


def mixer_constants(m, t):
    nc = m.nc
    exped = m.sem("a_exped")
    with nc.Block() as block:
        @block.gpsimd
        def _(pool):
            nc.gpsimd.memset(t.xpad[:, :, :, 0:t.PAD], 0.0)

        @block.scalar
        def _(act):
            act.wait_ge(m.l1_loaded, 16)
            nc.scalar.activation(t.A, m.l("a_log"), ACT.Exp).then_inc(exped, 1)

        @block.vector
        def _(dve):
            dve.wait_ge(m.l1_loaded, 16)
            for h in range(HALVES):
                nc.vector.tensor_copy(t.wrep[:, h * P:(h + 1) * P],
                                      m.l("w_x")[:, h * (2 * DS + 1):h * (2 * DS + 1) + 1].broadcast_to([P, P]))
                nc.vector.tensor_scalar(t.diag[:, h * P:(h + 1) * P], m.ident[:, :], m.l("dskip")[:, h:h + 1], None,
                                        ALU.mult)
            dve.wait_ge(exped, 1)
            nc.vector.tensor_scalar(t.A, t.A, -1.0, None, ALU.mult)


def mixer_input(m, t):
    nc = m.nc
    z = semaphores(m.sem, "mi_", ("x_done", "x_saved", "z_done", "tapped", "convolved"))
    ps = lambda i, s: m.bank[i][:, (s % 2) * SUP:(s % 2 + 1) * SUP]
    with nc.Block() as block:
        @block.tensor
        def _(pe):
            for b in range(B):
                for first, done in ((0, z.x_done), (HALVES, z.z_done)):
                    for h in range(HALVES):
                        if b:
                            pe.wait_ge(z.x_saved, (2 * (b - 1) + first // HALVES) * HALVES + h + 1)
                        for par in range(SUPB):
                            s = b * SUPB + par
                            mm = nc.tensor.matmul(ps(first + h, s), m.l("w_in")[:, (first + h) * P:(first + h + 1) * P],
                                                  t.h[:, s * SUP:(s + 1) * SUP], start=True, stop=True)
                        mm.then_inc(done, 1)

        @block.scalar
        def _(act):
            def activate(b, h):
                act.wait_ge(z.convolved, HALVES * b + h + 1)
                nc.scalar.activation(t.xs[:, h, b * T:(b + 1) * T], t.xs[:, h, b * T:(b + 1) * T], ACT.Silu,
                                     bias=m.l("b_conv")[:, h:h + 1])

            nc.scalar.preload_act_table(ACT.Silu)
            for b in range(B):
                for h in range(HALVES):
                    act.wait_ge(z.x_done, HALVES * b + h + 1)
                    w = m.l("w_conv")[:, (h + 1) * KC - 1:(h + 1) * KC]
                    nc.scalar.activation(t.xs[:, h, b * T:(b + 1) * T], m.bank[h][:, :], ACT.Copy, scale=w)
                    nc.scalar.activation(t.xpad[:, b, h, t.PAD:], m.bank[h][:, :], ACT.Copy).then_inc(z.x_saved, 1)
                for h in range(HALVES):
                    act.wait_ge(z.z_done, HALVES * b + h + 1)
                    nc.scalar.activation(t.sz[:, h, b * T:(b + 1) * T], m.bank[HALVES + h][:, :],
                                         ACT.Silu).then_inc(z.x_saved, 1)
            for b in range(B):
                for h in range(HALVES):
                    activate(b, h)

        @block.vector
        def _(dve):
            for b in range(B):
                for h in range(HALVES):
                    dve.wait_ge(z.x_saved, 2 * HALVES * b + h + 1)
                    out = t.xs[:, h, b * T:(b + 1) * T]
                    for k in range(KC - 1):
                        at = t.PAD - (KC - 1) + k
                        if k:
                            dve.wait_ge(z.tapped, (HALVES * b + h) * (KC - 2) + k)
                        nc.vector.scalar_tensor_tensor(
                            out=out, in0=t.xpad[:, b, h, at:at + T], scalar=m.l("w_conv")[:, h * KC + k:h * KC + k + 1],
                            in1=out, op0=ALU.mult, op1=ALU.add).then_inc(z.convolved if k == KC - 2 else z.tapped, 1)


def mixer_steps(m, t):
    nc = m.nc
    names = ("dt_raw", "affine", "abs", "logged", "bc_done", "first", "rest", "second", "third", "dt_free")
    z = semaphores(m.sem, "ms_", names)
    ps = lambda i, par: m.bank[i][:, par * SUP:(par + 1) * SUP]
    v = t.scratch[:, 0:HALVES * SUP * 2].rearrange("p (u h c) -> p u h c", u=2, h=HALVES)
    low = t.scratch[0:2 * DS, 2048:2048 + 2048]
    rest, part2, part3 = low[:, 0:SUP], low[:, SUP:SUP + SUP // 2].bitcast(BF16), low[:, 2 * SUP:2 * SUP + SUP // 2].bitcast(BF16)
    R = 2 * DS
    sup = lambda tile, s: tile[:, s * SUP:(s + 1) * SUP]
    with nc.Block() as block:
        @block.tensor
        def _(pe):
            for s in range(NSUP):
                par = s % 2
                if s >= 2:
                    pe.wait_ge(z.affine, s - 1)
                    pe.wait_ge(z.rest, s - 1)
                for h in range(HALVES):
                    mm = nc.tensor.matmul(ps(0, par), t.wrep[:, h * P:(h + 1) * P], sup(t.xs[:, h], s), start=(h == 0),
                                          stop=(h == HALVES - 1))
                mm.then_inc(z.dt_raw, 1)
                for h in range(HALVES):
                    c = h * (R + 1) + 1
                    mm = nc.tensor.matmul(ps(1, par)[0:R, :], m.l("w_x")[:, c:c + R], sup(t.xs[:, h], s), start=(h == 0),
                                          stop=(h == HALVES - 1))
                mm.then_inc(z.bc_done, 1)

        @block.vector
        def _(dve):
            def finish(s):
                dve.wait_ge(z.logged, s + 1)
                d = t.dt[:, :, s * SUP:(s + 1) * SUP]
                nc.vector.scalar_tensor_tensor(out=d, in0=d, scalar=0.0, in1=v[:, s % 2], op0=ALU.max,
                                               op1=ALU.add).then_inc(z.dt_free, 1)
                dve.wait_ge(z.dt_free, s + 1)
                nc.vector.tensor_tensor(t.u[:, :, s * SUP:(s + 1) * SUP], d, t.xs[:, :, s * SUP:(s + 1) * SUP], ALU.mult)

            for s in range(NSUP):
                par = s % 2
                dve.wait_ge(z.dt_raw, s + 1)
                for h in range(HALVES):
                    ins = nc.vector.tensor_scalar(sup(t.dt[:, h], s), ps(0, par), m.l("w_dt")[:, h:h + 1],
                                                  m.l("b_dt")[:, h:h + 1], ALU.mult, ALU.add)
                ins.then_inc(z.affine, 1)
                dve.wait_ge(z.bc_done, s + 1)
                if s:
                    dve.wait_ge(z.third, 2 * s)
                nc.vector.tensor_copy(sup(t.stack[0:R], s), ps(1, par)[0:R, :]).then_inc(z.first, 1)
                dve.wait_ge(z.first, s + 1)
                nc.vector.tensor_tensor(rest, ps(1, par)[0:R, :], sup(t.stack[0:R], s), ALU.subtract).then_inc(z.rest, 1)
                dve.wait_ge(z.rest, s + 1)
                nc.vector.tensor_copy(part2, rest).then_inc(z.second, 1)
                dve.wait_ge(z.second, 2 * s + 1)
                nc.vector.tensor_tensor(part3, rest, part2, ALU.subtract).then_inc(z.second, 1)
                if s:
                    finish(s - 1)
            finish(NSUP - 1)

        @block.scalar
        def _(act):
            nc.scalar.preload_act_table_set("natural_log_exp_and_others")
            for s in range(NSUP):
                par = s % 2
                d = t.dt[:, :, s * SUP:(s + 1) * SUP]
                step = m.act.on(act)
                act.wait_ge(z.affine, s + 1)
                if s >= 2:
                    act.wait_ge(z.dt_free, s - 1)
                step(nc.scalar.activation(v[:, par], d, ACT.Abs))
                step(nc.scalar.activation(v[:, par], v[:, par], ACT.Exp, scale=-1.0))
                nc.scalar.activation(v[:, par], v[:, par], ACT.Ln, bias=m.ones[:, 0:1]).then_inc(z.logged, 1)
                act.wait_ge(z.second, 2 * s + 2)
                nc.scalar.activation(sup(t.stack[R:2 * R], s), part2, ACT.Copy).then_inc(z.third, 1)
                nc.scalar.activation(sup(t.stack[2 * R:3 * R], s), part3, ACT.Copy).then_inc(z.third, 1)


def selective_scan(m, t):
    nc = m.nc
    names = ("b_spread", "c_spread", "b_used", "c_saved", "decayed", "scanned", "weighted", "y_added", "driven",
             "y_gated")
    z = semaphores(m.sem, "ss_", names)
    psB, psC = m.bank[0], m.bank[1]
    y = [m.bank[2], m.bank[3]]
    PAIRS = DS // 2
    halves_of = [(h, h * SUP, (h + 1) * SUP) for h in range(SUPB)]
    AHEAD = 4
    with nc.Block() as block:
        @block.tensor
        def _(pe):
            for b in range(B):
                def spread_b(b, n):
                    k = b * DS + n
                    pe.wait_ge(z.b_used, AHEAD + 2 * k)
                    apart(pe)
                    for _, a, c in halves_of:
                        mm = nc.tensor.matmul(psB[:, a:c], t.sel[:, n, :], t.stack[:, b * T + a:b * T + c], start=True, stop=True)
                    mm.then_inc(z.b_spread, 1)

                def spread_c(b, n):
                    k = b * DS + n
                    pe.wait_ge(z.c_saved, AHEAD + k)
                    apart(pe)
                    for _, a, c in halves_of:
                        mm = nc.tensor.matmul(psC[:, a:c], t.sel[:, n + DS, :], t.stack[:, b * T + a:b * T + c], start=True,
                                              stop=True)
                    mm.then_inc(z.c_spread, 1)

                def add_y(n, par, h, last=False):
                    pe.wait_ge(z.weighted, AHEAD + 2 * (b * DS + n) + h + 1)
                    for _, a, c in halves_of:
                        mm = nc.tensor.matmul(y[h][:, a:c], m.ident[:, :], t.g[:, par, h, a:c], start=False, stop=last)
                    mm.then_inc(z.y_added, 1)

                if b:
                    pe.wait_ge(z.y_gated, HALVES * b)
                else:
                    for n in range(2):
                        spread_b(b, n)
                        spread_c(b, n)
                for h in range(HALVES):
                    for _, a, c in halves_of:
                        nc.tensor.matmul(y[h][:, a:c], t.diag[:, h * P:(h + 1) * P], t.xs[:, h, b * T + a:b * T + c],
                                         start=True, stop=False)
                with pe.Fori(0, PAIRS - 1) as mm_:
                    for par in range(2):
                        n = 2 * mm_ + par
                        add_y(n, par, 0)
                        spread_b(b, n + 2)
                        spread_c(b, n + 2)
                        add_y(n, par, 1)
                for par in range(2):
                    last = par == 1
                    add_y(DS - 2 + par, par, 0, last)
                    if b + 1 < B:
                        spread_b(b + 1, par)
                        spread_c(b + 1, par)
                    add_y(DS - 2 + par, par, 1, last)

        @block.scalar
        def _(act):
            prime(act, z.c_saved, count=AHEAD)
            nc.scalar.preload_act_table(ACT.Exp)
            for b in range(B):
                with act.Fori(0, PAIRS) as mm_:
                    for par in range(2):
                        n = 2 * mm_ + par
                        k = b * DS + n
                        for h in range(HALVES):
                            act.wait_ge(z.scanned, AHEAD + 2 * k - 1 + h)
                            apart(act)
                            nc.scalar.activation(t.dA[:, h, :], t.dt[:, h, b * T:(b + 1) * T], ACT.Exp,
                                                 scale=t.A[:, bass.ds(h * DS + n, 1)]).then_inc(z.decayed, 1)
                            if h == 0:
                                act.wait_ge(z.c_spread, k + 1)
                                act.wait_ge(z.weighted, AHEAD + 2 * k - 2)
                                nc.scalar.activation(t.Cs[:, par, :], psC[:, :], ACT.Copy).then_inc(z.c_saved, 1)

        @block.vector
        def _(dve):
            prime(dve, z.b_used, z.scanned, count=AHEAD)

            def state(b, n, par):
                k = b * DS + n
                for h in range(HALVES):
                    dve.wait_ge(z.y_added, AHEAD + 2 * k + h - 3)
                    dve.wait_ge(z.b_spread, k + 1)
                    nc.vector.tensor_tensor(t.g[:, par, h, :], psB[:, :], t.u[:, h, b * T:(b + 1) * T],
                                            ALU.mult).then_inc(z.b_used, 1)
                for h in range(HALVES):
                    g = t.g[:, par, h, :]
                    dve.wait_ge(z.b_used, AHEAD + 2 * k + h + 1)
                    dve.wait_ge(z.decayed, 2 * k + h + 1)
                    nc.vector.tensor_tensor_scan(g, t.dA[:, h, :], g, 0.0, ALU.mult, ALU.add).then_inc(z.scanned, 1)

            def gate_y(b):
                for h in range(HALVES):
                    szb = t.sz[:, h, b * T:(b + 1) * T]
                    dve.wait_ge(z.y_added, AHEAD + HALVES * DS * (b + 1))
                    nc.vector.tensor_tensor(szb, y[h][:, :], szb, ALU.mult).then_inc(z.y_gated, 1)

            for b in range(B):
                if b:
                    state(b, 0, 0)
                    gate_y(b - 1)
                    state(b, 1, 1)
                with dve.Fori(1 if b else 0, PAIRS) as mm_:
                    for par in range(2):
                        state(b, 2 * mm_ + par, par)
            gate_y(B - 1)

        @block.gpsimd
        def _(pool):
            prime(pool, z.weighted, z.y_added, count=AHEAD)
            for b in range(B):
                with pool.Fori(0, PAIRS) as mm_:
                    for par in range(2):
                        k = b * DS + 2 * mm_ + par
                        for h in range(HALVES):
                            g = t.g[:, par, h, :]
                            pool.wait_ge(z.c_saved, AHEAD + k + 1)
                            pool.wait_ge(z.scanned, AHEAD + 2 * k + h + 1)
                            nc.gpsimd.tensor_tensor(g, g, t.Cs[:, par, :], ALU.mult).then_inc(z.weighted, 1)


def mixer_output(m, t):
    nc = m.nc
    z = semaphores(m.sem, "mo_", ("summed", "added"))
    with nc.Block() as block:
        @block.tensor
        def _(pe):
            for s in range(NSUP):
                for h in range(HALVES):
                    mm = nc.tensor.matmul(m.bank[s][:, 0:SUP], m.l("w_out")[:, h * D:(h + 1) * D],
                                          t.sz[:, h, s * SUP:(s + 1) * SUP], start=(h == 0), stop=(h == HALVES - 1))
                mm.then_inc(z.summed, 1)

        @block.vector
        def _(dve):
            for s in range(NSUP):
                x = m.xC[:, s * SUP:(s + 1) * SUP]
                dve.wait_ge(z.summed, s + 1)
                nc.vector.scalar_tensor_tensor(out=x, in0=m.bank[s][:, 0:SUP], scalar=m.gated(1, 2, s), in1=x,
                                               op0=ALU.mult, op1=ALU.add).then_inc(z.added, 1)



def experts(m):
    nc = m.nc
    m.w_high, m.w_low = m.sem("w_high"), m.sem("w_low")
    PIECES = 4

    def highs(act, weights, high, pieces=range(PIECES)):
        width = weights.shape[1] // PIECES
        for i in pieces:
            cut = slice(i * width, (i + 1) * width)
            nc.scalar.activation(high[:, cut], weights[:, cut], ACT.Copy).then_inc(m.w_high, 1)

    def lows(pool, weights, high, low, done):
        width = weights.shape[1] // PIECES
        for i in range(PIECES):
            cut = slice(i * width, (i + 1) * width)
            pool.wait_ge(m.w_high, done + i + 1)
            nc.gpsimd.tensor_tensor(low[:, cut], weights[:, cut], high[:, cut], ALU.subtract).then_inc(m.w_low, 1)

    with ExitStack() as stack:
        def tile(name, width, dt=F32):
            return stack.enter_context(nc.sbuf_tensor(name, [P, width], dt))

        m.hC, m.arena = tile("ex_h", N), tile("ex_tmp", N + 256)
        m.h_high, m.h_low = tile("h_high", N, F32R), tile("h_low", N, F32R)
        m.up_high, m.up_low = tile("up_high", (E + 1) * F, F32R), tile("up_low", (E + 1) * F, F32R)
        m.down_high, m.down_low = tile("down_high", (E + 1) * F, F32R), tile("down_low", (E + 1) * F, F32R)
        XB = 4
        x_parts = [tile(name, XB * SUP, F32R) for name in ("gelu_high", "gelu_low")]
        m.rwTf = m.l("up")[0:NPART * E, 0:N]
        sup = lambda tile: (lambda s: tile[:, s * SUP:(s + 1) * SUP])
        layer_norm(m, m.xC, sup(m.hC), lambda s: m.scale1(1, 4, s), lambda s: m.shift(1, 3, s), tmp=0,
                   act_first=lambda act: highs(act, m.l("up"), m.up_high), high=sup(m.h_high),
                   meanwhile=lambda pool: lows(pool, m.l("up"), m.up_high, m.up_low, 0))
        top_two_gating(m, m.arena, lambda act, i: highs(act, m.l("down"), m.down_high, (i,)),
                       lambda pool: lows(pool, m.l("down"), m.down_high, m.down_low, PIECES))
        expert_sums(m, m.l("down"), m.l("up")[:, N:N + 2 * SUP], XB, *x_parts)


def top_two_gating(m, tmp, act_first, meanwhile):
    nc, g = m.nc, m.gt
    call = m.gt_calls
    m.gt_calls += 1
    KE = NBLK * E
    at = 0

    def take(width):
        nonlocal at
        at += width
        return tmp[:, at - width:at]

    m.gate_rows = take(SUP)
    gw, sc, rw, total, mx, rest = take(TILE), take(KE), take(KE), take(NBLK), take(NBLK), take(KE)
    parts = take(NPART * KE // 2).bitcast(BF16).rearrange("p (k a e) -> p k a e", k=NBLK, a=NPART)
    top_tmp = take(6 * KE)
    ke = lambda v: v.rearrange("p (k e) -> p k e", e=E)
    with nc.Block() as block:
        @block.tensor
        def _(pe):
            pe.wait_ge(g.weights, 1)
            gate_products(m, pe, m.hC, gw, None, call)
            turn_weights(m, pe, parts, call)

        @block.gpsimd
        def _(pool):
            meanwhile(pool)

        @block.scalar
        def _(act):
            act_first(act, 0)
            nc.scalar.preload_act_table(ACT.Sigmoid)
            save_products(m, act, call)
            act_first(act, 1)
            act.wait_ge(g.act_in, call + 1)
            nc.scalar.activation(sc, sc, ACT.Sigmoid).then_inc(g.act_out, 1)
            act_first(act, 2)
            act_first(act, 3)
            copy_weights(m, act, call, also=m.rwTf)

        @block.vector
        def _(dve):
            step = m.dve.on(dve)
            step(nc.vector.memset(gw, 0.0))
            nc.vector.tensor_copy(gw[:, 0:E], m.l("gate_w")).then_inc(g.weights, 1)
            nc.vector.tensor_tensor(m.h_low[:, :], m.hC[:, :], m.h_high[:, :], ALU.subtract)
            dve.wait_ge(g.turned, call + 1)
            bias = m.r("gate_bias").unsqueeze(1).unsqueeze(1).broadcast_to([P, NSUP, BLKS, E])
            nc.vector.tensor_tensor(sc.rearrange("p (s j e) -> p s j e", s=NSUP, j=BLKS), by_token(m)[:, :, :, 0:E], bias,
                                    ALU.add).then_inc(g.act_in, 1)
            dve.wait_ge(g.act_out, 2 * call + 1)
            step(nc.vector.tensor_reduce(mx, ke(sc), AX.X, ALU.max))
            chosen = top_two(m, step, ke(sc), mx, top_tmp)
            step(nc.vector.tensor_tensor(ke(rw), ke(sc), chosen, ALU.mult))
            step(nc.vector.tensor_reduce(total, ke(rw), AX.X, ALU.add))
            step(nc.vector.tensor_scalar(total, total, 1e-6, None, ALU.add))
            step(nc.vector.reciprocal(total, total))
            step(nc.vector.tensor_tensor(ke(rw), ke(rw), total.unsqueeze(2).broadcast_to([P, NBLK, E]), ALU.mult))
            split_weights(m, step, ke(rw), parts, ke(rest))


def expert_sums(m, tmp, sums, XB, x_high, x_low):
    nc = m.nc
    names = ("up", "gelu", "spread", "scaled", "high", "low", "used", "biased", "added", "stored", "sbd")
    z = semaphores(m.sem, "ex_", names)
    CH = (E + 1) * FC
    LAG = 4
    SHARED = 0.1
    gelu, scaled, high, low = (v[:, 0:XB * SUP].rearrange("p (u c) -> p u c", u=XB)
                               for v in (tmp, tmp[:, XB * SUP:2 * XB * SUP], x_high, x_low))
    yb = sums.rearrange("p (u c) -> p u c", u=2)
    sbd = m.small[:, 40:41]
    up = [m.bank[i // 2][:, (i % 2) * SUP:(i % 2 + 1) * SUP] for i in range(4)]
    wB = [m.bank[2][:, 0:SUP], m.bank[2][:, SUP:2 * SUP]]
    acc = lambda par: m.bank[3][:, par * SUP:(par + 1) * SUP]
    PAIRS = NSUP // 2

    with nc.Block() as block:
        @block.tensor
        def _(pe):
            prime(pe, z.used)
            pe.wait_ge(m.w_low, 8)
            with pe.Fori(0, PAIRS) as p2:
                for par in range(2):
                    s = 2 * p2 + par
                    base = CH * s
                    at = bass.ds(s * SUP, SUP)
                    pe.wait_ge(z.scaled, PRIMED + base)
                    apart(pe)
                    spread(m, wB[0], 0, s).then_inc(z.spread, 1)
                    pe.wait_ge(z.added, PRIMED + 2 * p2)
                    apart(pe)
                    nc.tensor.matmul(acc(par), m.l("bd")[0:NPART * E, :], m.rwTf[:, at], start=True, stop=False)
                    for c in range(CH + LAG):
                        if c < CH:
                            cut = slice(c * P, (c + 1) * P)
                            pe.wait_ge(z.gelu, PRIMED + base + max(0, c - XB + 1))
                            apart(pe)
                            three_passes(m, up[c % XB], m.up_high[:, cut], m.up_low[:, cut], m.h_high[:, at], m.h_low[:, at],
                                         True, True).then_inc(z.up, 1)
                        if c >= LAG:
                            d = c - LAG
                            cut = slice(d * P, (d + 1) * P)
                            pe.wait_ge(z.low, base + d + 1)
                            apart(pe)
                            three_passes(m, acc(par), m.down_high[:, cut], m.down_low[:, cut], high[:, d % XB, :],
                                         low[:, d % XB, :], False, d == CH - 1).then_inc(z.used, 1)
                            if d % FC == 0 and d // FC + 1 < E:
                                spread(m, wB[(d // FC + 1) % 2], d // FC + 1, s).then_inc(z.spread, 1)

        @block.scalar
        def _(act):
            prime(act, z.gelu)
            nc.scalar.preload_act_table(ACT.Gelu)
            with act.Fori(0, PAIRS) as p2:
                for par in range(2):
                    s = 2 * p2 + par
                    base = CH * s
                    for c in range(CH + 1):
                        if c < CH:
                            act.wait_ge(z.scaled, PRIMED + base + max(0, c - XB + 1))
                            act.wait_ge(z.up, base + c + 1)
                            nc.scalar.activation(gelu[:, c % XB, :], up[c % XB], ACT.Gelu,
                                                 bias=m.l("up_bias")[:, c:c + 1]).then_inc(z.gelu, 1)
                        if c:
                            d = c - 1
                            act.wait_ge(z.used, PRIMED + base + max(0, d - XB + 1))
                            act.wait_ge(z.scaled, PRIMED + base + d + 1)
                            nc.scalar.activation(high[:, d % XB, :], scaled[:, d % XB, :], ACT.Copy).then_inc(z.high, 1)
                    act.wait_ge(z.sbd, 1)
                    act.wait_ge(z.added, PRIMED + 2 * p2)
                    act.wait_ge(z.used, PRIMED + base + CH)
                    nc.scalar.activation(yb[:, par, :], acc(par), ACT.Identity, bias=sbd).then_inc(z.biased, 1)

        @block.vector
        def _(dve):
            prime(dve, z.scaled, z.added)
            nc.vector.tensor_scalar(sbd, m.l("sbd"), SHARED, None, ALU.mult).then_inc(z.sbd, 1)

            def finish(s, par, p2):
                dve.wait_ge(z.biased, s + 1)
                apart(dve)
                x = m.xC[:, bass.ds(s * SUP, SUP)]
                nc.vector.scalar_tensor_tensor(out=x, in0=yb[:, par, :], scalar=m.gate[:, bass.ds((6 + 5) * B + p2, 1)],
                                               in1=x, op0=ALU.mult, op1=ALU.add).then_inc(z.added, 1)

            with dve.Fori(0, PAIRS) as p2:
                for par in range(2):
                    s = 2 * p2 + par
                    base = CH * s
                    for c in range(CH + 1):
                        if c < CH:
                            if c < E * FC:
                                dve.wait_ge(z.spread, E * s + c // FC + 1)
                            dve.wait_ge(z.gelu, PRIMED + base + c + 1)
                            if c < E * FC:
                                nc.vector.tensor_tensor(scaled[:, c % XB, :], gelu[:, c % XB, :], wB[(c // FC) % 2],
                                                        ALU.mult).then_inc(z.scaled, 1)
                            else:
                                nc.vector.tensor_scalar(scaled[:, c % XB, :], gelu[:, c % XB, :], SHARED, None,
                                                        ALU.mult).then_inc(z.scaled, 1)
                        if c:
                            d = c - 1
                            dve.wait_ge(z.high, base + d + 1)
                            nc.vector.tensor_tensor(low[:, d % XB, :], scaled[:, d % XB, :], high[:, d % XB, :],
                                                    ALU.subtract).then_inc(z.low, 1)
                    finish(s, par, p2)

        @block.sync
        def _(sp):
            for s in range(NSUP):
                sp.wait_ge(z.added, PRIMED + s + 1)
                sp.dma_start(m.out[:, s * SUP:(s + 1) * SUP], m.xC[:, s * SUP:(s + 1) * SUP]).then_inc(z.stored, 16)
            sp.wait_ge(z.stored, 16 * NSUP)



def packed(inputs):
    g = {k: np.asarray(v) for k, v in inputs.items()}
    col = lambda v: v.reshape(-1, 1)
    halves = lambda w: w.reshape(HALVES, P, -1).transpose(1, 0, 2).reshape(P, -1)
    experts = lambda w: w.transpose(1, 0, 2).reshape(P, -1)
    att = {"wq": g["L0_attn_Wq"].T, "wk": g["L0_attn_Wk"].T, "wv": g["L0_attn_Wv"].T, "wo": g["L0_attn_Wo"].T,
           "wmod0": g["L0_wmod"], "wmod1": g["L1_wmod"], "c": np.concatenate([g["L0_c"].T, g["L1_c"].T], axis=1),
           "bq": col(g["L0_attn_bq"]), "bk": col(g["L0_attn_bk"]), "bv": col(g["L0_attn_bv"]), "bo": col(g["L0_attn_bo"]),
           "ln1w": col(g["L0_ffn_ln1_w"]), "ln1b": col(g["L0_ffn_ln1_b"]), "ln2w": col(g["L0_ffn_ln2_w"]),
           "ln2b": col(g["L0_ffn_ln2_b"]), "smha_sim": g["L0_ffn_smha_sim"], "moe_sim": g["L0_ffn_moe_sim"]}
    ffn = {"qp": experts(g["L0_ffn_q_proj"]), "kp": experts(g["L0_ffn_k_proj"]), "vp": experts(g["L0_ffn_v_proj"]),
           "op": experts(g["L0_ffn_o_proj"]), "w1": experts(g["L0_ffn_w1"]), "w2": experts(g["L0_ffn_w2"])}
    bd = np.concatenate([g["L1_ffn_bd"]] * NPART + [np.zeros((P - NPART * E, D), np.float32)])
    l1 = {"w_in": g["L1_attn_W_in"], "w_x": halves(g["L1_attn_W_x"]), "w_out": halves(g["L1_attn_W_out"]),
          "b_conv": halves(g["L1_attn_b_conv"]), "w_conv": halves(g["L1_attn_W_conv"][:, 0, :]), "w_dt": halves(g["L1_attn_W_dt"][0]), "b_dt": halves(g["L1_attn_b_dt"]),
          "a_log": halves(g["L1_attn_A_log"]), "dskip": halves(g["L1_attn_D"]), "gate_w": g["L1_ffn_gate_w"].T,
          "up": np.concatenate([g["L1_ffn_Wu"].transpose(2, 0, 1).reshape(P, -1), g["L1_ffn_sWu"].T], axis=1),
          "down": np.concatenate([g["L1_ffn_Wd"].reshape(E, D, FC, P).transpose(3, 0, 2, 1).reshape(P, -1),
                                  g["L1_ffn_sWd"].reshape(D, FC, P).transpose(2, 1, 0).reshape(P, -1)], axis=1),
          "up_bias": np.concatenate([g["L1_ffn_bu"].reshape(E, FC, P).transpose(2, 0, 1).reshape(P, -1),
                                     g["L1_ffn_sbu"].reshape(FC, P).T], axis=1),
          "sbd": col(g["L1_ffn_sbd"]), "bd": bd}
    row = {"alpha": g["L0_attn_alpha"].reshape(1), "smha_gates": g["L0_ffn_smha_gates"], "moe_gates": g["L0_ffn_moe_gates"],
           "gate_bias": g["L1_ffn_gate_bias"]}
    side = lambda cols, parts: np.ascontiguousarray(np.concatenate([parts[k] for k in cols], axis=-1))
    return {"att_w": side(ATT_COLS, att), "ffn_w": side(FFN_COLS, ffn), "l1_w": side(L1_COLS, l1),
            "row_w": side(ROW_COLS, row).reshape(1, -1),
            "x_channels": np.ascontiguousarray(g["L0_attn_x"].reshape(N, D).T)}


def kernel(**inputs):
    import concourse.bacc as _bacc
    from concourse.bass_utils import run_bass_kernel_spmd as _run

    nc = _bacc.Bacc("TRN2", target_bir_lowering=False, num_devices=1)
    arrays = packed(inputs)
    args = {k: nc.dram_tensor(k, a.shape, mybir.dt.from_np(a.dtype), kind="ExternalInput").ap() for k, a in arrays.items()}
    out = nc.dram_tensor("out_channels", (P, N), F32, kind="ExternalOutput").ap()
    build(nc, args["att_w"], args["ffn_w"], args["l1_w"], args["row_w"], args["x_channels"], out)
    r = _run(nc, [arrays], core_ids=[0])
    return np.ascontiguousarray(r.results[0]["out_channels"].T).reshape(B, T, D)
```
